# Optimizing a Trainium2 kernel written in Bass

```python
import numpy as np
import jax
import jax.numpy as jnp

def _softmax(x, axis=-1):
    return jax.nn.softmax(x, axis=axis)

def _gelu(x):
    return jax.nn.gelu(x, approximate=True)

def _silu(x):
    return jax.nn.silu(x)

def _sigmoid(x):
    return jax.nn.sigmoid(x)

def _layernorm(x, axis=-1, eps=1e-05):
    m = jnp.mean(x, axis=axis, keepdims=True)
    v = jnp.var(x, axis=axis, keepdims=True)
    return (x - m) / jnp.sqrt(v + eps)

def _scatter_add(tgt, idx, src, axis=0):
    return tgt.at[idx].add(src)

def _segment_sum(src, seg, n):
    return jax.ops.segment_sum(src, seg, n)
kernel_name = 'mk_decoder_preln_d2_seqx_r8_6da7cf'

def setup_inputs(seed: int=0):
    np.random.seed(seed)
    _w = jnp.asarray

    def _rec_inputs():
        import jax
        import jax.numpy as jnp
        _rk = jax.random.key(seed)
        x = 7.22e-05 + 1 * jax.random.normal(jax.random.fold_in(_rk, 1), (16, 128, 128), jnp.float32)
        _lenS = 128 - jax.random.randint(jax.random.fold_in(_rk, 7), (16,), 0, max(1, 128 // 4) + 1, jnp.int32)
        _lenS2 = 128 - jax.random.randint(jax.random.fold_in(_rk, 8), (16,), 0, max(1, 128 // 4) + 1, jnp.int32)
        _ctx_1024P = jax.random.normal(jax.random.fold_in(_rk, 11), (16, 16, 128), jnp.float32)
        _ctx_1024c = jax.random.dirichlet(jax.random.fold_in(_rk, 511), 0.3 * jnp.ones((16,), jnp.float32), (16, 128))
        _ctx_1024t = jnp.einsum('bsk,bkd->bsd', _ctx_1024c, _ctx_1024P)
        _ctx_1024t = _ctx_1024t * jax.lax.rsqrt(jnp.mean(jnp.square(_ctx_1024t)) + 1e-12) * 0.953939
        ctx_1024 = 4.13588e-05 + 0.999923 * (_ctx_1024t + 0.3 * jax.random.normal(jax.random.fold_in(_rk, 611), (16, 128, 128), jnp.float32))
        return (x, ctx_1024)
    x, ctx_1024 = _rec_inputs()

    def _L0_attn_setup():
        import jax, jax.numpy as jnp
        import numpy as np
        B, S, D, H = (4, 256, 128, 16)
        DH = D // H
        key = jax.random.key(seed)
        ks = jax.random.split(key, 5)
        std = 1.0 / np.sqrt(D)
        return {'x': jax.random.normal(ks[0], (B, S, D), dtype=jnp.float32), 'mask': jnp.ones((S, S), dtype=bool), 'Wq': jax.random.normal(ks[1], (D, D), dtype=jnp.float32) * std, 'Wk': jax.random.normal(ks[2], (D, D), dtype=jnp.float32) * std, 'Wv': jax.random.normal(ks[3], (D, D), dtype=jnp.float32) * std, 'Wout': jax.random.normal(ks[4], (D, D), dtype=jnp.float32) * std}
    _L0_attn_all = _L0_attn_setup()
    _L0_attn_in = {k: v for k, v in _L0_attn_all.items() if k in ('mask', 'Wq', 'Wk', 'Wv', 'Wout')}
    del _L0_attn_all

    def _L0_xattn_setup():
        import jax, jax.numpy as jnp
        import numpy as np
        NUM_HEADS = 16
        key = jax.random.key(seed)
        k1, k2, k3, k4 = jax.random.split(key, 4)
        B, S, E = (4, 256, 128)
        return {'q': jax.random.normal(k1, (B, S, E), dtype=jnp.float32), 'k': jax.random.normal(k2, (B, S, E), dtype=jnp.float32), 'v': jax.random.normal(k3, (B, S, E), dtype=jnp.float32), 'w_out': jax.random.normal(k4, (E, E), dtype=jnp.float32) * E ** (-0.5), 'b_out': jnp.zeros((E,), dtype=jnp.float32)}
    _L0_xattn_all = _L0_xattn_setup()
    _L0_xattn_in = {k: v for k, v in _L0_xattn_all.items() if k in ('w_out', 'b_out')}
    del _L0_xattn_all

    def _L0_ffn_setup():
        import jax, jax.numpy as jnp
        import numpy as np
        D_MODEL = 128
        EXPANSION = 4
        D_HIDDEN = D_MODEL * EXPANSION
        NUM_STAGES = int(np.log2(D_HIDDEN))

        def butterfly(y, weights, dim):
            lead = y.shape[:-1]
            for stage in range(weights.shape[0]):
                s = 2 ** stage
                nb = dim // (2 * s)
                yr = y.reshape(*lead, nb, 2, s)
                a = yr[..., 0, :]
                b = yr[..., 1, :]
                w = weights[stage].reshape(nb, s, 2, 2)
                na = w[..., 0, 0] * a + w[..., 0, 1] * b
                nb2 = w[..., 1, 0] * a + w[..., 1, 1] * b
                y = jnp.stack([na, nb2], axis=-2).reshape(*lead, dim)
            return y
        key = jax.random.key(seed)
        ks = jax.random.split(key, 6)
        B, S = (4, 256)
        x = jax.random.normal(ks[0], (B, S, D_MODEL), jnp.float32)
        W_exp = jax.random.normal(ks[1], (D_MODEL, D_HIDDEN), jnp.float32) * 0.02
        b_exp = jnp.zeros((D_HIDDEN,), jnp.float32)
        up_weights = jax.random.normal(ks[2], (NUM_STAGES, D_HIDDEN // 2, 2, 2), jnp.float32) * 0.02
        up_bias = jnp.zeros((D_HIDDEN,), jnp.float32)
        down_weights = jax.random.normal(ks[3], (NUM_STAGES, D_HIDDEN // 2, 2, 2), jnp.float32) * 0.02
        W_con = jax.random.normal(ks[4], (D_HIDDEN, D_MODEL), jnp.float32) * 0.02
        b_con = jnp.zeros((D_MODEL,), jnp.float32)
        down_bias = jnp.zeros((D_MODEL,), jnp.float32)
        return dict(x=x, W_exp=W_exp, b_exp=b_exp, up_weights=up_weights, up_bias=up_bias, down_weights=down_weights, W_con=W_con, b_con=b_con, down_bias=down_bias)
    _L0_ffn_all = _L0_ffn_setup()
    _L0_ffn_in = {k: v for k, v in _L0_ffn_all.items() if k in ('W_exp', 'b_exp', 'up_weights', 'up_bias', 'down_weights', 'W_con', 'b_con', 'down_bias')}
    del _L0_ffn_all

    def _L1_attn_setup():
        import jax, jax.numpy as jnp
        import numpy as np
        B, T, D = (4, 256, 128)
        H, DK = (8, 64)
        EPS = 1e-06

        def _xavier(key, shape):
            fan_in, fan_out = (shape[1], shape[0])
            lim = float(np.sqrt(6.0 / (fan_in + fan_out)))
            return jax.random.uniform(key, shape, jnp.float32, -lim, lim)

        def _phi(u):
            return jax.nn.elu(u) + 1.0
        key = jax.random.key(seed)
        ks = jax.random.split(key, 7)
        x = jax.random.normal(ks[0], (B, T, D), jnp.float32)
        W_Q = _xavier(ks[1], (H * DK, D))
        W_K = _xavier(ks[2], (H * DK, D))
        W_V = _xavier(ks[3], (H * DK, D))
        W_g_w = _xavier(ks[4], (H * DK, D))
        W_g_b = jax.random.normal(ks[5], (H * DK,), jnp.float32) * 0.02
        W_O = _xavier(ks[6], (D, H * DK))
        decay_log = jnp.zeros((H,), jnp.float32)
        return {'x': x, 'W_Q': W_Q, 'W_K': W_K, 'W_V': W_V, 'W_g_w': W_g_w, 'W_g_b': W_g_b, 'W_O': W_O, 'decay_log': decay_log}
    _L1_attn_all = _L1_attn_setup()
    _L1_attn_in = {k: v for k, v in _L1_attn_all.items() if k in ('W_Q', 'W_K', 'W_V', 'W_g_w', 'W_g_b', 'W_O', 'decay_log')}
    del _L1_attn_all

    def _L1_xattn_setup():
        import jax, jax.numpy as jnp
        import numpy as np
        import math
        B, L, D, H = (8, 512, 128, 16)
        DK = D // H
        FACTOR = 1

        def _linear(x, W, b):
            return jnp.einsum('bld,od->blo', x, W) + b
        rng = jax.random.key(seed)
        ks = jax.random.split(rng, 11)
        s = 0.02
        return {'query': jax.random.normal(ks[0], (B, L, D), jnp.float32), 'key': jax.random.normal(ks[1], (B, L, D), jnp.float32), 'value': jax.random.normal(ks[2], (B, L, D), jnp.float32), 'Wq': jax.random.normal(ks[3], (D, D), jnp.float32) * s, 'bq': jax.random.normal(ks[4], (D,), jnp.float32) * s, 'Wk': jax.random.normal(ks[5], (D, D), jnp.float32) * s, 'bk': jax.random.normal(ks[6], (D,), jnp.float32) * s, 'Wv': jax.random.normal(ks[7], (D, D), jnp.float32) * s, 'bv': jax.random.normal(ks[8], (D,), jnp.float32) * s, 'Wo': jax.random.normal(ks[9], (D, D), jnp.float32) * s, 'bo': jax.random.normal(ks[10], (D,), jnp.float32) * s}
    _L1_xattn_all = _L1_xattn_setup()
    _L1_xattn_in = {k: v for k, v in _L1_xattn_all.items() if k in ('Wq', 'bq', 'Wk', 'bk', 'Wv', 'bv', 'Wo', 'bo')}
    del _L1_xattn_all

    def _L1_ffn_setup():
        import jax, jax.numpy as jnp
        import numpy as np
        import math
        E = 8
        K = 2
        CF = 1.2
        D = 128
        H = 512
        key = jax.random.key(seed)
        k0, k1, k2, k3 = jax.random.split(key, 4)
        B, T = (8, 256)
        x_btd = jax.random.normal(k0, (B, T, D), jnp.float32)
        Wr = jax.random.normal(k1, (D, E), jnp.float32) / np.sqrt(D)
        br = jnp.zeros((E,), jnp.float32)
        W1 = jax.random.normal(k2, (E, D, H), jnp.float32) / np.sqrt(D)
        b1 = jnp.zeros((E, H), jnp.float32)
        W2 = jax.random.normal(k3, (E, H, D), jnp.float32) / np.sqrt(H)
        b2 = jnp.zeros((E, D), jnp.float32)
        return dict(x_btd=x_btd, Wr=Wr, br=br, W1=W1, b1=b1, W2=W2, b2=b2)
    _L1_ffn_all = _L1_ffn_setup()
    _L1_ffn_in = {k: v for k, v in _L1_ffn_all.items() if k in ('Wr', 'br', 'W1', 'b1', 'W2', 'b2')}
    del _L1_ffn_all
    return {'x': x, 'ctx_1024': ctx_1024, 'L0_attn_mask': _L0_attn_in['mask'], 'L0_attn_Wq': _L0_attn_in['Wq'], 'L0_attn_Wk': _L0_attn_in['Wk'], 'L0_attn_Wv': _L0_attn_in['Wv'], 'L0_attn_Wout': _L0_attn_in['Wout'], 'L0_xattn_w_out': _L0_xattn_in['w_out'], 'L0_xattn_b_out': _L0_xattn_in['b_out'], 'L0_ffn_W_exp': _L0_ffn_in['W_exp'], 'L0_ffn_b_exp': _L0_ffn_in['b_exp'], 'L0_ffn_up_weights': _L0_ffn_in['up_weights'], 'L0_ffn_up_bias': _L0_ffn_in['up_bias'], 'L0_ffn_down_weights': _L0_ffn_in['down_weights'], 'L0_ffn_W_con': _L0_ffn_in['W_con'], 'L0_ffn_b_con': _L0_ffn_in['b_con'], 'L0_ffn_down_bias': _L0_ffn_in['down_bias'], 'L1_attn_W_Q': _L1_attn_in['W_Q'], 'L1_attn_W_K': _L1_attn_in['W_K'], 'L1_attn_W_V': _L1_attn_in['W_V'], 'L1_attn_W_g_w': _L1_attn_in['W_g_w'], 'L1_attn_W_g_b': _L1_attn_in['W_g_b'], 'L1_attn_W_O': _L1_attn_in['W_O'], 'L1_attn_decay_log': _L1_attn_in['decay_log'], 'L1_xattn_Wq': _L1_xattn_in['Wq'], 'L1_xattn_bq': _L1_xattn_in['bq'], 'L1_xattn_Wk': _L1_xattn_in['Wk'], 'L1_xattn_bk': _L1_xattn_in['bk'], 'L1_xattn_Wv': _L1_xattn_in['Wv'], 'L1_xattn_bv': _L1_xattn_in['bv'], 'L1_xattn_Wo': _L1_xattn_in['Wo'], 'L1_xattn_bo': _L1_xattn_in['bo'], 'L1_ffn_Wr': _L1_ffn_in['Wr'], 'L1_ffn_br': _L1_ffn_in['br'], 'L1_ffn_W1': _L1_ffn_in['W1'], 'L1_ffn_b1': _L1_ffn_in['b1'], 'L1_ffn_W2': _L1_ffn_in['W2'], 'L1_ffn_b2': _L1_ffn_in['b2']}

def reference(x, ctx_1024, L0_attn_mask, L0_attn_Wq, L0_attn_Wk, L0_attn_Wv, L0_attn_Wout, L0_xattn_w_out, L0_xattn_b_out, L0_ffn_W_exp, L0_ffn_b_exp, L0_ffn_up_weights, L0_ffn_up_bias, L0_ffn_down_weights, L0_ffn_W_con, L0_ffn_b_con, L0_ffn_down_bias, L1_attn_W_Q, L1_attn_W_K, L1_attn_W_V, L1_attn_W_g_w, L1_attn_W_g_b, L1_attn_W_O, L1_attn_decay_log, L1_xattn_Wq, L1_xattn_bq, L1_xattn_Wk, L1_xattn_bk, L1_xattn_Wv, L1_xattn_bv, L1_xattn_Wo, L1_xattn_bo, L1_ffn_Wr, L1_ffn_br, L1_ffn_W1, L1_ffn_b1, L1_ffn_W2, L1_ffn_b2):
    import jax
    import jax.numpy as jnp

    def _L0_attn_ref(x, mask, Wq, Wk, Wv, Wout):
        import jax, jax.numpy as jnp
        import numpy as np
        B, S, D, H = (4, 256, 128, 16)
        DH = D // H
        n, s, d = x.shape
        scale = 1.0 / np.sqrt(DH).astype(np.float32)
        q = (x @ Wq).reshape(n, s, H, DH)
        k = (x @ Wk).reshape(n, s, H, DH)
        v = (x @ Wv).reshape(n, s, H, DH)
        attn = jnp.einsum('nqhd,nkhd->nqkh', q, k) * scale
        attn = jax.nn.softmax(attn, axis=-2)
        z = jnp.einsum('nqkh,nkhd->nqhd', attn, v).reshape(n, s, d)
        z = jnp.einsum('nqd,de->nqe', z, Wout)
        return x + z

    def _L0_xattn_ref(q, k, v, w_out, b_out):
        import jax, jax.numpy as jnp
        import numpy as np
        NUM_HEADS = 16
        B, S, E = q.shape
        H = NUM_HEADS
        D = E // H
        scale = D ** (-0.5)

        def split(x):
            return x.reshape(B, S, H, D).transpose(0, 2, 1, 3)
        qh, kh, vh = (split(q), split(k), split(v))
        scores = jnp.einsum('bhqd,bhkd->bhqk', qh, kh) * scale
        weights = jax.nn.softmax(scores, axis=-1)
        out = jnp.einsum('bhqk,bhkd->bhqd', weights, vh)
        out = out.transpose(0, 2, 1, 3).reshape(B, S, E)
        return out @ w_out.T + b_out

    def _L0_ffn_ref(x, W_exp, b_exp, up_weights, up_bias, down_weights, W_con, b_con, down_bias):
        import jax, jax.numpy as jnp
        import numpy as np
        D_MODEL = 128
        EXPANSION = 4
        D_HIDDEN = D_MODEL * EXPANSION
        NUM_STAGES = int(np.log2(D_HIDDEN))

        def butterfly(y, weights, dim):
            lead = y.shape[:-1]
            for stage in range(weights.shape[0]):
                s = 2 ** stage
                nb = dim // (2 * s)
                yr = y.reshape(*lead, nb, 2, s)
                a = yr[..., 0, :]
                b = yr[..., 1, :]
                w = weights[stage].reshape(nb, s, 2, 2)
                na = w[..., 0, 0] * a + w[..., 0, 1] * b
                nb2 = w[..., 1, 0] * a + w[..., 1, 1] * b
                y = jnp.stack([na, nb2], axis=-2).reshape(*lead, dim)
            return y
        h = jnp.einsum('bsd,dh->bsh', x, W_exp) + b_exp
        h = butterfly(h, up_weights, D_HIDDEN)
        h = jax.nn.gelu(h + up_bias, approximate=False)
        h = butterfly(h, down_weights, D_HIDDEN)
        y = jnp.einsum('bsh,hd->bsd', h, W_con) + b_con
        return y + down_bias

    def _L1_attn_ref(x, W_Q, W_K, W_V, W_g_w, W_g_b, W_O, decay_log):
        import jax, jax.numpy as jnp
        import numpy as np
        B, T, D = (4, 256, 128)
        H, DK = (8, 64)
        EPS = 1e-06

        def _xavier(key, shape):
            fan_in, fan_out = (shape[1], shape[0])
            lim = float(np.sqrt(6.0 / (fan_in + fan_out)))
            return jax.random.uniform(key, shape, jnp.float32, -lim, lim)

        def _phi(u):
            return jax.nn.elu(u) + 1.0
        b, t, d = x.shape
        q = _phi((x @ W_Q.T).reshape(b, t, H, DK))
        k = _phi((x @ W_K.T).reshape(b, t, H, DK))
        v = (x @ W_V.T).reshape(b, t, H, DK)
        gamma = jax.nn.sigmoid(decay_log)
        g4 = gamma[None, :, None, None]
        g3 = gamma[None, :, None]
        qT = jnp.moveaxis(q, 1, 0)
        kT = jnp.moveaxis(k, 1, 0)
        vT = jnp.moveaxis(v, 1, 0)
        S0 = jnp.zeros((b, H, DK, DK), x.dtype)
        z0 = jnp.zeros((b, H, DK), x.dtype)

        def step(carry, inp):
            S, z = carry
            qt, kt, vt = inp
            S = g4 * S + jnp.einsum('bhi,bhj->bhij', kt, vt)
            z = g3 * z + kt
            num = jnp.einsum('bhij,bhi->bhj', S, qt)
            den = jnp.sum(z * qt, axis=-1, keepdims=True) + EPS
            return ((S, z), num / den)
        _, ys = jax.lax.scan(step, (S0, z0), (qT, kT, vT))
        outputs = jnp.moveaxis(ys, 0, 1)
        gate = jax.nn.sigmoid(x @ W_g_w.T + W_g_b).reshape(b, t, H, DK)
        y = (outputs * gate).reshape(b, t, H * DK)
        return y @ W_O.T

    def _L1_xattn_ref(query, key, value, Wq, bq, Wk, bk, Wv, bv, Wo, bo):
        import jax, jax.numpy as jnp
        import numpy as np
        import math
        B, L, D, H = (8, 512, 128, 16)
        DK = D // H
        FACTOR = 1

        def _linear(x, W, b):
            return jnp.einsum('bld,od->blo', x, W) + b
        Bx, Lx, _ = query.shape
        Q = _linear(query, Wq, bq).reshape(Bx, Lx, H, DK).transpose(0, 2, 1, 3)
        K = _linear(key, Wk, bk).reshape(Bx, Lx, H, DK).transpose(0, 2, 1, 3)
        V = _linear(value, Wv, bv).reshape(Bx, Lx, H, DK).transpose(0, 2, 1, 3)
        Qf = jnp.fft.rfft(Q, axis=2)
        Kf = jnp.fft.rfft(K, axis=2)
        corr = jnp.fft.irfft(Qf * jnp.conj(Kf), n=Lx, axis=2)
        corr_mean = corr.mean(axis=-1)
        top_k = max(1, int(FACTOR * math.log(Lx + 1)))
        top_k = min(top_k, Lx)
        top_w, top_idx = jax.lax.top_k(corr_mean, top_k)
        top_w = jax.nn.softmax(top_w, axis=-1)
        pos = jnp.arange(Lx)
        out = jnp.zeros_like(V)
        for i in range(top_k):
            gidx = (pos[None, None, :] - top_idx[:, :, i, None]) % Lx
            rolled = jnp.take_along_axis(V, gidx[..., None], axis=2)
            out = out + top_w[:, :, i, None, None] * rolled
        out = out.transpose(0, 2, 1, 3).reshape(Bx, Lx, D)
        out = _linear(out, Wo, bo)
        return out

    def _L1_ffn_ref(x_btd, Wr, br, W1, b1, W2, b2):
        import jax, jax.numpy as jnp
        import numpy as np
        import math
        E = 8
        K = 2
        CF = 1.2
        D = 128
        H = 512
        B, T, Dm = x_btd.shape
        N = B * T
        x = x_btd.reshape(N, Dm)
        cap = int(math.ceil(CF * N / E))
        probs = jax.nn.softmax(x @ Wr + br, axis=-1)
        gates, ids = jax.lax.top_k(probs, K)
        flat_ids = ids.reshape(-1)
        flat_g = gates.reshape(-1)
        M = N * K
        order = jnp.lexsort((-flat_g, flat_ids))
        s_ids = flat_ids[order]
        s_tok = (order // K).astype(jnp.int32)
        s_g = flat_g[order]
        counts = jnp.bincount(flat_ids, length=E)
        starts = jnp.concatenate([jnp.zeros((1,), counts.dtype), jnp.cumsum(counts)[:-1]])
        rank = jnp.arange(M) - starts[s_ids]
        valid = rank < cap
        pos = jnp.where(valid, s_ids * cap + rank, E * cap)
        disp_tok = jnp.zeros((E * cap + 1,), jnp.int32).at[pos].set(s_tok)[:E * cap]
        disp_g = jnp.zeros((E * cap + 1,), x.dtype).at[pos].set(s_g)[:E * cap]
        xg = x[disp_tok].reshape(E, cap, Dm)
        h = jax.nn.silu(jnp.einsum('ecd,edh->ech', xg, W1) + b1[:, None, :])
        out = jnp.einsum('ech,ehd->ecd', h, W2) + b2[:, None, :]
        gated = out * disp_g.reshape(E, cap, 1)
        y = jnp.zeros((N, Dm), x.dtype).at[disp_tok].add(gated.reshape(E * cap, Dm))
        return y.reshape(B, T, Dm)
    x = x + _L0_attn_ref(_layernorm(x, axis=-1), L0_attn_mask, L0_attn_Wq, L0_attn_Wk, L0_attn_Wv, L0_attn_Wout)
    x = x + _L0_xattn_ref(_layernorm(x, axis=-1), ctx_1024, ctx_1024, L0_xattn_w_out, L0_xattn_b_out)
    x = x + _L0_ffn_ref(_layernorm(x, axis=-1), L0_ffn_W_exp, L0_ffn_b_exp, L0_ffn_up_weights, L0_ffn_up_bias, L0_ffn_down_weights, L0_ffn_W_con, L0_ffn_b_con, L0_ffn_down_bias)
    x = x + _L1_attn_ref(_layernorm(x, axis=-1), L1_attn_W_Q, L1_attn_W_K, L1_attn_W_V, L1_attn_W_g_w, L1_attn_W_g_b, L1_attn_W_O, L1_attn_decay_log)
    x = x + _L1_xattn_ref(_layernorm(x, axis=-1), ctx_1024, ctx_1024, L1_xattn_Wq, L1_xattn_bq, L1_xattn_Wk, L1_xattn_bk, L1_xattn_Wv, L1_xattn_bv, L1_xattn_Wo, L1_xattn_bo)
    x = x + _L1_ffn_ref(_layernorm(x, axis=-1), L1_ffn_Wr, L1_ffn_br, L1_ffn_W1, L1_ffn_b1, L1_ffn_W2, L1_ffn_b2)
    return x

_drawn_inputs = setup_inputs


def setup_inputs(seed=0):
    import zlib

    import numpy as np

    out = dict(_drawn_inputs(seed))
    spreads = {'L0_xattn_b_out': (0.0, 0.1),
     'L0_ffn_b_exp': (0.0, 0.1),
     'L0_ffn_up_bias': (0.0, 0.1),
     'L0_ffn_b_con': (0.0, 0.1),
     'L0_ffn_down_bias': (0.0, 0.1),
     'L1_attn_decay_log': (0.0, 0.8),
     'L1_ffn_br': (0.0, 0.484),
     'L1_ffn_b1': (0.0, 0.659),
     'L1_ffn_b2': (0.0, 0.403)}
    factors = {'L1_attn_W_Q': 23.394,
     'L1_attn_W_K': 8.0,
     'L1_attn_W_g_b': 30.239,
     'L1_xattn_Wq': 4.533,
     'L1_xattn_bq': 64.0,
     'L1_xattn_Wk': 4.394,
     'L1_xattn_bk': 64.0,
     'L1_xattn_Wv': 3.016,
     'L1_xattn_bv': 8.0,
     'L1_xattn_Wo': 3.118,
     'L1_xattn_bo': 4.711}
    for name, (base, spread) in spreads.items():
        noise = np.random.default_rng([zlib.crc32(name.encode()), seed]).standard_normal(out[name].shape)
        drawn = base * np.exp(spread * noise) if base else spread * noise
        out[name] = jnp.asarray(drawn.astype(out[name].dtype))
    for name, factor in factors.items():
        out[name] = (out[name] * factor).astype(out[name].dtype)
    return out
```

```python
import numpy as np
from contextlib import ExitStack

import concourse.bass as bass
from concourse import mybir

FP32 = mybir.dt.float32
BF16 = mybir.dt.bfloat16
I32 = mybir.dt.int32
U32 = mybir.dt.uint32
ALU = mybir.AluOpType
ACT = mybir.ActivationFunctionType
AX = mybir.AxisListType

B = 16
T = 128
D = 128
EPS = 1e-5
G, J = 4, 4
DH = D // (G * J)


class Core:

    def __init__(self, nc, ctx):
        self.nc, self.ctx = nc, ctx
        self.x = self.sb("x", [T, B, D])
        self.stats = self.sb("stats", [T, B, 6])
        self.mean = self.sb("mean", [T, B, 1])
        self.rstd = self.sb("rstd", [T, B, 1])
        self.dev = self.sb("dev", [T, B])
        self.var = self.sb("var", [T, B])
        self.eps = self.sb("eps", [T, B])
        self.neg_half = self.sb("neg_half", [T, B])
        self.ident = self.sb("ident", [128, 128])
        self.ident_b = self.sb("ident_b", [128, 128], BF16)
        self.ones = self.sb("ones", [128, 128])
        self.bank = [ctx.enter_context(nc.psum_tensor(f"bank{i}", [128, 512], FP32)) for i in range(8)]
        self.layer_sems = []

    def sb(self, name, shape, dt=FP32):
        return self.ctx.enter_context(self.nc.sbuf_tensor(name, shape, dt))

    def sem(self, name):
        self.layer_sems.append(self.nc.alloc_semaphore(name))
        return self.layer_sems[-1]

    def sems(self, layer, names):
        return [self.sem(f"{layer}_{n}") for n in names.split()]

    def free_semaphores(self):
        self.nc.clear_and_free_semaphores(self.layer_sems)
        self.layer_sems = []
        self.nc.all_engine_barrier()


def over(ap, n):
    p, m = ap.shape
    return ap.unsqueeze(1).to_broadcast([p, n, m])


def setup(core, a):
    nc = core.nc
    x_in, made, stat = core.sems("setup", "x_in made stat")
    with nc.Block() as block:
        @block.sync
        def _(sp):
            sp.dma_start(core.ident[:, :], a["c_ident"]).then_inc(x_in, 16)
            for h in range(4):
                sp.dma_start(core.x[:, 4 * h:4 * h + 4, :],
                             a["x"][4 * h:4 * h + 4].rearrange("b t d -> t b d")).then_inc(x_in, 16)

        @block.gpsimd
        def _(pool):
            pool.memset(core.ones[:, :], 1.0).then_inc(made, 1)
            pool.memset(core.eps[:, :], EPS).then_inc(made, 1)
            pool.memset(core.neg_half[:, :], -0.5).then_inc(made, 1)
            pool.wait_ge(x_in, 80)
            pool.tensor_copy(core.ident_b[:, :], core.ident[:, :]).then_inc(made, 1)
            pool.wait_ge(made, 4)

        @block.vector
        def _(dve):
            dve.wait_ge(x_in, 80)
            with dve.Fori(0, B) as b:
                dve.bn_stats(core.stats[:, b, :], core.x[:, b, :]).then_inc(stat, 1)
            dve.wait_ge(stat, B)


def norm_dve(core, dve, s_var):
    st = core.stats
    dve.tensor_tensor(core.mean[:, :, 0], st[:, :, 1], st[:, :, 4], ALU.add).then_inc(s_var, 1)
    dve.tensor_tensor(core.dev[:, :], st[:, :, 1], st[:, :, 4], ALU.subtract).then_inc(s_var, 1)
    dve.tensor_tensor(core.var[:, :], st[:, :, 2], st[:, :, 5], ALU.add).then_inc(s_var, 1)
    dve.wait_ge(s_var, 3)
    dve.tensor_scalar(core.mean[:, :, 0], core.mean[:, :, 0], 0.5, None, ALU.mult).then_inc(s_var, 1)
    dve.scalar_tensor_tensor(out=core.dev[:, :], in0=core.dev[:, :], scalar=0.25, in1=core.dev[:, :],
                             op0=ALU.mult, op1=ALU.mult).then_inc(s_var, 1)
    dve.wait_ge(s_var, 5)
    dve.scalar_tensor_tensor(out=core.var[:, :], in0=core.var[:, :], scalar=1.0 / D, in1=core.dev[:, :],
                             op0=ALU.mult, op1=ALU.add).then_inc(s_var, 1)


def norm_pool(core, pool, s_var, s_rstd):
    pool.wait_ge(s_var, 6)
    pool.tensor_tensor(core.var[:, :], core.var[:, :], core.eps[:, :], ALU.add).then_inc(s_rstd, 1)
    pool.wait_ge(s_rstd, 1)
    pool.tensor_tensor(core.rstd[:, :, 0], core.var[:, :], core.neg_half[:, :], ALU.pow).then_inc(s_rstd, 1)


def normalise(core, dve, dst, b):
    return dve.tensor_scalar(dst, core.x[:, b, :], core.mean[:, b, :], core.rstd[:, b, :],
                             ALU.subtract, ALU.mult)


class AttnMem:

    def __init__(self, core):
        sb = core.sb
        self.n = sb("at_n", [T, 2, D])
        self.nT = sb("at_nT", [D, T])
        self.qT = sb("at_qT", [D, T])
        self.kT = sb("at_kT", [D, T])
        self.q_j = sb("at_q_j", [D, 2, J, T])
        self.k_g = sb("at_k_g", [D, 2, G, T])
        self.q_gb = sb("at_q_gb", [D, G, T], BF16)
        self.k_jb = sb("at_k_jb", [D, J, T], BF16)
        self.v = sb("at_v", [T, 2, G * J, 32])
        self.nmax = sb("at_nmax", [T, G * J], BF16)
        self.p = sb("at_p", [T, G, J, T])
        self.o_raw = sb("at_o_raw", [128, G, T])
        self.rden = sb("at_rden", [T, G, J])
        self.o = sb("at_o", [T, G * J, DH])
        self.oT = sb("at_oT", [D, T])
        self.mask_j = sb("at_mask_j", [D, J, T])
        self.mask_g = sb("at_mask_g", [D, G, T])
        self.w_out = [sb(f"at_w_out{i}", [D, D]) for i in range(2)]
        self.wq, self.wk, self.wv = (sb(f"at_{w}", [D, D]) for w in ("wq", "wk", "wv"))
        self.ctx = sb("ctx", [T, B, D])
        self.ctxT = sb("ctxT", [D, B, T])
        self.bias = sb("at_bias", [T, D])


def attn_setup(core, m, a):
    nc = core.nc
    loaded, zeroed = core.sems("at", "loaded zeroed")
    with nc.Block() as block:
        @block.sync
        def _(sp):
            for dst, src in ((m.wq, "L0_attn_Wq"), (m.wk, "L0_attn_Wk"), (m.wv, "L0_attn_Wv")):
                sp.dma_start(dst[:, :], a[src]).then_inc(loaded, 16)
            sp.dma_start(m.mask_j[:, :, :], a["c_mask_j"].rearrange("p (j t) -> p j t", j=J)).then_inc(loaded, 16)
            sp.dma_start(m.mask_g[:, :, :], a["c_mask_g"].rearrange("p (j t) -> p j t", j=J)).then_inc(loaded, 16)
            for w, src in zip(m.w_out, ("L0_attn_Wout", "L0_xattn_w_outT")):
                sp.dma_start(w[:, :], a[src]).then_inc(loaded, 16)
            sp.dma_start(m.bias[:, :], a["L0_xattn_b_out"].partition_broadcast(T)).then_inc(loaded, 16)
            sp.dma_start(m.ctx[:, :, :], a["ctx_1024"].rearrange("b t d -> t b d")).then_inc(loaded, 16)
            sp.dma_start(m.ctxT[:, :, :], a["ctxT"].rearrange("b d t -> d b t")).then_inc(loaded, 16)
            sp.wait_ge(loaded, 16 * 10)

        @block.vector
        def _(dve):
            dve.memset(m.v[:, :, :, :], 0.0).then_inc(zeroed, 1)
            dve.wait_ge(zeroed, 1)
            dve.memset(m.v[:, :, :, DH:DH + 1], 1.0).then_inc(zeroed, 1)
            dve.wait_ge(zeroed, 2)


def softmax_attention(core, m, layer):
    nc = core.nc
    cross = layer == 1
    (s_var, s_rstd, normed, n_turned, n_copied, projected, qk_copied, v_copied, masked, res_made, scored,
     maxed, shifted, exped, pv_done, raw_copied, raw_turned, rden_done, o_done, o_turned, o_copied, out_done,
     x_done) = core.sems(
        f"at{layer}", "var rstd normed n_turned n_copied projected qk_copied v_copied masked res_made scored "
        "maxed shifted exped pv_done raw_copied raw_turned rden_done o_done o_turned o_copied out_done x_done")
    bank_st, bank_s = core.bank[0:2], core.bank[2:4]
    bank_p, bank_v, bank_d, bank_z = core.bank[4:8]
    qk_copies = 1 if cross else 2
    scale = float(DH) ** -0.5
    LAST = B - 1

    with nc.Block() as block:
        @block.vector
        def _(dve):
            def prepare(b, par, reused=True):
                if reused:
                    dve.wait_ge(res_made, b - 1)
                normalise(core, dve, m.n[:, par, :], b).then_inc(normed, 1)

            def maximum(b, g):
                dve.wait_ge(scored, G * b + g + 1)
                dve.tensor_reduce(m.nmax[:, J * g:J * g + J],
                                  bank_s[g % 2][:, :].rearrange("p (j t) -> p j t", j=J),
                                  AX.X, ALU.max, negate=True).then_inc(maxed, 1)

            def divide(b):
                raw = bank_d[:, :].rearrange("p (h w) -> p h w", w=32)
                dve.wait_ge(raw_turned, b + 1)
                dve.reciprocal(m.rden[:, :, :], raw[:, :, DH].rearrange("p (g j) -> p g j", g=G))\
                    .then_inc(rden_done, 1)
                dve.wait_ge(rden_done, b + 1)
                dve.tensor_tensor(m.o[:, :, :], raw[:, :, 0:DH],
                                  m.rden[:, :, :].rearrange("p g j -> p (g j)").unsqueeze(2)
                                  .to_broadcast([T, G * J, DH]), ALU.mult).then_inc(o_done, 1)

            def finish(b):
                dve.wait_ge(out_done, b + 1)
                dve.wait_ge(res_made, b + 1)
                dve.tensor_tensor(core.x[:, b, :], bank_z[:, 0:D], core.x[:, b, :], ALU.add)\
                    .then_inc(x_done, 1)
                dve.wait_ge(x_done, b + 1)
                dve.bn_stats(core.stats[:, b, :], core.x[:, b, :]).then_inc(s_var, 1)

            def step(b, par, first=False):
                prepare(b + 1, 1 - par, reused=not first)
                if not first:
                    divide(b - 1)
                    finish(b - 1)
                for g in range(G):
                    maximum(b + 1, g)

            norm_dve(core, dve, s_var)
            dve.wait_ge(s_rstd, 2)
            prepare(0, 0, reused=False)
            for g in range(G):
                maximum(0, g)
            step(0, 0, first=True)
            with dve.Fori(0, (B - 2) // 2) as i:
                step(2 * i + 1, 1)
                step(2 * i + 2, 0)
            for b in (LAST - 1, LAST):
                divide(b)
                finish(b)
            dve.wait_ge(s_var, 6 + B)

        @block.gpsimd
        def _(pool):
            def prepare(b, par):
                pool.wait_ge(normed, b + 1)
                pool.tensor_tensor(core.x[:, b, :], core.x[:, b, :],
                                   m.bias[:, :] if cross else m.n[:, par, :], ALU.add).then_inc(res_made, 1)
                pool.wait_ge(qk_copied, qk_copies * (b + 1))
                kT = m.ctxT[:, b, :] if cross else m.kT[:, :]
                for dst, src, mask in ((m.q_gb[:, :, :], m.qT[:, :], m.mask_g), (m.k_jb[:, :, :], kT, m.mask_j),
                                       (m.k_g[:, par, :, :], kT, m.mask_g),
                                       (m.q_j[:, par, :, :], m.qT[:, :], m.mask_j)):
                    pool.tensor_tensor(dst, over(src, G), mask[:, :, :], ALU.mult).then_inc(masked, 1)

            norm_pool(core, pool, s_var, s_rstd)
            prepare(0, 0)
            prepare(1, 1)
            with pool.Fori(0, (B - 2) // 2) as i:
                prepare(2 * i + 2, 0)
                prepare(2 * i + 3, 1)

        @block.scalar
        def _(act):
            def copy_n(b):
                act.wait_ge(n_turned, b + 1)
                dst = m.qT if cross else m.nT
                act.activation(dst[:, :], bank_p[:, 0:T], ACT.Copy)\
                    .then_inc(qk_copied if cross else n_copied, 1)

            def copy_qkv(b, par):
                v_dst = m.v[:, par, :, 0:DH]
                if cross:
                    act.activation(v_dst, m.ctx[:, b, :].rearrange("p (h d) -> p h d", d=DH), ACT.Copy)\
                        .then_inc(v_copied, 1)
                    return
                act.wait_ge(projected, b + 1)
                act.activation(m.qT[:, :], bank_p[:, T:2 * T], ACT.Copy).then_inc(qk_copied, 1)
                act.activation(m.kT[:, :], bank_p[:, 2 * T:3 * T], ACT.Copy).then_inc(qk_copied, 1)
                act.activation(v_dst, bank_p[:, 3 * T:3 * T + D].rearrange("p (h d) -> p h d", d=DH), ACT.Copy)\
                    .then_inc(v_copied, 1)

            def exps(b, g):
                act.wait_ge(shifted, G * b + g + 1)
                act.activation(m.p[:, g, :, :], bank_st[g % 2][:, :].rearrange("p (j t) -> p j t", j=J),
                               ACT.Exp, scale=scale).then_inc(exped, 1)

            def copy_raw(b):
                act.wait_ge(pv_done, b + 1)
                act.activation(m.o_raw[:, :, :], bank_v[:, :].rearrange("p (g t) -> p g t", g=G), ACT.Copy)\
                    .then_inc(raw_copied, 1)

            def copy_o(b):
                act.wait_ge(o_turned, b + 1)
                act.activation(m.oT[:, :], bank_z[:, D:D + T], ACT.Copy).then_inc(o_copied, 1)

            def step(b, par, first=False, last=False):
                if not first:
                    copy_raw(b - 1)
                exps(b, 0)
                exps(b, 1)
                if not last:
                    copy_n(b + 1)
                exps(b, 2)
                if not first:
                    copy_o(b - 1)
                if not last:
                    copy_qkv(b + 1, 1 - par)
                exps(b, 3)

            copy_n(0)
            copy_qkv(0, 0)
            step(0, 0, first=True)
            with act.Fori(0, (B - 2) // 2) as i:
                step(2 * i + 1, 1)
                step(2 * i + 2, 0)
            step(LAST, 1, last=True)
            copy_raw(LAST)
            copy_o(LAST)

        @block.tensor
        def _(pe):
            def turn(b, par):
                pe.wait_ge(normed, b + 1)
                pe.transpose(bank_p[:, 0:T], m.n[:, par, :], core.ident[:, :]).then_inc(n_turned, 1)

            def project(b):
                if cross:
                    return
                pe.wait_ge(n_copied, b + 1)
                pe.matmul(bank_p[:, T:2 * T], m.wq[:, :], m.nT[:, :], start=True, stop=True)
                pe.matmul(bank_p[:, 2 * T:3 * T], m.wk[:, :], m.nT[:, :], start=True, stop=True)
                pe.matmul(bank_p[:, 3 * T:3 * T + D], m.nT[:, :], m.wv[:, :], start=True, stop=True)\
                    .then_inc(projected, 1)

            def scores(b, g):
                if g == 0:
                    pe.wait_ge(masked, 4 * b + 2)
                if g >= 2:
                    pe.wait_ge(maxed, G * b + g - 1)
                pe.matmul(bank_s[g % 2][:, :], m.q_gb[:, g, :],
                          m.k_jb[:, :, :].rearrange("p j t -> p (j t)"), start=True, stop=True)\
                    .then_inc(scored, 1)

            def shifted_scores(b, par, g):
                if g == 0:
                    pe.wait_ge(masked, 4 * b + 4)
                if g >= 2:
                    pe.wait_ge(exped, G * b + g - 1)
                pe.wait_ge(maxed, G * b + g + 1)
                for j in range(J):
                    h = J * g + j
                    pe.matmul(bank_st[g % 2][:, j * T:(j + 1) * T],
                              m.nmax[:, h:h + 1].to_broadcast([T, T]), core.ident_b[:, :],
                              start=(j == 0), stop=False, skip_group_check=True)
                pe.matmul(bank_st[g % 2][:, :], m.k_g[:, par, g, :],
                          m.q_j[:, par, :, :].rearrange("p j t -> p (j t)"), start=False, stop=True,
                          skip_group_check=True).then_inc(shifted, 1)

            def values(b, par):
                pe.wait_ge(v_copied, b + 1)
                pe.wait_ge(exped, G * (b + 1))
                for g in range(G):
                    for j in range(J):
                        mm = pe.matmul(bank_v[32 * j:32 * j + 32, g * T:(g + 1) * T],
                                       m.v[:, par, J * g + j, :], m.p[:, g, j, :], start=True, stop=True)
                mm.then_inc(pv_done, 1)

            def turn_raw(b):
                pe.wait_ge(raw_copied, b + 1)
                for g in range(G):
                    mm = pe.transpose(bank_d[:, g * T:(g + 1) * T], m.o_raw[:, g, :], core.ident[:, :])
                mm.then_inc(raw_turned, 1)

            def turn_o(b):
                pe.wait_ge(o_done, b + 1)
                pe.transpose(bank_z[:, D:D + T], m.o[:, :, :].rearrange("p h d -> p (h d)"), core.ident[:, :])\
                    .then_inc(o_turned, 1)

            def out(b):
                pe.wait_ge(o_copied, b + 1)
                pe.matmul(bank_z[:, 0:D], m.oT[:, :], m.w_out[layer][:, :], start=True, stop=True)\
                    .then_inc(out_done, 1)

            def step(b, par, first=False, last=False):
                shifted_scores(b, par, 0)
                if not first:
                    turn_raw(b - 1)
                shifted_scores(b, par, 1)
                if not last:
                    pe.wait_ge(v_copied, b + 1)
                    turn(b + 1, 1 - par)
                if not first:
                    turn_o(b - 1)
                shifted_scores(b, par, 2)
                if not last:
                    project(b + 1)
                if not first:
                    out(b - 1)
                shifted_scores(b, par, 3)
                if not last:
                    scores(b + 1, 0)
                    scores(b + 1, 1)
                values(b, par)
                if not last:
                    scores(b + 1, 2)
                    scores(b + 1, 3)

            turn(0, 0)
            project(0)
            for g in range(G):
                scores(0, g)
            step(0, 0, first=True)
            with pe.Fori(0, (B - 2) // 2) as i:
                step(2 * i + 1, 1)
                step(2 * i + 2, 0)
            step(LAST, 1, last=True)
            turn_raw(LAST)
            turn_o(LAST)
            out(LAST)


H3 = 512
CH = H3 // 128
STAGES = 9
Q = 4


class FoldMem:

    def __init__(self, core):
        sb = core.sb
        self.w_up = [sb(f"fo_up{i}", [D, H3]) for i in range(2)]
        self.b_up = [sb(f"fo_bias{i}", [1, H3]) for i in range(2)]
        self.w_down = [sb(f"fo_down{i}", [D, H3]) for i in range(2)]
        self.up_bias = sb("fo_up_bias", [128, CH])
        self.bias_col = sb("fo_bias_col", [128, CH])
        self.down = sb("fo_down", [128, CH, D])
        self.out_bias = sb("fo_out_bias", [T, 2, D])


def butterfly_stage(eng, stage, transposed, w, src, dst, part, done, count):
    s = 1 << stage
    for o in range(2):
        pair = w[:, :, o, :] if transposed else w[:, o, :, :]
        eng.tensor_tensor(part[:, o, :].rearrange("p (n i s) -> p n i s", i=2, s=s),
                          pair.rearrange("p i (n s) -> p n i s", s=s),
                          src.rearrange("p (n i s) -> p n i s", i=2, s=s), ALU.mult).then_inc(done, 1)
    count += 2
    eng.wait_ge(done, count)
    for o in range(2):
        prod = part[:, o, :].rearrange("p (n i s) -> p n i s", i=2, s=s)
        eng.tensor_tensor(dst.rearrange("p (n i s) -> p n i s", i=2, s=s)[:, :, o, :],
                          prod[:, :, 0, :], prod[:, :, 1, :], ALU.add).then_inc(done, 1)
    count += 2
    eng.wait_ge(done, count)
    return count


def fold_butterflies(core, f, a):
    nc = core.nc
    up_loaded, down_loaded, up_done, down_done, turned = core.sems("fo", "up_loaded down_loaded up_done down_done "
                                                                    "turned")
    with ExitStack() as ctx:
        def sb(name, shape):
            return ctx.enter_context(nc.sbuf_tensor(name, shape, FP32))

        w_up = sb("fo_w_up", [D, STAGES, 2, 2, H3 // 2])
        w_down = sb("fo_w_down", [D, STAGES, 2, 2, H3 // 2])
        part_up, part_down, part_bias = sb("fo_part_up", [D, 2, H3]), sb("fo_part_down", [D, 2, H3]), \
            sb("fo_part_bias", [1, 2, H3])
        with nc.Block() as block:
            @block.sync
            def _(sp):
                sp.dma_start(f.w_up[0][:, :], a["L0_ffn_W_exp"]).then_inc(up_loaded, 16)
                sp.dma_start(f.b_up[0][:, :], a["L0_ffn_b_exp"].unsqueeze(0)).then_inc(up_loaded, 16)
                sp.dma_start(f.up_bias[:, :], a["up_bias_col"]).then_inc(up_loaded, 16)
                sp.dma_start(f.out_bias[:, 0, :], a["L0_ffn_b_con"].partition_broadcast(T)).then_inc(up_loaded, 16)
                sp.dma_start(f.out_bias[:, 1, :], a["L0_ffn_down_bias"].partition_broadcast(T)).then_inc(up_loaded, 16)
                for k in range(STAGES):
                    sp.dma_start(w_up[:, k, :, :, :].rearrange("p o i k -> p (o i k)"),
                                 a["up_planes"][k].partition_broadcast(D)).then_inc(up_loaded, 16)

            @block.scalar
            def _(act):
                act.dma_start(f.w_down[0][:, :], a["W_conT"]).then_inc(down_loaded, 16)
                for k in reversed(range(STAGES)):
                    act.dma_start(w_down[:, k, :, :, :].rearrange("p o i k -> p (o i k)"),
                                  a["down_planes"][k].partition_broadcast(D)).then_inc(down_loaded, 16)
                act.wait_ge(down_loaded, 16 * (STAGES + 1))

            @block.vector
            def _(dve):
                done = 0
                dve.wait_ge(up_loaded, 16 * (5 + STAGES))
                for k in range(STAGES):
                    w = w_up[:, k, :, :, :]
                    done = butterfly_stage(dve, k, False, w, f.w_up[k % 2][:, :], f.w_up[1 - k % 2][:, :],
                                           part_up, up_done, done)
                    done = butterfly_stage(dve, k, False, w[0:1], f.b_up[k % 2][:, :], f.b_up[1 - k % 2][:, :],
                                           part_bias, up_done, done)
                dve.wait_ge(turned, 1)
                dve.tensor_tensor(f.bias_col[:, :], core.bank[0][:, 0:CH], f.up_bias[:, :], ALU.add)\
                    .then_inc(up_done, 1)
                dve.tensor_copy(f.down[:, :, :], core.bank[1][:, :].rearrange("p (c d) -> p c d", c=CH))\
                    .then_inc(up_done, 1)
                dve.wait_ge(up_done, done + 2)

            @block.gpsimd
            def _(pool):
                done = 0
                pool.wait_ge(down_loaded, 16 * (STAGES + 1))
                for n, k in enumerate(reversed(range(STAGES))):
                    done = butterfly_stage(pool, k, True, w_down[:, k, :, :, :], f.w_down[n % 2][:, :],
                                           f.w_down[1 - n % 2][:, :], part_down, down_done, done)
                pool.wait_ge(up_loaded, 16 * (5 + STAGES))
                pool.tensor_tensor(f.out_bias[:, 0, :], f.out_bias[:, 0, :], f.out_bias[:, 1, :], ALU.add)\
                    .then_inc(down_done, 1)
                pool.wait_ge(down_done, done + 1)

            @block.tensor
            def _(pe):
                pe.wait_ge(up_done, 8 * STAGES)
                for c in range(CH):
                    pe.matmul(core.bank[0][:, c:c + 1], f.b_up[STAGES % 2][:, c * 128:(c + 1) * 128],
                              core.ones[0:1, 0:1], start=True, stop=True)
                pe.wait_ge(down_done, 4 * STAGES)
                for c in range(CH):
                    mm = pe.transpose(core.bank[1][:, c * D:(c + 1) * D],
                                      f.w_down[STAGES % 2][:, c * 128:(c + 1) * 128], core.ident[:, :])
                mm.then_inc(turned, 1)


def feed_forward(core, f):
    nc = core.nc
    s_var, s_rstd, normed, turned, n_copied, biased, up_done, gelu_done, down_done, x_done = core.sems(
        "ff", "var rstd normed turned n_copied biased up_done gelu_done down_done x_done")
    bank_n, bank_up, bank_down = core.bank[0], core.bank[1:3], core.bank[3:7]
    groups = B // Q
    with ExitStack() as ctx:
        def sb(name, shape):
            return ctx.enter_context(nc.sbuf_tensor(name, shape, FP32))

        n = sb("ff_n", [T, Q, D])
        nT = sb("ff_nT", [D, Q * T])
        h = sb("ff_h", [128, CH, Q * T])
        w_up = f.w_up[STAGES % 2]
        with nc.Block() as block:
            @block.vector
            def _(dve):
                def prepare(q):
                    for i in range(Q):
                        normalise(core, dve, n[:, i, :], Q * q + i).then_inc(normed, 1)
                    dve.wait_ge(turned, q + 1)
                    dve.tensor_copy(nT[:, :], bank_n[:, :]).then_inc(n_copied, 1)

                def finish(q):
                    dve.wait_ge(down_done, q + 1)
                    dve.wait_ge(biased, Q * (q + 1))
                    for i in range(Q):
                        dve.tensor_tensor(core.x[:, Q * q + i, :], bank_down[i][:, 0:D], core.x[:, Q * q + i, :],
                                          ALU.add).then_inc(x_done, 1)
                    for i in range(Q):
                        dve.wait_ge(x_done, Q * q + i + 1)
                        dve.bn_stats(core.stats[:, Q * q + i, :], core.x[:, Q * q + i, :]).then_inc(s_var, 1)

                norm_dve(core, dve, s_var)
                dve.wait_ge(s_rstd, 2)
                prepare(0)
                with dve.Fori(0, groups - 1) as q:
                    prepare(q + 1)
                    finish(q)
                finish(groups - 1)
                dve.wait_ge(s_var, 6 + B)

            @block.gpsimd
            def _(pool):
                norm_pool(core, pool, s_var, s_rstd)
                with pool.Fori(0, B) as b:
                    pool.wait_ge(normed, b + 1)
                    pool.tensor_tensor(core.x[:, b, :], core.x[:, b, :], f.out_bias[:, 0, :], ALU.add)\
                        .then_inc(biased, 1)

            @block.scalar
            def _(act):
                with act.Fori(0, groups) as q:
                    for c in range(CH):
                        act.wait_ge(up_done, CH * q + c + 1)
                        act.activation(h[:, c, :], bank_up[c % 2][:, :], ACT.Gelu, bias=f.bias_col[:, c:c + 1])\
                            .then_inc(gelu_done, 1)

            @block.tensor
            def _(pe):
                def turn(q):
                    pe.wait_ge(normed, Q * (q + 1))
                    for i in range(Q):
                        mm = pe.transpose(bank_n[:, i * T:(i + 1) * T], n[:, i, :], core.ident[:, :])
                    mm.then_inc(turned, 1)

                def up(q, c):
                    if c == 0:
                        pe.wait_ge(n_copied, q + 1)
                    if c >= 2:
                        pe.wait_ge(gelu_done, CH * q + c - 1)
                    pe.matmul(bank_up[c % 2][:, :], w_up[:, c * 128:(c + 1) * 128], nT[:, :],
                              start=True, stop=True).then_inc(up_done, 1)

                def down(q, c, first):
                    pe.wait_ge(gelu_done, CH * q + c + 1)
                    if c == 0 and not first:
                        pe.wait_ge(x_done, Q * q)
                    for i in range(Q):
                        mm = pe.matmul(bank_down[i][:, 0:D], h[:, c, i * T:(i + 1) * T], f.down[:, c, :],
                                       start=(c == 0), stop=(c == CH - 1))
                    if c == CH - 1:
                        mm.then_inc(down_done, 1)

                def step(q, first=False, last=False):
                    up(q, 0)
                    up(q, 1)
                    down(q, 0, first)
                    up(q, 2)
                    down(q, 1, first)
                    up(q, 3)
                    down(q, 2, first)
                    if not last:
                        turn(q + 1)
                    down(q, 3, first)

                turn(0)
                step(0, first=True)
                with pe.Fori(1, groups - 1) as q:
                    step(q)
                step(groups - 1, last=True)


H4, K4 = 8, 64
C4 = H4 * K4 // 128
DEN_EPS = 1e-6


class LinMem:
    def __init__(self, core):
        sb = core.sb
        self.wq, self.wk, self.wv, self.wg = (sb(f"li_{w}", [D, C4 * 128]) for w in ("wq", "wk", "wv", "wg"))
        self.wo = sb("li_wo", [128, C4, D])
        self.gate_bias = sb("li_gate_bias", [128, C4])
        self.decay = sb("li_decay", [T, H4])
        self.gap = sb("li_gap", [T, T])
        self.tri = sb("li_tri", [T, T])
        self.mask = sb("li_mask", [T, H4, T])


def linear_setup(core, m, a):
    nc = core.nc
    loaded, done, raised = core.sems("ls", "loaded done raised")
    with nc.Block() as block:
        @block.sync
        def _(sp):
            for dst, src in ((m.decay, a["L1_attn_decay_log"].partition_broadcast(T)), (m.gap, a["c_gap"]),
                             (m.tri, a["c_tri"]), (m.wq, a["lin_WqT"]), (m.wk, a["lin_WkT"]), (m.wv, a["lin_WvT"]),
                             (m.wg, a["lin_WgT"]), (m.gate_bias, a["gate_bias_col"])):
                sp.dma_start(dst[:, :], src).then_inc(loaded, 16)
            sp.dma_start(m.wo[:, :, :], a["lin_WoT"].rearrange("(c p) e -> p c e", p=128)).then_inc(loaded, 16)
            sp.wait_ge(loaded, 16 * 9)

        @block.vector
        def _(dve):
            dve.wait_ge(loaded, 16 * 9)
            dve.tensor_scalar(m.decay[:, :], m.decay[:, :], -80.0, None, ALU.max).then_inc(done, 1)
            dve.tensor_scalar(m.gate_bias[:, :], m.gate_bias[:, :], 0.5, None, ALU.mult).then_inc(done, 1)
            dve.wait_ge(raised, 2)
            dve.tensor_scalar(m.decay[:, :], m.decay[:, :], -1.0, None, ALU.mult).then_inc(done, 1)
            dve.wait_ge(raised, 2 + H4)
            dve.tensor_tensor(m.mask[:, :, :], m.mask[:, :, :], over(m.tri[:, :], H4), ALU.mult).then_inc(done, 1)
            dve.wait_ge(done, 4)

        @block.scalar
        def _(act):
            act.wait_ge(done, 1)
            act.activation(m.decay[:, :], m.decay[:, :], ACT.Exp, scale=-1.0).then_inc(raised, 1)
            act.wait_ge(raised, 1)
            act.activation(m.decay[:, :], m.decay[:, :], ACT.Ln, bias=1.0).then_inc(raised, 1)
            act.wait_ge(done, 3)
            for h in range(H4):
                act.activation(m.mask[:, h, :], m.gap[:, :], ACT.Exp, scale=m.decay[:, h:h + 1]).then_inc(raised, 1)


def linear_attention(core, m):
    nc = core.nc
    (s_var, s_rstd, normed, turned, n_copied, k_proj, q_proj, gate_proj, v_proj, clipped, raised, tanhed,
     v_copied, zeroed, phi_done, a_done, decayed, num_done, den_done, inv_done, y_done, y_turned, gated, out_done,
     x_done) = core.sems(
        "li", "var rstd normed turned n_copied k_proj q_proj gate_proj v_proj clipped raised tanhed v_copied "
        "zeroed phi_done a_done decayed num_done den_done inv_done y_done y_turned gated out_done x_done")
    bank_q, bank_k, bank_g, bank_v = core.bank[0:4]
    bank_a, bank_num = core.bank[4:6], core.bank[6:8]
    bank_y, bank_z = core.bank[4:6]
    half = H4 // 2
    V1 = K4 + 1

    def by_chunk(ap):
        return ap.rearrange("p (c t) -> p c t", c=C4)

    with ExitStack() as ctx:
        def sb(name, shape):
            return ctx.enter_context(nc.sbuf_tensor(name, shape, FP32))

        n = sb("li_n", [T, D])
        nT = sb("li_nT", [D, T])
        clip_k, clip_q = sb("li_clip_k", [128, C4, T]), sb("li_clip_q", [128, C4, T])
        exp_k, exp_q = sb("li_exp_k", [128, C4, T]), sb("li_exp_q", [128, C4, T])
        phi_k = sb("li_phi_k", [128, C4, T])
        phi_q = sb("li_phi_q", [128, C4, 2, T])
        v = sb("li_v", [T, H4, V1])
        tanh = sb("li_tanh", [128, C4, T])
        am = sb("li_am", [T, H4, T])
        den, inv = sb("li_den", [T, H4]), sb("li_inv", [T, H4])
        y = sb("li_y", [T, H4, K4])
        yT = sb("li_yT", [128, C4, T])

        with nc.Block() as block:
            @block.vector
            def _(dve):
                def prepare(b):
                    normalise(core, dve, n[:, :], b).then_inc(normed, 1)

                def phi(b):
                    dve.wait_ge(raised, 2 * b + 1)
                    dve.scalar_tensor_tensor(out=phi_k[:, :, :], in0=by_chunk(bank_k[:, :]), scalar=0.0,
                                             in1=exp_k[:, :, :], op0=ALU.max, op1=ALU.add).then_inc(phi_done, 1)
                    dve.wait_ge(raised, 2 * b + 2)
                    for r in range(2):
                        rows = slice(64 * r, 64 * r + 64)
                        dve.scalar_tensor_tensor(out=phi_q[rows, :, r, :], in0=by_chunk(bank_q[rows, :]), scalar=0.0,
                                                 in1=exp_q[rows, :, :], op0=ALU.max, op1=ALU.add)\
                            .then_inc(phi_done, 1)

                def decay(b):
                    for i in range(2):
                        dve.wait_ge(a_done, 2 * b + i + 1)
                        dve.tensor_tensor(am[:, half * i:half * i + half, :],
                                          bank_a[i][:, :].rearrange("p (h t) -> p h t", h=half),
                                          m.mask[:, half * i:half * i + half, :], ALU.mult).then_inc(decayed, 1)

                def divide(b):
                    dve.wait_ge(num_done, b + 1)
                    for i in range(2):
                        num = bank_num[i][:, 0:half * V1].rearrange("p (h w) -> p h w", w=V1)
                        dve.tensor_scalar(den[:, half * i:half * i + half], num[:, :, K4], DEN_EPS, 2.0,
                                          ALU.add, ALU.mult).then_inc(den_done, 1)
                    dve.wait_ge(den_done, 2 * b + 2)
                    dve.reciprocal(inv[:, :], den[:, :]).then_inc(inv_done, 1)
                    dve.wait_ge(inv_done, b + 1)
                    for i in range(2):
                        num = bank_num[i][:, 0:half * V1].rearrange("p (h w) -> p h w", w=V1)
                        dve.tensor_tensor(y[:, half * i:half * i + half, :], num[:, :, 0:K4],
                                          inv[:, half * i:half * i + half].unsqueeze(2)
                                          .to_broadcast([T, half, K4]), ALU.mult).then_inc(y_done, 1)

                def gate(b):
                    dve.wait_ge(y_turned, b + 1)
                    dve.wait_ge(tanhed, b + 1)
                    dve.scalar_tensor_tensor(out=yT[:, :, :], in0=tanh[:, :, :], scalar=1.0,
                                             in1=by_chunk(bank_y[:, :]), op0=ALU.add, op1=ALU.mult)\
                        .then_inc(gated, 1)

                def finish(b):
                    dve.wait_ge(out_done, b + 1)
                    dve.tensor_tensor(core.x[:, b, :], bank_z[:, 0:D], core.x[:, b, :], ALU.add).then_inc(x_done, 1)
                    dve.wait_ge(x_done, b + 1)
                    dve.bn_stats(core.stats[:, b, :], core.x[:, b, :]).then_inc(s_var, 1)

                def step(b, last=False):
                    if not last:
                        prepare(b + 1)
                    decay(b)
                    divide(b)
                    if not last:
                        phi(b + 1)
                    gate(b)
                    finish(b)

                dve.memset(phi_q[:, :, :, :], 0.0).then_inc(zeroed, 1)
                dve.memset(v[:, :, K4:V1], 1.0).then_inc(zeroed, 1)
                norm_dve(core, dve, s_var)
                dve.wait_ge(s_rstd, 2)
                prepare(0)
                dve.wait_ge(zeroed, 2)
                phi(0)
                with dve.Fori(0, B - 1) as b:
                    step(b)
                step(B - 1, last=True)
                dve.wait_ge(s_var, 6 + B)

            @block.gpsimd
            def _(pool):
                norm_pool(core, pool, s_var, s_rstd)

            @block.scalar
            def _(act):
                def prepare(b, first=False):
                    act.wait_ge(turned, b + 1)
                    act.activation(nT[:, :], bank_v[:, 0:T], ACT.Copy).then_inc(n_copied, 1)
                    for i, (proj, bank, clip, ex) in enumerate(((k_proj, bank_k, clip_k, exp_k),
                                                                (q_proj, bank_q, clip_q, exp_q))):
                        act.wait_ge(proj, b + 1)
                        act.activation(clip[:, :, :], by_chunk(bank[:, :]), ACT.Relu, scale=-1.0)\
                            .then_inc(clipped, 1)
                        act.wait_ge(clipped, 2 * b + i + 1)
                        act.activation(ex[:, :, :], clip[:, :, :], ACT.Exp, scale=-1.0).then_inc(raised, 1)
                    act.wait_ge(v_proj, b + 1)
                    act.activation(v[:, :, 0:K4], bank_v[:, :].rearrange("p (h w) -> p h w", h=H4), ACT.Copy)\
                        .then_inc(v_copied, 1)
                    act.wait_ge(gate_proj, b + 1)
                    if not first:
                        act.wait_ge(gated, b)
                    for c in range(C4):
                        ins = act.activation(tanh[:, c, :], bank_g[:, c * T:(c + 1) * T], ACT.Tanh,
                                             bias=m.gate_bias[:, c:c + 1], scale=0.5)
                    ins.then_inc(tanhed, 1)

                act.wait_ge(zeroed, 2)
                prepare(0, first=True)
                with act.Fori(1, B) as b:
                    prepare(b)

            @block.tensor
            def _(pe):
                def turn(b):
                    pe.wait_ge(normed, b + 1)
                    pe.transpose(bank_v[:, 0:T], n[:, :], core.ident[:, :]).then_inc(turned, 1)

                def project(b, w, bank, proj):
                    for c in range(C4):
                        mm = pe.matmul(bank[:, c * T:(c + 1) * T], w[:, c * 128:(c + 1) * 128], nT[:, :],
                                       start=True, stop=True)
                    mm.then_inc(proj, 1)

                def project_kq(b):
                    pe.wait_ge(n_copied, b + 1)
                    project(b, m.wk, bank_k, k_proj)
                    project(b, m.wq, bank_q, q_proj)

                def project_gv(b, first=False):
                    pe.matmul(bank_v[:, :], nT[:, :], m.wv[:, :], start=True, stop=True).then_inc(v_proj, 1)
                    if not first:
                        pe.wait_ge(tanhed, b)
                    project(b, m.wg, bank_g, gate_proj)

                def attend(b, first=False):
                    pe.wait_ge(phi_done, 3 * (b + 1))
                    for c in range(C4):
                        if c == C4 // 2 and not first:
                            pe.wait_ge(x_done, b)
                        mm = pe.matmul(bank_a[c // 2][:, 256 * (c % 2):256 * (c % 2) + 256], phi_k[:, c, :],
                                       phi_q[:, c, :, :].rearrange("p r t -> p (r t)"), start=True, stop=True)
                        if c % 2:
                            mm.then_inc(a_done, 1)

                def numerator(b):
                    pe.wait_ge(v_copied, b + 1)
                    for h in range(H4):
                        if h % half == 0:
                            pe.wait_ge(decayed, 2 * b + h // half + 1)
                        i = h % half
                        mm = pe.matmul(bank_num[h // half][:, i * V1:(i + 1) * V1], am[:, h, :], v[:, h, :],
                                       start=True, stop=True)
                    mm.then_inc(num_done, 1)

                def turn_y(b):
                    pe.wait_ge(y_done, 2 * b + 2)
                    for c in range(C4):
                        mm = pe.transpose(bank_y[:, c * T:(c + 1) * T],
                                          y[:, 2 * c:2 * c + 2, :].rearrange("p h w -> p (h w)"), core.ident[:, :])
                    mm.then_inc(y_turned, 1)

                def out(b):
                    pe.wait_ge(gated, b + 1)
                    for c in range(C4):
                        mm = pe.matmul(bank_z[:, 0:D], yT[:, c, :], m.wo[:, c, :],
                                       start=(c == 0), stop=(c == C4 - 1))
                    mm.then_inc(out_done, 1)

                def step(b, first=False, last=False):
                    attend(b, first)
                    if not last:
                        pe.wait_ge(v_copied, b + 1)
                        turn(b + 1)
                        project_kq(b + 1)
                    numerator(b)
                    if not last:
                        project_gv(b + 1)
                    turn_y(b)
                    out(b)

                turn(0)
                project_kq(0)
                project_gv(0, first=True)
                step(0, first=True)
                with pe.Fori(1, B - 1) as b:
                    step(b)
                step(B - 1, last=True)


NH5 = 16
D5 = D // NH5
TOP = 4
COS, SIN, CAS, SAC = range(4)
BH = B * NH5
HALVES = BH // 128


def autocorrelation(core, a):
    nc = core.nc
    groups = B // Q
    (loaded, ctx_loaded0, ctx_loaded1, zeroed, scaled, s_var, s_rstd, normed, q_turned, c_turned, zq_copied, zc_copied, projected, read,
     spectra, odd_done, even_done, diff_done, summed, corr_done, corr_copied, top, idx, coded, w_sum, w_exp, kernels,
     k_turned, k_copied, k_spec, k_spec_copied, biased, y_part, y_done, o_done, o_copied, out_done, x_done) = core.sems(
        "au", "loaded ctx_loaded0 ctx_loaded1 zeroed scaled var rstd normed q_turned c_turned zq_copied zc_copied projected read "
        "spectra odd_done even_done diff_done summed corr_done corr_copied top idx coded w_sum w_exp kernels "
        "k_turned k_copied k_spec k_spec_copied biased y_part y_done o_done o_copied out_done x_done")
    ctx_loaded = (ctx_loaded0, ctx_loaded1)
    bank_zq, bank_zc = core.bank[0:2]
    bank_qc, bank_qs, bank_ke, bank_ko, bank_vc, bank_vs = core.bank[2:8]

    def four(ap):
        return ap.rearrange("p (i d) -> p i d", i=Q)

    with ExitStack() as ctx:
        def sb(name, shape, dt=FP32):
            return ctx.enter_context(nc.sbuf_tensor(name, shape, dt))

        dft = sb("au_dft", [T, 4, T])
        inv = sb("au_inv", [T, T])
        wq, wk, wv, wo = (sb(f"au_{w}", [D, D]) for w in ("wq", "wk", "wv", "wo"))
        bias = [sb(f"au_bias_{w}", [T, Q, D]) for w in ("q", "k", "v")]
        out_bias = sb("au_out_bias", [T, D])
        iota = sb("au_iota", [128, T])
        n = sb("au_n", [T, 2, Q, D])
        cx = sb("au_ctx", [T, 2, Q, D])
        zq = sb("au_zq", [D, 2, 2, T])
        zc = sb("au_zc", [D, 2, 4, T])
        q_cas, q_sac = sb("au_q_cas", [T, Q, D]), sb("au_q_sac", [T, Q, D])
        k_even = sb("au_k_even", [T, Q, D])
        even, odd = sb("au_even", [T, 2, Q, D]), sb("au_odd", [T, 2, Q, D])
        v_cas, v_sac = sb("au_v_cas", [T, B, D]), sb("au_v_sac", [T, B, D])
        spec = sb("au_spec", [T, B, NH5])
        corr = sb("au_corr", [128, HALVES, T])
        top_v = sb("au_top_v", [128, HALVES, 8])
        top_i = sb("au_top_i", [128, HALVES, 8], U32)
        lag = sb("au_lag", [128, HALVES, 8])
        w, w_tot, w_inv = sb("au_w", [128, HALVES, TOP]), sb("au_w_tot", [128, HALVES]), sb("au_w_inv", [128, HALVES])
        pick = sb("au_pick", [128, HALVES, TOP, T])
        kern_t = sb("au_kern_t", [T, BH])
        k_sp = sb("au_k_sp", [T, 2, B, NH5])
        y_even, y_odd = sb("au_y_even", [T, 2, Q, D]), sb("au_y_odd", [T, 2, Q, D])
        oT = sb("au_oT", [D, 2, T])

        with nc.Block() as block:
            @block.sync
            def _(sp):
                def load_ctx(g):
                    sp.dma_start(cx[:, g % 2, :, :],
                                 a["ctx_1024"][Q * g:Q * g + Q].rearrange("b t d -> t b d"))\
                        .then_inc(ctx_loaded[g % 2], 16)

                sp.dma_start(dft[:, :, :], a["c_dft"].rearrange("p (k t) -> p k t", k=4)).then_inc(loaded, 16)
                load_ctx(0)
                for dst, src in ((wq, "auto_WqT"), (wk, "auto_WkT"), (wv, "auto_WvT"), (wo, "auto_WoT"),
                                 (iota, "c_iota")):
                    sp.dma_start(dst[:, :], a[src]).then_inc(loaded, 16)
                sp.dma_start(out_bias[:, :], a["L1_xattn_bo"].partition_broadcast(T)).then_inc(loaded, 16)
                load_ctx(1)
                sp.wait_ge(zeroed, 3)
                for dst, src in zip(bias, ("L1_xattn_bq", "L1_xattn_bk", "L1_xattn_bv")):
                    for i in range(Q):
                        sp.dma_start(dst[0:1, i, :], a[src].unsqueeze(0)).then_inc(loaded, 16)
                for g in range(2, groups):
                    sp.wait_ge(c_turned, Q * (g - 1))
                    load_ctx(g)

            @block.vector
            def _(dve):
                def prepare(g, par):
                    for i in range(Q):
                        normalise(core, dve, n[:, par, i, :], Q * g + i).then_inc(normed, 1)

                def correlate(g, par):
                    dve.wait_ge(projected, Q * (g + 1))
                    dve.wait_ge(even_done, g)
                    for dst, bank, b in ((q_cas[:, :, :], bank_qc, bias[0]), (k_even[:, :, :], bank_ke, bias[1]),
                                         (q_sac[:, :, :], bank_qs, bias[0]),
                                         (v_cas[:, bass.ds(Q * g, Q), :], bank_vc, bias[2]),
                                         (v_sac[:, bass.ds(Q * g, Q), :], bank_vs, bias[2])):
                        dve.tensor_tensor(dst, four(bank[:, :]), b[:, :, :], ALU.add).then_inc(spectra, 1)
                    dve.wait_ge(spectra, 5 * g + 3)
                    dve.tensor_tensor(odd[:, par, :, :], four(bank_ko[:, :]), q_sac[:, :, :], ALU.mult)\
                        .then_inc(odd_done, 1)

                def head_sums(g, par):
                    dve.wait_ge(diff_done, g + 1)
                    dve.tensor_reduce(spec[:, bass.ds(Q * g, Q), :],
                                      even[:, par, :, :].rearrange("p i (h d) -> p i h d", d=D5), AX.X, ALU.add)\
                        .then_inc(summed, 1)

                for t in bias:
                    dve.memset(t[:, :, :], 0.0).then_inc(zeroed, 1)
                norm_dve(core, dve, s_var)
                dve.wait_ge(s_rstd, 2)
                prepare(0, 0)
                prepare(1, 1)
                dve.wait_ge(loaded, 16 * (7 + 3 * Q))
                for t in bias:
                    dve.tensor_scalar(t[0:1, :, :], t[0:1, :, :], float(T), None, ALU.mult).then_inc(scaled, 1)
                dve.tensor_scalar(inv[:, :], dft[:, CAS, :], 1.0 / T, None, ALU.mult).then_inc(scaled, 1)
                dve.wait_ge(scaled, 4)
                dve.sem_inc(even_done, 1)
                for g in range(groups):
                    correlate(g, g % 2)
                    if g + 2 < groups:
                        dve.wait_ge(q_turned, Q * (g + 1))
                        prepare(g + 2, g % 2)
                    head_sums(g, g % 2)

                for i in range(HALVES):
                    dve.wait_ge(corr_copied, i + 1)
                    dve.max(top_v[:, i, :], corr[:, i, :]).then_inc(top, 1)
                dve.wait_ge(top, HALVES)
                for i in range(HALVES):
                    dve.max_index(top_i[:, i, :], top_v[:, i, :], corr[:, i, :]).then_inc(idx, 1)
                dve.tensor_tensor(w[:, :, :], top_v[:, :, 0:TOP], top_v[:, :, 0:1].to_broadcast([128, HALVES, TOP]),
                                  ALU.subtract).then_inc(coded, 1)
                dve.wait_ge(idx, HALVES)
                dve.tensor_copy(lag[:, :, :], top_i[:, :, :]).then_inc(coded, 1)
                dve.wait_ge(w_exp, 1)
                dve.tensor_reduce(w_tot[:, :], w[:, :, :], AX.X, ALU.add).then_inc(w_sum, 1)
                dve.wait_ge(w_sum, 1)
                dve.reciprocal(w_inv[:, :], w_tot[:, :]).then_inc(w_sum, 1)
                dve.wait_ge(w_sum, 2)
                dve.tensor_tensor(w[:, :, :], w[:, :, :], w_inv[:, :].unsqueeze(2).to_broadcast([128, HALVES, TOP]),
                                  ALU.mult).then_inc(w_sum, 1)
                dve.wait_ge(w_sum, 3)
                dve.wait_ge(coded, 2)
                for i in range(HALVES):
                    for k in range(TOP):
                        dve.tensor_scalar(pick[:, i, k, :], iota[:, :], lag[:, i, k:k + 1], w[:, i, k:k + 1],
                                          ALU.is_equal, ALU.mult).then_inc(kernels, 1)
                count = HALVES * TOP
                for step in (2, 1):
                    dve.wait_ge(kernels, count)
                    dve.tensor_tensor(pick[:, :, 0:step, :], pick[:, :, 0:step, :], pick[:, :, step:2 * step, :],
                                      ALU.add).then_inc(kernels, 1)
                    count += 1

                def convolve(g, par):
                    k = [k_sp[:, r, bass.ds(Q * g, Q), :].rearrange("p b h -> p (b h)").unsqueeze(2)
                         .to_broadcast([T, Q * NH5, D5]) for r in range(2)]
                    for r, (y, src) in enumerate(((y_even, v_cas), (y_odd, v_sac))):
                        dve.tensor_tensor(y[:, par, :, :].rearrange("p i (h d) -> p (i h) d", d=D5),
                                          src[:, bass.ds(Q * g, Q), :].rearrange("p i (h d) -> p (i h) d", d=D5),
                                          k[r], ALU.mult).then_inc(y_part, 1)
                    dve.wait_ge(y_part, 2 * g + 2)
                    dve.tensor_tensor(y_even[:, par, :, :], y_even[:, par, :, :], y_odd[:, par, :, :], ALU.add)\
                        .then_inc(y_done, 1)

                def finish(b):
                    dve.wait_ge(out_done, b + 1)
                    dve.tensor_tensor(core.x[:, b, :], core.bank[2 + b % 2][:, 0:D], core.x[:, b, :], ALU.add)\
                        .then_inc(x_done, 1)
                    dve.wait_ge(x_done, b + 1)
                    dve.bn_stats(core.stats[:, b, :], core.x[:, b, :]).then_inc(s_var, 1)

                dve.wait_ge(k_spec_copied, 2)
                dve.wait_ge(biased, B)
                convolve(0, 0)
                for g in range(groups):
                    if g + 1 < groups:
                        if g >= 1:
                            dve.wait_ge(o_done, Q * g)
                        convolve(g + 1, (g + 1) % 2)
                    for i in range(Q):
                        finish(Q * g + i)
                dve.wait_ge(s_var, 6 + B)

            @block.gpsimd
            def _(pool):
                norm_pool(core, pool, s_var, s_rstd)
                for g in range(groups):
                    par = g % 2
                    pool.wait_ge(spectra, 5 * g + 2)
                    if g >= 2:
                        pool.wait_ge(summed, g - 1)
                    pool.tensor_tensor(even[:, par, :, :], q_cas[:, :, :], k_even[:, :, :], ALU.mult)\
                        .then_inc(even_done, 1)
                    pool.wait_ge(odd_done, g + 1)
                    pool.wait_ge(even_done, g + 2)
                    pool.tensor_tensor(even[:, par, :, :], even[:, par, :, :], odd[:, par, :, :], ALU.subtract)\
                        .then_inc(diff_done, 1)
                pool.wait_ge(normed, B)
                pool.wait_ge(loaded, 16 * (7 + 3 * Q))
                with pool.Fori(0, B) as b:
                    pool.tensor_tensor(core.x[:, b, :], core.x[:, b, :], out_bias[:, :], ALU.add).then_inc(biased, 1)

            @block.scalar
            def _(act):
                for b in range(B):
                    act.wait_ge(q_turned, b + 1)
                    if b >= 2:
                        act.wait_ge(projected, b - 1)
                    act.activation(zq[:, b % 2, :, :], bank_zq[:, 0:2 * T].rearrange("p (k t) -> p k t", k=2),
                                   ACT.Copy).then_inc(zq_copied, 1)
                    act.wait_ge(c_turned, b + 1)
                    act.activation(zc[:, b % 2, :, :], bank_zc[:, :].rearrange("p (k t) -> p k t", k=4),
                                   ACT.Copy).then_inc(zc_copied, 1)
                for i in range(HALVES):
                    act.wait_ge(corr_done, i + 1)
                    act.activation(corr[:, i, :], core.bank[i][:, 0:T], ACT.Copy, scale=1.0 / D5)\
                        .then_inc(corr_copied, 1)
                act.wait_ge(coded, 1)
                act.activation(w[:, :, :], w[:, :, :], ACT.Exp).then_inc(w_exp, 1)
                act.wait_ge(k_turned, 1)
                act.activation(kern_t[:, :], core.bank[4][:, 0:BH], ACT.Copy).then_inc(k_copied, 1)
                for r in range(2):
                    act.wait_ge(k_spec, r + 1)
                    act.activation(k_sp[:, r, :, :], core.bank[5 + r][:, 0:BH].rearrange("p (b h) -> p b h", b=B),
                                   ACT.Copy).then_inc(k_spec_copied, 1)
                for b in range(B):
                    act.wait_ge(o_done, b + 1)
                    if b >= 2:
                        act.wait_ge(out_done, b - 1)
                    act.activation(oT[:, b % 2, :], core.bank[b % 2][:, 0:T], ACT.Copy).then_inc(o_copied, 1)

            @block.tensor
            def _(pe):
                def transform(b):
                    g, i = b // Q, b % Q
                    if b >= 1:
                        pe.wait_ge(zq_copied, b)
                    pe.wait_ge(normed, b + 1)
                    pe.matmul(bank_zq[:, 0:2 * T], n[:, g % 2, i, :],
                              dft[:, CAS:SAC + 1, :].rearrange("p k t -> p (k t)"), start=True, stop=True)\
                        .then_inc(q_turned, 1)
                    if b >= 1:
                        pe.wait_ge(zc_copied, b)
                    pe.wait_ge(ctx_loaded[g % 2], 16 * (g // 2 + 1))
                    pe.matmul(bank_zc[:, :], cx[:, g % 2, i, :], dft[:, :, :].rearrange("p k t -> p (k t)"),
                              start=True, stop=True).then_inc(c_turned, 1)

                def project(b):
                    g, i = b // Q, b % Q
                    if i == 0 and g >= 1:
                        pe.wait_ge(spectra, 5 * g)
                        pe.wait_ge(odd_done, g)
                    cols = slice(i * D, (i + 1) * D)
                    pe.wait_ge(zq_copied, b + 1)
                    pe.matmul(bank_qc[:, cols], zq[:, b % 2, 0, :], wq[:, :], start=True, stop=True)
                    pe.matmul(bank_qs[:, cols], zq[:, b % 2, 1, :], wq[:, :], start=True, stop=True)
                    pe.wait_ge(zc_copied, b + 1)
                    for bank, k, wgt in ((bank_ke, COS, wk), (bank_ko, SIN, wk), (bank_vc, CAS, wv),
                                         (bank_vs, SAC, wv)):
                        mm = pe.matmul(bank[:, cols], zc[:, b % 2, k, :], wgt[:, :], start=True, stop=True)
                    mm.then_inc(projected, 1)

                pe.wait_ge(loaded, 16 * (7 + 3 * Q))
                transform(0)
                for b in range(B):
                    if b + 1 < B:
                        transform(b + 1)
                    project(b)
                pe.wait_ge(scaled, 4)
                for i in range(HALVES):
                    seqs = B // HALVES
                    pe.wait_ge(summed, groups // HALVES * (i + 1))
                    pe.matmul(core.bank[i][:, 0:T],
                              spec[:, seqs * i:seqs * (i + 1), :].rearrange("p b h -> p (b h)"), inv[:, :],
                              start=True, stop=True).then_inc(corr_done, 1)
                pe.wait_ge(kernels, HALVES * TOP + 2)
                for i in range(HALVES):
                    mm = pe.transpose(core.bank[4][:, i * 128:(i + 1) * 128], pick[:, i, 0, :], core.ident[:, :])
                mm.then_inc(k_turned, 1)
                pe.wait_ge(k_copied, 1)
                for r, k in enumerate((COS, SIN)):
                    pe.matmul(core.bank[5 + r][:, 0:BH], dft[:, k, :], kern_t[:, :], start=True, stop=True)\
                        .then_inc(k_spec, 1)

                def inverse(b):
                    g, i = b // Q, b % Q
                    if i == 0:
                        pe.wait_ge(y_done, g + 1)
                    if b >= 2:
                        pe.wait_ge(o_copied, b - 1)
                    pe.matmul(core.bank[b % 2][:, 0:T], y_even[:, g % 2, i, :], inv[:, :], start=True, stop=True)\
                        .then_inc(o_done, 1)

                def out(b):
                    pe.wait_ge(o_copied, b + 1)
                    if b >= 2:
                        pe.wait_ge(x_done, b - 1)
                    pe.matmul(core.bank[2 + b % 2][:, 0:D], oT[:, b % 2, :], wo[:, :], start=True, stop=True)\
                        .then_inc(out_done, 1)

                inverse(0)
                for b in range(B):
                    if b + 1 < B:
                        inverse(b + 1)
                    out(b)


E6 = 8
H6 = 512
CH6 = H6 // 128
CAP = -(-12 * B * T // (10 * E6))
SLOTS = E6 * CAP
ROWS = [min(128, CAP - r) for r in range(0, CAP, 128)]
BITS = 30


def experts(core, a):
    nc = core.nc
    groups = B // Q
    x_slots = nc.dram_tensor("mo_x_slots", (SLOTS, D), FP32, kind="Internal").ap()
    y_slots = nc.dram_tensor("mo_y_slots", (SLOTS + 1, D), FP32, kind="Internal").ap()
    with ExitStack() as ctx:
        def sb(name, shape, dt=FP32):
            return ctx.enter_context(nc.sbuf_tensor(name, shape, dt))

        n_all = sb("mo_n_all", [T, B, D])
        gate = [sb(f"mo_gate{k}", [T, B]) for k in range(2)]
        slot = [sb(f"mo_slot{k}", [T, B], U32) for k in range(2)]
        y_got = [sb(f"mo_y_got{k}", [T, B, D]) for k in range(2)]
        zeros = sb("mo_zeros", [128, CAP])
        b1 = sb("mo_b1", [128, E6, CH6])
        b2 = sb("mo_b2", [128, E6, D])
        cleared = core.sem("mo_cleared")
        with ExitStack() as part:
            route(core, a, part, n_all, gate, slot, x_slots, y_slots, zeros, b1, b2, cleared)
        expert_loop(core, a, n_all, gate, slot, y_got, x_slots, y_slots, b1, b2)


def route(core, a, ctx, n_all, gate, slot, x_slots, y_slots, zeros, b1, b2, cleared):
    nc = core.nc
    groups = B // Q

    def sb(name, shape, dt=FP32):
        return ctx.enter_context(nc.sbuf_tensor(name, shape, dt))

    wr, br = sb("ro_wr", [D, E6]), sb("ro_br", [T, E6])
    iota = sb("ro_iota", [T, E6])
    base = sb("ro_base", [T, E6])
    bit_f, bit_i = sb("ro_bit_f", [T, BITS]), sb("ro_bit_i", [T, BITS, E6], I32)
    lower = sb("ro_lower", [T, T])
    first = sb("ro_first", [T, E6 * B])
    n4, nT = sb("ro_n4", [T, Q, D]), sb("ro_nT", [D, Q * T])
    p, tmp, tmp2 = sb("ro_p", [T, B, E6]), sb("ro_tmp", [T, B, E6]), sb("ro_tmp2", [T, B, E6])
    pick = [sb(f"ro_pick{k}", [T, B, E6]) for k in range(2)]
    v = sb("ro_v", [T, B, E6])
    red = sb("ro_red", [T, B])
    keep, equal = sb("ro_keep", [T, B, E6]), sb("ro_equal", [T, B, E6])
    count = sb("ro_count", [T, E6])
    thr, cand, won = (sb(f"ro_{w}", [T, E6], I32) for w in ("thr", "cand", "won"))
    need = sb("ro_need", [T, E6])
    total, before = sb("ro_total", [T, E6 * B]), sb("ro_before", [T, E6 * B])
    (loaded, made, s_var, s_rstd, normed, turned, n_copied, n_kept, logits, biased, s, expd, counted, compared,
     prefix, won_done) = core.sems(
        "ro", "loaded made var rstd normed turned n_copied n_kept logits biased step expd counted compared prefix won_done")
    bank_n, bank_l, bank_c, bank_p, bank_t = core.bank[0:5]

    def per_token(ap):
        return ap.unsqueeze(2).to_broadcast([T, B, E6])

    def per_expert(ap):
        return ap.unsqueeze(1).to_broadcast([T, B, E6])

    def expert_major(ap):
        return ap.rearrange("t b e -> t e b")

    def by_expert(ap):
        return ap.rearrange("t (e b) -> t b e", e=E6)

    with nc.Block() as block:
        @block.sync
        def _(sp):
            for dst, src in ((wr, a["L1_ffn_Wr"]), (br, a["L1_ffn_br"].partition_broadcast(T)),
                             (iota, a["c_expert"].partition_broadcast(T)),
                             (base, a["c_expert_base"].partition_broadcast(T)),
                             (bit_f, a["c_bit_f"].partition_broadcast(T)), (lower, a["c_lower"]),
                             (first, a["c_first"].partition_broadcast(T))):
                sp.dma_start(dst[:, :], src).then_inc(loaded, 16)
            sp.dma_start(bit_i[:, :, :].rearrange("t i e -> t (i e)"), a["c_bit_i"].partition_broadcast(T))\
                .then_inc(loaded, 16)
            sp.dma_start(b1[:, :, :], a["moe_b1_col"].rearrange("p (e c) -> p e c", e=E6)).then_inc(loaded, 16)
            sp.dma_start(b2[:, :, :].rearrange("p e d -> p (e d)"),
                         a["L1_ffn_b2"].rearrange("e d -> (e d)").partition_broadcast(T)).then_inc(loaded, 16)
            sp.wait_ge(made, 1)
            sp.dma_start(x_slots.rearrange("s d -> (s d)").rearrange("(p e n) -> p e n", p=128, e=E6),
                         over(zeros[:, :], E6)).then_inc(cleared, 16)
            sp.dma_start(y_slots[SLOTS:SLOTS + 1, :], zeros[0:1, 0:D]).then_inc(cleared, 16)
            sp.wait_ge(loaded, 16 * 10)
            sp.wait_ge(cleared, 32)

        @block.gpsimd
        def _(pool):
            pool.memset(zeros[:, :], 0.0).then_inc(made, 1)
            norm_pool(core, pool, s_var, s_rstd)

        @block.scalar
        def _(act):
            with act.Fori(0, groups) as g:
                act.wait_ge(normed, Q * (g + 1))
                act.activation(n_all[:, bass.ds(Q * g, Q), :], n4[:, :, :], ACT.Copy).then_inc(n_kept, 1)
                act.wait_ge(turned, g + 1)
                act.activation(nT[:, :], bank_n[:, :], ACT.Copy).then_inc(n_copied, 1)
            act.wait_ge(s, 2)
            act.activation(p[:, :, :], p[:, :, :], ACT.Exp).then_inc(expd, 1)

        @block.tensor
        def _(pe):
            pe.wait_ge(loaded, 160)
            with pe.Fori(0, groups) as g:
                pe.wait_ge(normed, Q * (g + 1))
                for i in range(Q):
                    mm = pe.transpose(bank_n[:, i * T:(i + 1) * T], n4[:, i, :], core.ident[:, :])
                mm.then_inc(turned, 1)
                pe.wait_ge(n_copied, g + 1)
                for i in range(Q):
                    mm = pe.matmul(bank_l[:, i * E6:(i + 1) * E6], nT[:, i * T:(i + 1) * T], wr[:, :],
                                   start=True, stop=True)
                mm.then_inc(logits, 1)
            with pe.Fori(0, BITS + 1) as i:
                pe.wait_ge(counted, i + 1)
                pe.matmul(bank_c[:, 0:E6], core.ones[:, :], count[:, :], start=True, stop=True).then_inc(compared, 1)
            for k, flags in enumerate((equal, keep)):
                pe.wait_ge(counted, BITS + 2 + k)
                rhs = expert_major(flags[:, :, :])
                pe.matmul(bank_p[:, 0:E6 * B].rearrange("t (e b) -> t e b", e=E6), lower[:, :], rhs,
                          start=True, stop=True)
                pe.matmul(bank_t[:, 0:E6 * B].rearrange("t (e b) -> t e b", e=E6), core.ones[:, :], rhs,
                          start=True, stop=True).then_inc(prefix, 1)

        @block.vector
        def _(dve):
            steps = 0

            def done(ins):
                nonlocal steps
                steps += 1
                ins.then_inc(s, 1)
                dve.wait_ge(s, steps)

            norm_dve(core, dve, s_var)
            dve.wait_ge(s_rstd, 2)

            def prepare(g):
                for i in range(Q):
                    normalise(core, dve, n4[:, i, :], Q * g + i).then_inc(normed, 1)

            def add_bias(g):
                dve.wait_ge(logits, g + 1)
                dve.tensor_tensor(p[:, bass.ds(Q * g, Q), :], bank_l[:, 0:Q * E6].rearrange("t (i e) -> t i e", i=Q),
                                  over(br[:, :], Q), ALU.add).then_inc(biased, 1)

            dve.wait_ge(loaded, 160)
            prepare(0)
            with dve.Fori(0, groups - 1) as g:
                add_bias(g)
                dve.wait_ge(n_kept, g + 1)
                prepare(g + 1)
            add_bias(groups - 1)
            dve.wait_ge(biased, groups)

            done(dve.tensor_reduce(red[:, :], p[:, :, :], AX.X, ALU.max))
            done(dve.tensor_tensor(p[:, :, :], p[:, :, :], per_token(red[:, :]), ALU.subtract))
            dve.wait_ge(expd, 1)
            done(dve.tensor_reduce(red[:, :], p[:, :, :], AX.X, ALU.add))
            done(dve.reciprocal(red[:, :], red[:, :]))
            done(dve.tensor_tensor(p[:, :, :], p[:, :, :], per_token(red[:, :]), ALU.mult))

            for k in range(2):
                q = (p, tmp2)[k]
                done(dve.tensor_reduce(gate[k][:, :], q[:, :, :], AX.X, ALU.max))
                done(dve.tensor_tensor(tmp[:, :, :], q[:, :, :], per_token(gate[k][:, :]), ALU.is_equal))
                done(dve.tensor_tensor(tmp[:, :, :], tmp[:, :, :], per_expert(iota[:, :]), ALU.mult))
                done(dve.tensor_reduce(red[:, :], tmp[:, :, :], AX.X, ALU.min))
                done(dve.tensor_tensor(pick[k][:, :, :], per_expert(iota[:, :]), per_token(red[:, :]), ALU.is_equal))
                if k == 0:
                    done(dve.scalar_tensor_tensor(out=tmp2[:, :, :].rearrange("t b e -> t (b e)"),
                                                  in0=pick[0][:, :, :].rearrange("t b e -> t (b e)"), scalar=-4.0,
                                                  in1=p[:, :, :].rearrange("t b e -> t (b e)"),
                                                  op0=ALU.mult, op1=ALU.add))
            done(dve.tensor_tensor(tmp[:, :, :], pick[0][:, :, :], pick[1][:, :, :], ALU.add))
            done(dve.tensor_tensor(v[:, :, :], tmp[:, :, :], p[:, :, :], ALU.mult))
            done(dve.memset(thr[:, :], 0))

            with dve.Fori(0, BITS) as i:
                c = steps + 3 * i
                dve.tensor_tensor(cand[:, :], thr[:, :], bit_i[:, i, :], ALU.bitwise_or).then_inc(s, 1)
                dve.wait_ge(s, c + 1)
                dve.tensor_tensor(tmp[:, :, :], v[:, :, :], per_expert(cand[:, :].bitcast(FP32)), ALU.is_ge)\
                    .then_inc(s, 1)
                dve.wait_ge(s, c + 2)
                dve.tensor_reduce(count[:, :], expert_major(tmp[:, :, :]), AX.X, ALU.add).then_inc(counted, 1)
                dve.wait_ge(compared, i + 1)
                dve.tensor_scalar(won[:, :], bank_c[:, 0:E6], CAP - 0.5, bit_f[:, bass.ds(i, 1)], ALU.is_ge, ALU.mult)\
                    .then_inc(won_done, 1)
                dve.wait_ge(won_done, i + 1)
                dve.tensor_tensor(thr[:, :], thr[:, :], won[:, :], ALU.bitwise_or).then_inc(s, 1)
                dve.wait_ge(s, c + 3)
            steps += 3 * BITS
            level = per_expert(thr[:, :].bitcast(FP32))
            done(dve.tensor_tensor(keep[:, :, :], v[:, :, :], level, ALU.is_gt))
            done(dve.tensor_tensor(equal[:, :, :], v[:, :, :], level, ALU.is_equal))
            dve.tensor_reduce(count[:, :], expert_major(keep[:, :, :]), AX.X, ALU.add).then_inc(counted, 1)
            done(dve.tensor_scalar(tmp[:, :, :], v[:, :, :], 0.0, None, ALU.is_gt))
            dve.tensor_tensor(equal[:, :, :], equal[:, :, :], tmp[:, :, :], ALU.mult).then_inc(counted, 1)
            dve.wait_ge(compared, BITS + 1)
            done(dve.tensor_scalar(need[:, :], bank_c[:, 0:E6], -1.0, float(CAP), ALU.mult, ALU.add))

            def number(k):
                dve.wait_ge(prefix, k + 1)
                done(dve.tensor_copy(total[:, :], bank_t[:, 0:E6 * B]))
                done(dve.tensor_tensor_scan(before[:, :], first[:, :], total[:, :], 0.0, ALU.mult, ALU.add))
                done(dve.tensor_tensor(before[:, :], before[:, :], total[:, :], ALU.subtract))
                done(dve.tensor_tensor(tmp[:, :, :], by_expert(bank_p[:, 0:E6 * B]), by_expert(before[:, :]),
                                       ALU.add))

            number(0)
            done(dve.tensor_tensor(tmp[:, :, :], tmp[:, :, :], per_expert(need[:, :]), ALU.is_lt))
            done(dve.tensor_tensor(tmp[:, :, :], tmp[:, :, :], equal[:, :, :], ALU.mult))
            dve.tensor_tensor(keep[:, :, :], keep[:, :, :], tmp[:, :, :], ALU.add).then_inc(counted, 1)
            number(1)
            done(dve.tensor_tensor(tmp[:, :, :], tmp[:, :, :], per_expert(base[:, :]), ALU.add))
            done(dve.tensor_tensor(tmp[:, :, :], tmp[:, :, :], keep[:, :, :], ALU.mult))
            for k in range(2):
                done(dve.tensor_tensor(tmp2[:, :, :], tmp[:, :, :], pick[k][:, :, :], ALU.mult))
                done(dve.tensor_reduce(red[:, :], tmp2[:, :, :], AX.X, ALU.add))
                done(dve.tensor_scalar(slot[k][:, :], red[:, :], float(SLOTS), None, ALU.add))


def expert_loop(core, a, n_all, gate, slot, y_got, x_slots, y_slots, b1, b2):
    nc = core.nc
    (sent, w_in0, w_in1, x_in0, x_in1, turned, x_copied, up_done, silu_done, down_done, y_added, stored0, stored1,
     fetched, x_done) = core.sems(
        "mo", "sent w_in0 w_in1 x_in0 x_in1 turned x_copied up_done silu_done down_done y_added stored0 stored1 fetched "
        "x_done")
    w_in, x_in, stored = (w_in0, w_in1), (x_in0, x_in1), (stored0, stored1)
    bank_x, bank_up, bank_y = core.bank[0], core.bank[1:3], core.bank[3:6]
    full = len(ROWS) - 1
    at = [128 * r for r in range(len(ROWS))]
    with ExitStack() as ctx:
        def sb(name, shape):
            return ctx.enter_context(nc.sbuf_tensor(name, shape, FP32))

        w1, w2 = sb("mo_w1", [D, 2, H6]), sb("mo_w2", [128, 2, CH6, D])
        rows = sb("mo_rows", [128, 2, len(ROWS), D])
        xT = sb("mo_xT", [D, CAP])
        h = sb("mo_h", [128, CH6, CAP])
        y = sb("mo_y", [128, 2, len(ROWS), D])
        with nc.Block() as block:
            @block.sync
            def _(sp):
                def load_weights(e, par):
                    sp.dma_start(w1[:, par, :], a["L1_ffn_W1"][bass.ds(e, 1)].rearrange("e d h -> (e d) h"))\
                        .then_inc(w_in[par], 16)
                    sp.dma_start(w2[:, par, :, :], a["L1_ffn_W2"][bass.ds(e, 1)]
                                 .rearrange("e (c p) d -> p (e c) d", p=128)).then_inc(w_in[par], 16)

                def load_rows(e, par):
                    sp.dma_start(rows[:, par, 0:full, :], x_slots[bass.ds(e * CAP, 128 * full), :]
                                 .rearrange("(r p) d -> p r d", p=128)).then_inc(x_in[par], 16)
                    sp.dma_start(rows[0:ROWS[-1], par, full, :],
                                 x_slots[bass.ds(e * CAP + 128 * full, ROWS[-1]), :]).then_inc(x_in[par], 16)

                load_weights(0, 0)
                load_weights(1, 1)
                sp.wait_ge(sent, 16 * 2 * B)
                load_rows(0, 0)
                load_rows(1, 1)
                with sp.Fori(1, E6 // 2) as i:
                    for par in range(2):
                        e = 2 * i + par
                        sp.wait_ge(turned, e - 1)
                        load_rows(e, par)
                        sp.wait_ge(down_done, e - 1)
                        load_weights(e, par)

            @block.gpsimd
            def _(pool):
                for b in range(B):
                    for k in range(2):
                        pool.indirect_dma_start(
                            out=x_slots, out_offset=bass.IndirectOffsetOnAxis(ap=slot[k][:, b:b + 1], axis=0),
                            in_=n_all[:, b, :], in_offset=None, bounds_check=SLOTS - 1, oob_is_err=False)\
                            .then_inc(sent, 16)

                with pool.Fori(0, E6 // 2) as i:
                    for par in range(2):
                        e = 2 * i + par
                        pool.wait_ge(y_added, e + 1)
                        pool.dma_start(y_slots[bass.ds(e * CAP, 128 * full), :].rearrange("(r p) d -> p r d", p=128),
                                       y[:, par, 0:full, :]).then_inc(stored[par], 16)
                        pool.dma_start(y_slots[bass.ds(e * CAP + 128 * full, ROWS[-1]), :],
                                       y[0:ROWS[-1], par, full, :]).then_inc(stored[par], 16)
                for par in range(2):
                    pool.wait_ge(stored[par], 16 * E6)
                for b in range(B):
                    for k in range(2):
                        pool.indirect_dma_start(
                            out=y_got[k][:, b, :], out_offset=None, in_=y_slots,
                            in_offset=bass.IndirectOffsetOnAxis(ap=slot[k][:, b:b + 1], axis=0))\
                            .then_inc(fetched, 16)

            @block.tensor
            def _(pe):
                def turn(e, par):
                    pe.wait_ge(x_in[par], 16 * (e + 2 - par))
                    for r, m in enumerate(ROWS):
                        mm = pe.transpose(bank_x[:, at[r]:at[r] + m], rows[0:m, par, r, :], core.ident[0:m, 0:m])
                    mm.then_inc(turned, 1)

                def up(e, par, c):
                    if c == 0:
                        pe.wait_ge(x_copied, e + 1)
                        pe.wait_ge(w_in[par], 16 * (e + 2 - par))
                    if c >= 2:
                        pe.wait_ge(silu_done, CH6 * e + c - 1)
                    pe.matmul(bank_up[c % 2][:, 0:CAP], w1[:, par, c * 128:(c + 1) * 128], xT[:, :],
                              start=True, stop=True).then_inc(up_done, 1)

                def down(e, par, c, first=False):
                    pe.wait_ge(silu_done, CH6 * e + c + 1)
                    if c == 0 and not first:
                        pe.wait_ge(y_added, e)
                    for r, m in enumerate(ROWS):
                        mm = pe.matmul(bank_y[r][0:m, 0:D], h[:, c, at[r]:at[r] + m], w2[:, par, c, :],
                                       start=(c == 0), stop=(c == CH6 - 1))
                    if c == CH6 - 1:
                        mm.then_inc(down_done, 1)

                def step(e, par, first=False, last=False):
                    up(e, par, 0)
                    up(e, par, 1)
                    down(e, par, 0, first)
                    up(e, par, 2)
                    down(e, par, 1)
                    up(e, par, 3)
                    down(e, par, 2)
                    if not last:
                        turn(e + 1, 1 - par)
                    down(e, par, 3)

                turn(0, 0)
                step(0, 0, first=True)
                with pe.Fori(0, E6 // 2 - 1) as i:
                    step(2 * i + 1, 1)
                    step(2 * i + 2, 0)
                step(E6 - 1, 1, last=True)

            @block.scalar
            def _(act):
                with act.Fori(0, E6) as e:
                    for c in range(CH6):
                        act.wait_ge(up_done, CH6 * e + c + 1)
                        act.activation(h[:, c, :], bank_up[c % 2][:, 0:CAP], ACT.Silu,
                                       bias=b1[:, e, c:c + 1]).then_inc(silu_done, 1)

            @block.vector
            def _(dve):
                def copy_x(e):
                    dve.wait_ge(turned, e + 1)
                    dve.tensor_copy(xT[:, :], bank_x[:, 0:CAP]).then_inc(x_copied, 1)

                def add_bias(e, par, first=False):
                    dve.wait_ge(down_done, e + 1)
                    if not first:
                        dve.wait_ge(stored[par], 16 * (e - par))
                    for r, m in enumerate(ROWS):
                        ins = dve.tensor_tensor(y[0:m, par, r, :], bank_y[r][0:m, 0:D], b2[0:m, e, :], ALU.add)
                    ins.then_inc(y_added, 1)

                copy_x(0)
                copy_x(1)
                add_bias(0, 0, first=True)
                copy_x(2)
                add_bias(1, 1, first=True)
                with dve.Fori(1, E6 // 2 - 1) as i:
                    copy_x(2 * i + 1)
                    add_bias(2 * i, 0)
                    copy_x(2 * i + 2)
                    add_bias(2 * i + 1, 1)
                copy_x(E6 - 1)
                add_bias(E6 - 2, 0)
                add_bias(E6 - 1, 1)
                dve.wait_ge(fetched, 16 * 2 * B)
                with dve.Fori(0, B) as b:
                    for k in range(2):
                        dve.scalar_tensor_tensor(out=core.x[:, b, :], in0=y_got[k][:, b, :],
                                                 scalar=gate[k][:, bass.ds(b, 1)], in1=core.x[:, b, :],
                                                 op0=ALU.mult, op1=ALU.add).then_inc(x_done, 1)
                        dve.wait_ge(x_done, 2 * b + k + 1)


def store(core, out):
    stored = core.sem("stored")
    with core.nc.Block() as block:
        @block.sync
        def _(sp):
            for h in range(4):
                sp.dma_start(out[4 * h:4 * h + 4].rearrange("b t d -> t b d"),
                             core.x[:, 4 * h:4 * h + 4, :]).then_inc(stored, 16)
            sp.wait_ge(stored, 64)


def decoder(nc, a, out):
    with ExitStack() as ctx:
        core = Core(nc, ctx)
        setup(core, a)
        with ExitStack() as part:
            m = AttnMem(core)
            attn_setup(core, m, a)
            softmax_attention(core, m, 0)
            softmax_attention(core, m, 1)
        core.free_semaphores()
        f = FoldMem(core)
        fold_butterflies(core, f, a)
        feed_forward(core, f)
        m = LinMem(core)
        linear_setup(core, m, a)
        linear_attention(core, m)
        autocorrelation(core, a)
        experts(core, a)
        store(core, out)


def _constants():
    p = np.arange(128)
    c = {"c_ident": np.eye(128, dtype=np.float32)}
    for name, pick in (("c_mask_j", p // DH % J), ("c_mask_g", p // (DH * J))):
        c[name] = np.repeat(pick[:, None] == np.arange(J), T, axis=1).astype(np.float32)
    gap = p[None, :] - p[:, None]
    c["c_gap"] = np.maximum(gap, 0).astype(np.float32)
    c["c_tri"] = (gap >= 0).astype(np.float32)
    angle = 2 * np.pi * (p[:, None] * p[None, :] % T) / T
    cos, sin = np.cos(angle), np.sin(angle)
    c["c_dft"] = np.concatenate([cos, sin, cos + sin, cos - sin], axis=1).astype(np.float32)
    c["c_iota"] = np.tile(p.astype(np.float32), (128, 1))
    c["c_expert"] = (np.arange(E6) - E6).astype(np.float32)
    c["c_expert_base"] = (np.arange(E6) * CAP - SLOTS).astype(np.float32)
    bit = 2 ** np.arange(BITS - 1, -1, -1)
    c["c_bit_f"] = bit.astype(np.float32)
    c["c_bit_i"] = np.repeat(bit, E6).astype(np.int32)
    c["c_lower"] = (gap > 0).astype(np.float32)
    c["c_first"] = np.tile(np.arange(B) > 0, E6).astype(np.float32)
    return c


def kernel(**inputs):
    import concourse.bacc as _bacc
    from concourse.bass_utils import run_bass_kernel_spmd as _run

    arrays = {k: np.ascontiguousarray(v) for k, v in inputs.items() if k != "L0_attn_mask"}
    arrays["ctxT"] = np.ascontiguousarray(inputs["ctx_1024"].transpose(0, 2, 1))
    arrays["L0_xattn_w_outT"] = np.ascontiguousarray(inputs["L0_xattn_w_out"].T)
    for name, w in (("up_planes", "L0_ffn_up_weights"), ("down_planes", "L0_ffn_down_weights")):
        w = inputs[w].transpose(0, 2, 3, 1)
        arrays[name] = np.ascontiguousarray(w.reshape(w.shape[0], -1))
    arrays["W_conT"] = np.ascontiguousarray(inputs["L0_ffn_W_con"].T)
    arrays["up_bias_col"] = np.ascontiguousarray(inputs["L0_ffn_up_bias"].reshape(CH, 128).T)
    for name, w in (("lin_WqT", "L1_attn_W_Q"), ("lin_WkT", "L1_attn_W_K"), ("lin_WvT", "L1_attn_W_V"),
                    ("lin_WgT", "L1_attn_W_g_w"), ("lin_WoT", "L1_attn_W_O")):
        arrays[name] = np.ascontiguousarray(inputs[w].T)
    for name, w in (("auto_WqT", "L1_xattn_Wq"), ("auto_WkT", "L1_xattn_Wk"), ("auto_WvT", "L1_xattn_Wv"),
                    ("auto_WoT", "L1_xattn_Wo")):
        arrays[name] = np.ascontiguousarray(inputs[w].T)
    arrays["moe_b1_col"] = np.ascontiguousarray(
        inputs["L1_ffn_b1"].reshape(E6, CH6, 128).transpose(2, 0, 1).reshape(128, E6 * CH6))
    arrays["gate_bias_col"] = np.ascontiguousarray(inputs["L1_attn_W_g_b"].reshape(C4, 128).T)
    arrays.update(_constants())
    nc = _bacc.Bacc("TRN2", target_bir_lowering=False, num_devices=1)
    args = {k: nc.dram_tensor("in_" + k, v.shape, mybir.dt.from_np(v.dtype), kind="ExternalInput").ap()
            for k, v in arrays.items()}
    out = nc.dram_tensor("out_0", (B, T, D), FP32, kind="ExternalOutput").ap()
    decoder(nc, args, out)
    r = _run(nc, [{"in_" + k: v for k, v in arrays.items()}], core_ids=[0])
    return r.results[0]["out_0"]
```

```python
import numpy as np
from contextlib import ExitStack

import concourse.bass as bass
from concourse import mybir

FP32 = mybir.dt.float32
BF16 = mybir.dt.bfloat16
I32 = mybir.dt.int32
U32 = mybir.dt.uint32
ALU = mybir.AluOpType
ACT = mybir.ActivationFunctionType
AX = mybir.AxisListType

B = 16
T = 128
D = 128
EPS = 1e-5
G, J = 4, 4
DH = D // (G * J)


class Core:

    def __init__(self, nc, ctx):
        self.nc, self.ctx = nc, ctx
        self.x = self.sb("x", [T, B, D])
        self.stats = self.sb("stats", [T, B, 6])
        self.mean = self.sb("mean", [T, B, 1])
        self.rstd = self.sb("rstd", [T, B, 1])
        self.dev = self.sb("dev", [T, B])
        self.var = self.sb("var", [T, B])
        self.eps = self.sb("eps", [T, B])
        self.neg_half = self.sb("neg_half", [T, B])
        self.ident = self.sb("ident", [128, 128])
        self.ident_b = self.sb("ident_b", [128, 128], BF16)
        self.ones = self.sb("ones", [128, 128])
        self.bank = [ctx.enter_context(nc.psum_tensor(f"bank{i}", [128, 512], FP32)) for i in range(8)]
        self.layer_sems = []

    def sb(self, name, shape, dt=FP32):
        return self.ctx.enter_context(self.nc.sbuf_tensor(name, shape, dt))

    def sem(self, name):
        self.layer_sems.append(self.nc.alloc_semaphore(name))
        return self.layer_sems[-1]

    def sems(self, layer, names):
        return [self.sem(f"{layer}_{n}") for n in names.split()]

    def keep_sem(self, name):
        return self.nc.alloc_semaphore(name)

    def free_semaphores(self):
        self.nc.clear_and_free_semaphores(self.layer_sems)
        self.layer_sems = []
        self.nc.all_engine_barrier()


def over(ap, n):
    p, m = ap.shape
    return ap.unsqueeze(1).to_broadcast([p, n, m])


def setup(core, m, f, lin, a):
    nc = core.nc
    x_in, loaded, decay_in, made, zeroed, stat, decay_ready, raised = core.sems(
        "setup", "x_in loaded decay_in made zeroed stat decay_ready raised")
    with nc.Block() as block:
        @block.sync
        def _(sp):
            for h in range(4):
                sp.dma_start(core.x[:, 4 * h:4 * h + 4, :],
                             a["x"][4 * h:4 * h + 4].rearrange("b t d -> t b d")).then_inc(x_in, 16)
            for dst, src in ((core.ident, "c_ident"), (m.wq, "L0_attn_Wq"), (m.wk, "L0_attn_Wk"),
                             (m.wv, "L0_attn_Wv"), (m.w_out[0], "L0_attn_Wout")):
                sp.dma_start(dst[:, :], a[src]).then_inc(loaded, 16)
            for dst, src in ((m.mask_j, "c_mask_j"), (m.mask_g, "c_mask_g")):
                sp.dma_start(dst[:, :, :], a[src].rearrange("p (j t) -> p j t", j=J)).then_inc(loaded, 16)
            sp.dma_start(f.up[:, :], a["L0_ffn_W_exp"]).then_inc(f.up_loaded, 16)
            sp.dma_start(f.bias[:, :], a["L0_ffn_b_exp"].unsqueeze(0)).then_inc(f.up_loaded, 16)
            sp.dma_start(f.w_up[:, :, :, :].rearrange("p s o n -> p (s o n)"),
                         a["up_stages"].partition_broadcast(D)).then_inc(f.up_loaded, 16)
            sp.dma_start(m.w_out[1][:, :], a["L0_xattn_w_outT"]).then_inc(m.cross_loaded, 16)
            sp.dma_start(m.bias[:, :], a["L0_xattn_b_out"].partition_broadcast(T)).then_inc(m.cross_loaded, 16)
            sp.dma_start(m.ctx[:, :, :], a["ctx_1024"].rearrange("b t d -> t b d")).then_inc(m.cross_loaded, 16)
            sp.dma_start(m.ctxT[:, :, :], a["ctxT"].rearrange("b d t -> d b t")).then_inc(m.cross_loaded, 16)
            sp.dma_start(f.down_w[:, :], a["W_conT"]).then_inc(f.down_loaded, 16)
            sp.dma_start(f.w_down[:, :, :, :].rearrange("p s o n -> p (s o n)"),
                         a["down_stages"].partition_broadcast(D)).then_inc(f.down_loaded, 16)
            sp.dma_start(f.up_bias[:, :], a["up_bias_col"]).then_inc(f.bias_loaded, 16)
            for i, src in enumerate(("L0_ffn_b_con", "L0_ffn_down_bias")):
                sp.dma_start(f.out_bias[:, i, :], a[src].partition_broadcast(T)).then_inc(f.bias_loaded, 16)
            for dst, src in ((lin.wq, "lin_WqT"), (lin.wk, "lin_WkT"), (lin.wv, "lin_WvT"), (lin.wg, "lin_WgT")):
                sp.dma_start(dst[:, :], a[src]).then_inc(lin.loaded, 16)
            sp.dma_start(lin.wo[:, :, :], a["lin_WoT"].rearrange("(c p) e -> p c e", p=128)).then_inc(lin.loaded, 16)

        @block.gpsimd
        def _(pool):
            pool.memset(core.ones[:, :], 1.0).then_inc(made, 1)
            pool.memset(core.eps[:, :], EPS).then_inc(made, 1)
            pool.memset(core.neg_half[:, :], -0.5).then_inc(made, 1)
            pool.wait_ge(loaded, 112)
            pool.tensor_copy(core.ident_b[:, :], core.ident[:, :]).then_inc(made, 1)
            pool.wait_ge(made, 4)

        @block.scalar
        def _(act):
            for dst, src in ((lin.decay, a["L1_attn_decay_log"].partition_broadcast(T)), (lin.gap, a["c_gap"]),
                             (lin.tri, a["c_tri"]), (lin.gate_bias, a["gate_bias_col"])):
                act.dma_start(dst[:, :], src).then_inc(decay_in, 16)
            act.wait_ge(decay_ready, 1)
            act.activation(lin.decay[:, :], lin.decay[:, :], ACT.Exp, scale=-1.0).then_inc(raised, 1)
            act.wait_ge(raised, 1)
            act.activation(lin.decay[:, :], lin.decay[:, :], ACT.Ln, bias=1.0).then_inc(raised, 1)
            act.wait_ge(decay_ready, 3)
            for h in range(H4):
                act.activation(lin.mask[:, h, :], lin.gap[:, :], ACT.Exp, scale=lin.decay[:, h:h + 1])\
                    .then_inc(raised, 1)

        @block.vector
        def _(dve):
            dve.memset(m.v[:, :, :, :], 0.0).then_inc(zeroed, 1)
            dve.wait_ge(zeroed, 1)
            dve.memset(m.v[:, :, :, DH:DH + 1], 1.0).then_inc(zeroed, 1)
            dve.wait_ge(decay_in, 64)
            dve.tensor_scalar(lin.decay[:, :], lin.decay[:, :], -80.0, None, ALU.max).then_inc(decay_ready, 1)
            dve.tensor_scalar(lin.gate_bias[:, :], lin.gate_bias[:, :], 0.5, None, ALU.mult).then_inc(decay_ready, 1)
            dve.wait_ge(raised, 2)
            dve.tensor_scalar(lin.decay[:, :], lin.decay[:, :], -1.0, None, ALU.mult).then_inc(decay_ready, 1)
            dve.wait_ge(x_in, 64)
            with dve.Fori(0, B) as b:
                dve.bn_stats(core.stats[:, b, :], core.x[:, b, :]).then_inc(stat, 1)
            dve.wait_ge(raised, 2 + H4)
            dve.tensor_tensor(lin.mask[:, :, :], lin.mask[:, :, :], over(lin.tri[:, :], H4), ALU.mult)\
                .then_inc(decay_ready, 1)
            dve.wait_ge(decay_ready, 4)
            dve.wait_ge(stat, B)
            dve.wait_ge(zeroed, 2)


def norm_dve(core, dve, s_var):
    st = core.stats
    dve.tensor_tensor(core.mean[:, :, 0], st[:, :, 1], st[:, :, 4], ALU.add).then_inc(s_var, 1)
    dve.tensor_tensor(core.dev[:, :], st[:, :, 1], st[:, :, 4], ALU.subtract).then_inc(s_var, 1)
    dve.tensor_tensor(core.var[:, :], st[:, :, 2], st[:, :, 5], ALU.add).then_inc(s_var, 1)
    dve.wait_ge(s_var, 3)
    dve.tensor_scalar(core.mean[:, :, 0], core.mean[:, :, 0], 0.5, None, ALU.mult).then_inc(s_var, 1)
    dve.scalar_tensor_tensor(out=core.dev[:, :], in0=core.dev[:, :], scalar=0.25, in1=core.dev[:, :],
                             op0=ALU.mult, op1=ALU.mult).then_inc(s_var, 1)
    dve.wait_ge(s_var, 5)
    dve.scalar_tensor_tensor(out=core.var[:, :], in0=core.var[:, :], scalar=1.0 / D, in1=core.dev[:, :],
                             op0=ALU.mult, op1=ALU.add).then_inc(s_var, 1)


def norm_pool(core, pool, s_var, s_rstd):
    pool.wait_ge(s_var, 6)
    pool.tensor_tensor(core.var[:, :], core.var[:, :], core.eps[:, :], ALU.add).then_inc(s_rstd, 1)
    pool.wait_ge(s_rstd, 1)
    pool.tensor_tensor(core.rstd[:, :, 0], core.var[:, :], core.neg_half[:, :], ALU.pow).then_inc(s_rstd, 1)


def normalise(core, dve, dst, b):
    return dve.tensor_scalar(dst, core.x[:, b, :], core.mean[:, b, :], core.rstd[:, b, :],
                             ALU.subtract, ALU.mult)


class AttnMem:

    def __init__(self, core, part):
        def sb(name, shape, dt=FP32):
            return part.enter_context(core.nc.sbuf_tensor(name, shape, dt))

        self.n = sb("at_n", [T, 2, D])
        self.nT = sb("at_nT", [D, T])
        self.qT = sb("at_qT", [D, T])
        self.kT = sb("at_kT", [D, T])
        self.q_j = sb("at_q_j", [D, 2, J, T])
        self.k_g = sb("at_k_g", [D, 2, G, T])
        self.q_gb = sb("at_q_gb", [D, G, T], BF16)
        self.k_jb = sb("at_k_jb", [D, J, T], BF16)
        self.v = sb("at_v", [T, 2, G * J, 32])
        self.nmax = sb("at_nmax", [T, G * J], BF16)
        self.p = sb("at_p", [T, G, J, T])
        self.o_raw = sb("at_o_raw", [128, G, T])
        self.rden = sb("at_rden", [T, G, J])
        self.o = sb("at_o", [T, G * J, DH])
        self.oT = sb("at_oT", [D, T])
        self.mask_j = sb("at_mask_j", [D, J, T])
        self.mask_g = sb("at_mask_g", [D, G, T])
        self.w_out = [sb(f"at_w_out{i}", [D, D]) for i in range(2)]
        self.wq, self.wk, self.wv = (sb(f"at_{w}", [D, D]) for w in ("wq", "wk", "wv"))
        self.ctx = sb("ctx", [T, B, D])
        self.ctxT = sb("ctxT", [D, B, T])
        self.bias = sb("at_bias", [T, D])
        self.cross_loaded = core.sem("at_cross_loaded")


def softmax_attention(core, m, f, layer):
    nc = core.nc
    cross = layer == 1
    (s_var, s_rstd, normed, n_turned, n_copied, projected, qk_copied, v_copied, masked, k_masked, res_made, scored,
     maxed, shifted, exped, pv_done, raw_copied, raw_turned, rden_done, o_done, o_turned, o_copied, out_done,
     x_done) = core.sems(
        f"at{layer}", "var rstd normed n_turned n_copied projected qk_copied v_copied masked k_masked res_made scored "
        "maxed shifted exped pv_done raw_copied raw_turned rden_done o_done o_turned o_copied out_done x_done")
    bank_st, bank_s = core.bank[0:2], core.bank[2:4]
    bank_p, bank_v, bank_d, bank_z = core.bank[4:8]
    qk_copies = 1 if cross else 2
    scale = float(DH) ** -0.5
    LAST = B - 1
    PAIRS = (B - 2) // 2

    with nc.Block() as block:
        @block.vector
        def _(dve):
            def prepare(b, par, reused=True):
                if reused:
                    dve.wait_ge(res_made, b - 1)
                normalise(core, dve, m.n[:, par, :], b).then_inc(normed, 1)

            def maximum(b, g):
                dve.wait_ge(scored, G * b + g + 1)
                dve.tensor_reduce(m.nmax[:, J * g:J * g + J],
                                  bank_s[g % 2][:, :].rearrange("p (j t) -> p j t", j=J),
                                  AX.X, ALU.max, negate=True).then_inc(maxed, 1)

            def divide(b):
                raw = bank_d[:, :].rearrange("p (h w) -> p h w", w=32)
                dve.wait_ge(raw_turned, b + 1)
                dve.reciprocal(m.rden[:, :, :], raw[:, :, DH].rearrange("p (g j) -> p g j", g=G))\
                    .then_inc(rden_done, 1)
                dve.wait_ge(rden_done, b + 1)
                dve.tensor_tensor(m.o[:, :, :], raw[:, :, 0:DH],
                                  m.rden[:, :, :].rearrange("p g j -> p (g j)").unsqueeze(2)
                                  .to_broadcast([T, G * J, DH]), ALU.mult).then_inc(o_done, 1)

            def finish(b):
                dve.wait_ge(out_done, b + 1)
                dve.wait_ge(res_made, b + 1)
                dve.tensor_tensor(core.x[:, b, :], bank_z[:, 0:D], core.x[:, b, :], ALU.add)\
                    .then_inc(x_done, 1)
                dve.wait_ge(x_done, b + 1)
                dve.bn_stats(core.stats[:, b, :], core.x[:, b, :]).then_inc(s_var, 1)

            def mask_k(b):
                dve.wait_ge(qk_copied, qk_copies * (b + 1))
                dve.tensor_tensor(m.k_jb[:, :, :], over(m.ctxT[:, b, :] if cross else m.kT[:, :], J),
                                  m.mask_j[:, :, :], ALU.mult).then_inc(k_masked, 1)

            def fold(stage):
                if not cross:
                    fold_stage(dve, stage, f.w_up, f.up, f.part_up, f.up_done, forward=True)

            def step(b, par, first=False, stage=None):
                prepare(b + 1, 1 - par, reused=not first)
                if not first:
                    divide(b - 1)
                    if stage is not None:
                        fold(stage)
                    finish(b - 1)
                mask_k(b + 1)
                for g in range(G):
                    maximum(b + 1, g)

            norm_dve(core, dve, s_var)
            dve.wait_ge(s_rstd, 2)
            dve.wait_ge(*((m.cross_loaded, 64) if cross else (f.up_loaded, 48)))
            prepare(0, 0, reused=False)
            mask_k(0)
            for g in range(G):
                maximum(0, g)
            step(0, 0, first=True)
            with dve.Fori(0, PAIRS) as i:
                step(2 * i + 1, 1)
                step(2 * i + 2, 0, stage=i)
            for n, b in enumerate((LAST - 1, LAST)):
                divide(b)
                fold(PAIRS + n)
                finish(b)
            dve.wait_ge(s_var, 6 + B)

        @block.gpsimd
        def _(pool):
            def prepare(b, par):
                pool.wait_ge(normed, b + 1)
                pool.tensor_tensor(core.x[:, b, :], core.x[:, b, :],
                                   m.bias[:, :] if cross else m.n[:, par, :], ALU.add).then_inc(res_made, 1)
                pool.wait_ge(qk_copied, qk_copies * (b + 1))
                kT = m.ctxT[:, b, :] if cross else m.kT[:, :]
                for dst, src, mask in ((m.q_gb[:, :, :], m.qT[:, :], m.mask_g),
                                       (m.k_g[:, par, :, :], kT, m.mask_g),
                                       (m.q_j[:, par, :, :], m.qT[:, :], m.mask_j)):
                    pool.tensor_tensor(dst, over(src, G), mask[:, :, :], ALU.mult).then_inc(masked, 1)

            def fold(stage):
                if cross:
                    fold_stage(pool, stage, f.w_down, f.down_w, f.part_down, f.down_done, forward=False)
                else:
                    fold_stage(pool, stage, f.w_up[0:1], f.bias, f.part_bias, f.bias_done, forward=True)

            norm_pool(core, pool, s_var, s_rstd)
            if cross:
                pool.wait_ge(m.cross_loaded, 64)
            prepare(0, 0)
            prepare(1, 1)
            if cross:
                pool.wait_ge(f.down_loaded, 32)
            else:
                pool.wait_ge(f.up_loaded, 48)
            with pool.Fori(0, PAIRS) as i:
                prepare(2 * i + 2, 0)
                prepare(2 * i + 3, 1)
                fold(i)
            for stage in range(PAIRS, STAGES):
                fold(stage)
            if cross:
                pool.wait_ge(f.bias_loaded, 48)
                pool.tensor_tensor(f.out_bias[:, 0, :], f.out_bias[:, 0, :], f.out_bias[:, 1, :], ALU.add)\
                    .then_inc(f.bias_done, 1)
                pool.wait_ge(f.bias_done, 2 * STAGES + 1)

        @block.scalar
        def _(act):
            def copy_n(b):
                act.wait_ge(n_turned, b + 1)
                dst = m.qT if cross else m.nT
                act.activation(dst[:, :], bank_p[:, 0:T], ACT.Copy)\
                    .then_inc(qk_copied if cross else n_copied, 1)

            def copy_qkv(b, par):
                v_dst = m.v[:, par, :, 0:DH]
                if cross:
                    act.activation(v_dst, m.ctx[:, b, :].rearrange("p (h d) -> p h d", d=DH), ACT.Copy)\
                        .then_inc(v_copied, 1)
                    return
                act.wait_ge(projected, b + 1)
                act.activation(m.qT[:, :], bank_p[:, T:2 * T], ACT.Copy).then_inc(qk_copied, 1)
                act.activation(m.kT[:, :], bank_p[:, 2 * T:3 * T], ACT.Copy).then_inc(qk_copied, 1)
                act.activation(v_dst, bank_p[:, 3 * T:3 * T + D].rearrange("p (h d) -> p h d", d=DH), ACT.Copy)\
                    .then_inc(v_copied, 1)

            def exps(b, g):
                act.wait_ge(shifted, G * b + g + 1)
                act.activation(m.p[:, g, :, :], bank_st[g % 2][:, :].rearrange("p (j t) -> p j t", j=J),
                               ACT.Exp, scale=scale).then_inc(exped, 1)

            def copy_raw(b):
                act.wait_ge(pv_done, b + 1)
                act.activation(m.o_raw[:, :, :], bank_v[:, :].rearrange("p (g t) -> p g t", g=G), ACT.Copy)\
                    .then_inc(raw_copied, 1)

            def copy_o(b):
                act.wait_ge(o_turned, b + 1)
                act.activation(m.oT[:, :], bank_z[:, D:D + T], ACT.Copy).then_inc(o_copied, 1)

            def step(b, par, first=False, last=False):
                if not first:
                    copy_raw(b - 1)
                exps(b, 0)
                if not last:
                    copy_n(b + 1)
                exps(b, 1)
                if not last:
                    copy_qkv(b + 1, 1 - par)
                if not first:
                    copy_o(b - 1)
                exps(b, 2)
                exps(b, 3)

            if cross:
                act.wait_ge(m.cross_loaded, 64)
            copy_n(0)
            copy_qkv(0, 0)
            step(0, 0, first=True)
            with act.Fori(0, PAIRS) as i:
                step(2 * i + 1, 1)
                step(2 * i + 2, 0)
            step(LAST, 1, last=True)
            copy_raw(LAST)
            copy_o(LAST)

        @block.tensor
        def _(pe):
            def turn(b, par):
                pe.wait_ge(normed, b + 1)
                pe.transpose(bank_p[:, 0:T], m.n[:, par, :], core.ident[:, :]).then_inc(n_turned, 1)

            def project(b):
                if cross:
                    return
                pe.wait_ge(n_copied, b + 1)
                pe.matmul(bank_p[:, T:2 * T], m.wq[:, :], m.nT[:, :], start=True, stop=True)
                pe.matmul(bank_p[:, 2 * T:3 * T], m.wk[:, :], m.nT[:, :], start=True, stop=True)
                pe.matmul(bank_p[:, 3 * T:3 * T + D], m.nT[:, :], m.wv[:, :], start=True, stop=True)\
                    .then_inc(projected, 1)

            def scores(b, g):
                if g == 0:
                    pe.wait_ge(masked, 3 * b + 1)
                    pe.wait_ge(k_masked, b + 1)
                if g >= 2:
                    pe.wait_ge(maxed, G * b + g - 1)
                pe.matmul(bank_s[g % 2][:, :], m.q_gb[:, g, :],
                          m.k_jb[:, :, :].rearrange("p j t -> p (j t)"), start=True, stop=True)\
                    .then_inc(scored, 1)

            def shifted_scores(b, par, g):
                if g == 0:
                    pe.wait_ge(masked, 3 * b + 3)
                if g >= 2:
                    pe.wait_ge(exped, G * b + g - 1)
                pe.wait_ge(maxed, G * b + g + 1)
                for j in range(J):
                    h = J * g + j
                    pe.matmul(bank_st[g % 2][:, j * T:(j + 1) * T],
                              m.nmax[:, h:h + 1].to_broadcast([T, T]), core.ident_b[:, :],
                              start=(j == 0), stop=False, skip_group_check=True)
                pe.matmul(bank_st[g % 2][:, :], m.k_g[:, par, g, :],
                          m.q_j[:, par, :, :].rearrange("p j t -> p (j t)"), start=False, stop=True,
                          skip_group_check=True).then_inc(shifted, 1)

            def values(b, par):
                pe.wait_ge(v_copied, b + 1)
                pe.wait_ge(exped, G * b + G - 1)
                for g in range(G):
                    if g == G - 1:
                        pe.wait_ge(exped, G * (b + 1))
                    for j in range(J):
                        mm = pe.matmul(bank_v[32 * j:32 * j + 32, g * T:(g + 1) * T],
                                       m.v[:, par, J * g + j, :], m.p[:, g, j, :], start=True, stop=True)
                mm.then_inc(pv_done, 1)

            def turn_raw(b):
                pe.wait_ge(raw_copied, b + 1)
                for g in range(G):
                    mm = pe.transpose(bank_d[:, g * T:(g + 1) * T], m.o_raw[:, g, :], core.ident[:, :])
                mm.then_inc(raw_turned, 1)

            def turn_o(b):
                pe.wait_ge(o_done, b + 1)
                pe.transpose(bank_z[:, D:D + T], m.o[:, :, :].rearrange("p h d -> p (h d)"), core.ident[:, :])\
                    .then_inc(o_turned, 1)

            def out(b):
                pe.wait_ge(o_copied, b + 1)
                pe.matmul(bank_z[:, 0:D], m.oT[:, :], m.w_out[layer][:, :], start=True, stop=True)\
                    .then_inc(out_done, 1)

            def step(b, par, first=False, last=False):
                shifted_scores(b, par, 0)
                if not last:
                    pe.wait_ge(v_copied, b + 1)
                    turn(b + 1, 1 - par)
                if not first:
                    turn_raw(b - 1)
                shifted_scores(b, par, 1)
                if not last:
                    project(b + 1)
                if not first:
                    turn_o(b - 1)
                shifted_scores(b, par, 2)
                if not first:
                    out(b - 1)
                shifted_scores(b, par, 3)
                if not last:
                    scores(b + 1, 0)
                    scores(b + 1, 1)
                values(b, par)
                if not last:
                    scores(b + 1, 2)
                    scores(b + 1, 3)

            turn(0, 0)
            project(0)
            for g in range(G):
                scores(0, g)
            step(0, 0, first=True)
            with pe.Fori(0, PAIRS) as i:
                step(2 * i + 1, 1)
                step(2 * i + 2, 0)
            step(LAST, 1, last=True)
            turn_raw(LAST)
            turn_o(LAST)
            out(LAST)


H3 = 512
CH = H3 // 128
STAGES = 9
Q = 4


class FoldMem:

    def __init__(self, core, part):
        sb = core.sb

        def sb_part(name, shape):
            return part.enter_context(core.nc.sbuf_tensor(name, shape, FP32))

        self.up = sb("fo_up", [D, H3])
        self.bias = sb("fo_bias", [1, H3])
        self.down_w = sb("fo_down_w", [D, H3])
        self.up_bias = sb("fo_up_bias", [128, CH])
        self.bias_col = sb("fo_bias_col", [128, CH])
        self.down = sb("fo_down", [128, CH, D])
        self.out_bias = sb("fo_out_bias", [T, 2, D])
        self.w_up = sb_part("fo_w_up", [D, STAGES, 2, H3])
        self.w_down = sb_part("fo_w_down", [D, STAGES, 2, H3])
        self.part_up, self.part_down = sb_part("fo_part_up", [D, 2, H3]), sb_part("fo_part_down", [D, 2, H3])
        self.part_bias = sb_part("fo_part_bias", [1, 2, H3])
        self.up_loaded, self.down_loaded, self.bias_loaded, self.up_done, self.down_done, self.bias_done = core.sems(
            "fo", "up_loaded down_loaded bias_loaded up_done down_done bias_done")


def fold_stage(eng, stage, w, row, part, done, forward):
    if not (isinstance(stage, int) and stage == 0):
        eng.wait_ge(done, 2 * stage)
    eng.tensor_tensor(part[:, :, :], w[:, stage, :, :], over(row[:, :], 2), ALU.mult).then_inc(done, 1)
    eng.wait_ge(done, 2 * stage + 1)
    if forward:
        dst = row[:, :].rearrange("p (o k) -> p o k", o=2)
        a, b = (part[:, :, :].rearrange("p o (k i) -> p o k i", i=2)[:, :, :, i] for i in range(2))
    else:
        dst = row[:, :].rearrange("p (k o) -> p o k", o=2)
        a, b = (part[:, :, :].rearrange("p o (i k) -> p o i k", i=2)[:, :, i, :] for i in range(2))
    eng.tensor_tensor(dst, a, b, ALU.add).then_inc(done, 1)


def feed_forward(core, f):
    nc = core.nc
    (folded_turned, folded_copied, s_var, s_rstd, normed, turned, n_copied, biased, up_done, gelu_done, down_done,
     x_done) = core.sems(
        "ff", "folded_turned folded_copied var rstd normed turned n_copied biased up_done gelu_done down_done x_done")
    bank_n, bank_up, bank_down, bank_fold = core.bank[0], core.bank[1:3], core.bank[3:7], core.bank[7]
    groups = B // Q
    with ExitStack() as ctx:
        def sb(name, shape):
            return ctx.enter_context(nc.sbuf_tensor(name, shape, FP32))

        n = sb("ff_n", [T, Q, D])
        nT = sb("ff_nT", [D, Q * T])
        h = sb("ff_h", [128, CH, Q * T])
        w_up = f.up
        with nc.Block() as block:
            @block.vector
            def _(dve):
                def prepare(q):
                    for i in range(Q):
                        normalise(core, dve, n[:, i, :], Q * q + i).then_inc(normed, 1)
                    dve.wait_ge(turned, q + 1)
                    dve.tensor_copy(nT[:, :], bank_n[:, :]).then_inc(n_copied, 1)

                def finish(q):
                    dve.wait_ge(down_done, q + 1)
                    dve.wait_ge(biased, Q * (q + 1))
                    for i in range(Q):
                        dve.tensor_tensor(core.x[:, Q * q + i, :], bank_down[i][:, 0:D], core.x[:, Q * q + i, :],
                                          ALU.add).then_inc(x_done, 1)
                    for i in range(Q):
                        dve.wait_ge(x_done, Q * q + i + 1)
                        dve.bn_stats(core.stats[:, Q * q + i, :], core.x[:, Q * q + i, :]).then_inc(s_var, 1)

                norm_dve(core, dve, s_var)
                dve.wait_ge(s_rstd, 2)
                prepare(0)
                dve.wait_ge(folded_turned, 1)
                dve.tensor_tensor(f.bias_col[:, :], bank_down[0][:, 0:CH], f.up_bias[:, :], ALU.add)\
                    .then_inc(folded_copied, 1)
                with dve.Fori(0, groups - 1) as q:
                    prepare(q + 1)
                    finish(q)
                finish(groups - 1)
                dve.wait_ge(s_var, 6 + B)

            @block.gpsimd
            def _(pool):
                norm_pool(core, pool, s_var, s_rstd)
                with pool.Fori(0, B) as b:
                    pool.wait_ge(normed, b + 1)
                    pool.tensor_tensor(core.x[:, b, :], core.x[:, b, :], f.out_bias[:, 0, :], ALU.add)\
                        .then_inc(biased, 1)

            @block.scalar
            def _(act):
                act.wait_ge(folded_turned, 2)
                act.activation(f.down[:, :, :], bank_fold[:, :].rearrange("p (c d) -> p c d", c=CH), ACT.Copy)\
                    .then_inc(folded_copied, 1)
                act.wait_ge(folded_copied, 2)
                with act.Fori(0, groups) as q:
                    for c in range(CH):
                        act.wait_ge(up_done, CH * q + c + 1)
                        act.activation(h[:, c, :], bank_up[c % 2][:, :], ACT.Gelu, bias=f.bias_col[:, c:c + 1])\
                            .then_inc(gelu_done, 1)

            @block.tensor
            def _(pe):
                def turn(q):
                    pe.wait_ge(normed, Q * (q + 1))
                    for i in range(Q):
                        mm = pe.transpose(bank_n[:, i * T:(i + 1) * T], n[:, i, :], core.ident[:, :])
                    mm.then_inc(turned, 1)

                def up(q, c):
                    if c == 0:
                        pe.wait_ge(n_copied, q + 1)
                    if c >= 2:
                        pe.wait_ge(gelu_done, CH * q + c - 1)
                    pe.matmul(bank_up[c % 2][:, :], w_up[:, c * 128:(c + 1) * 128], nT[:, :],
                              start=True, stop=True).then_inc(up_done, 1)

                def down(q, c, first):
                    pe.wait_ge(gelu_done, CH * q + c + 1)
                    if c == 0 and not first:
                        pe.wait_ge(x_done, Q * q)
                    for i in range(Q):
                        mm = pe.matmul(bank_down[i][:, 0:D], h[:, c, i * T:(i + 1) * T], f.down[:, c, :],
                                       start=(c == 0), stop=(c == CH - 1))
                    if c == CH - 1:
                        mm.then_inc(down_done, 1)

                def step(q, first=False, last=False):
                    up(q, 0)
                    up(q, 1)
                    down(q, 0, first)
                    up(q, 2)
                    down(q, 1, first)
                    up(q, 3)
                    down(q, 2, first)
                    if not last:
                        turn(q + 1)
                    down(q, 3, first)

                turn(0)
                for c in range(CH):
                    mm = pe.matmul(bank_down[0][:, c:c + 1], f.bias[:, c * 128:(c + 1) * 128],
                                   core.ones[0:1, 0:1], start=True, stop=True)
                mm.then_inc(folded_turned, 1)
                for c in range(CH):
                    mm = pe.transpose(bank_fold[:, c * D:(c + 1) * D], f.down_w[:, c * 128:(c + 1) * 128],
                                      core.ident[:, :])
                mm.then_inc(folded_turned, 1)
                pe.wait_ge(folded_copied, 2)
                step(0, first=True)
                with pe.Fori(1, groups - 1) as q:
                    step(q)
                step(groups - 1, last=True)


H4, K4 = 8, 64
C4 = H4 * K4 // 128
DEN_EPS = 1e-6


class LinMem:
    def __init__(self, core):
        sb = core.sb
        self.wq, self.wk, self.wv, self.wg = (sb(f"li_{w}", [D, C4 * 128]) for w in ("wq", "wk", "wv", "wg"))
        self.wo = sb("li_wo", [128, C4, D])
        self.gate_bias = sb("li_gate_bias", [128, C4])
        self.decay = sb("li_decay", [T, H4])
        self.gap = sb("li_gap", [T, T])
        self.tri = sb("li_tri", [T, T])
        self.mask = sb("li_mask", [T, H4, T])
        self.loaded = core.keep_sem("li_loaded")


def linear_attention(core, m):
    nc = core.nc
    (s_var, s_rstd, normed, turned, n_copied, k_proj, q_proj, gate_proj, v_proj, clipped, raised, tanhed,
     v_copied, zeroed, phi_done, a_done, decayed, num_done, den_done, inv_done, y_done, y_turned, gated, out_done,
     x_done) = core.sems(
        "li", "var rstd normed turned n_copied k_proj q_proj gate_proj v_proj clipped raised tanhed v_copied "
        "zeroed phi_done a_done decayed num_done den_done inv_done y_done y_turned gated out_done x_done")
    bank_q, bank_k, bank_g, bank_v = core.bank[0:4]
    bank_a, bank_num = core.bank[4:6], core.bank[6:8]
    bank_y, bank_z = core.bank[4:6]
    half = H4 // 2
    V1 = K4 + 1

    def by_chunk(ap):
        return ap.rearrange("p (c t) -> p c t", c=C4)

    with ExitStack() as ctx:
        def sb(name, shape):
            return ctx.enter_context(nc.sbuf_tensor(name, shape, FP32))

        n = sb("li_n", [T, D])
        nT = sb("li_nT", [D, T])
        clip_k, clip_q = sb("li_clip_k", [128, C4, T]), sb("li_clip_q", [128, C4, T])
        exp_k, exp_q = sb("li_exp_k", [128, C4, T]), sb("li_exp_q", [128, C4, T])
        phi_k = sb("li_phi_k", [128, C4, T])
        phi_q = sb("li_phi_q", [128, C4, 2, T])
        v = sb("li_v", [T, H4, V1])
        tanh = sb("li_tanh", [128, C4, T])
        am = sb("li_am", [T, H4, T])
        den, inv = sb("li_den", [T, H4]), sb("li_inv", [T, H4])
        y = sb("li_y", [T, H4, K4])
        yT = sb("li_yT", [128, C4, T])

        with nc.Block() as block:
            @block.vector
            def _(dve):
                def prepare(b):
                    normalise(core, dve, n[:, :], b).then_inc(normed, 1)

                def phi(b):
                    dve.wait_ge(raised, 2 * b + 1)
                    dve.scalar_tensor_tensor(out=phi_k[:, :, :], in0=by_chunk(bank_k[:, :]), scalar=0.0,
                                             in1=exp_k[:, :, :], op0=ALU.max, op1=ALU.add).then_inc(phi_done, 1)
                    dve.wait_ge(raised, 2 * b + 2)
                    for r in range(2):
                        rows = slice(64 * r, 64 * r + 64)
                        dve.scalar_tensor_tensor(out=phi_q[rows, :, r, :], in0=by_chunk(bank_q[rows, :]), scalar=0.0,
                                                 in1=exp_q[rows, :, :], op0=ALU.max, op1=ALU.add)\
                            .then_inc(phi_done, 1)

                def decay(b):
                    for i in range(2):
                        dve.wait_ge(a_done, 2 * b + i + 1)
                        dve.tensor_tensor(am[:, half * i:half * i + half, :],
                                          bank_a[i][:, :].rearrange("p (h t) -> p h t", h=half),
                                          m.mask[:, half * i:half * i + half, :], ALU.mult).then_inc(decayed, 1)

                def divide(b):
                    dve.wait_ge(num_done, b + 1)
                    for i in range(2):
                        num = bank_num[i][:, 0:half * V1].rearrange("p (h w) -> p h w", w=V1)
                        dve.tensor_scalar(den[:, half * i:half * i + half], num[:, :, K4], DEN_EPS, 2.0,
                                          ALU.add, ALU.mult).then_inc(den_done, 1)
                    dve.wait_ge(den_done, 2 * b + 2)
                    dve.reciprocal(inv[:, :], den[:, :]).then_inc(inv_done, 1)
                    dve.wait_ge(inv_done, b + 1)
                    for i in range(2):
                        num = bank_num[i][:, 0:half * V1].rearrange("p (h w) -> p h w", w=V1)
                        dve.tensor_tensor(y[:, half * i:half * i + half, :], num[:, :, 0:K4],
                                          inv[:, half * i:half * i + half].unsqueeze(2)
                                          .to_broadcast([T, half, K4]), ALU.mult).then_inc(y_done, 1)

                def gate(b):
                    dve.wait_ge(y_turned, b + 1)
                    dve.wait_ge(tanhed, b + 1)
                    dve.scalar_tensor_tensor(out=yT[:, :, :], in0=tanh[:, :, :], scalar=1.0,
                                             in1=by_chunk(bank_y[:, :]), op0=ALU.add, op1=ALU.mult)\
                        .then_inc(gated, 1)

                def finish(b):
                    dve.wait_ge(out_done, b + 1)
                    dve.tensor_tensor(core.x[:, b, :], bank_z[:, 0:D], core.x[:, b, :], ALU.add).then_inc(x_done, 1)
                    dve.wait_ge(x_done, b + 1)
                    dve.bn_stats(core.stats[:, b, :], core.x[:, b, :]).then_inc(s_var, 1)

                def step(b, last=False):
                    if not last:
                        prepare(b + 1)
                    decay(b)
                    divide(b)
                    gate(b)
                    if not last:
                        phi(b + 1)
                    finish(b)

                dve.memset(phi_q[:, :, :, :], 0.0).then_inc(zeroed, 1)
                dve.memset(v[:, :, K4:V1], 1.0).then_inc(zeroed, 1)
                norm_dve(core, dve, s_var)
                dve.wait_ge(s_rstd, 2)
                prepare(0)
                dve.wait_ge(zeroed, 2)
                phi(0)
                with dve.Fori(0, B - 1) as b:
                    step(b)
                step(B - 1, last=True)
                dve.wait_ge(s_var, 6 + B)

            @block.gpsimd
            def _(pool):
                norm_pool(core, pool, s_var, s_rstd)

            @block.scalar
            def _(act):
                def prepare(b, first=False):
                    act.wait_ge(turned, b + 1)
                    act.activation(nT[:, :], bank_v[:, 0:T], ACT.Copy).then_inc(n_copied, 1)
                    for i, (proj, bank, clip, ex) in enumerate(((k_proj, bank_k, clip_k, exp_k),
                                                                (q_proj, bank_q, clip_q, exp_q))):
                        act.wait_ge(proj, b + 1)
                        act.activation(clip[:, :, :], by_chunk(bank[:, :]), ACT.Relu, scale=-1.0)\
                            .then_inc(clipped, 1)
                        act.wait_ge(clipped, 2 * b + i + 1)
                        act.activation(ex[:, :, :], clip[:, :, :], ACT.Exp, scale=-1.0).then_inc(raised, 1)
                    act.wait_ge(v_proj, b + 1)
                    act.activation(v[:, :, 0:K4], bank_v[:, :].rearrange("p (h w) -> p h w", h=H4), ACT.Copy)\
                        .then_inc(v_copied, 1)
                    act.wait_ge(gate_proj, b + 1)
                    if not first:
                        act.wait_ge(gated, b)
                    for c in range(C4):
                        ins = act.activation(tanh[:, c, :], bank_g[:, c * T:(c + 1) * T], ACT.Tanh,
                                             bias=m.gate_bias[:, c:c + 1], scale=0.5)
                    ins.then_inc(tanhed, 1)

                act.wait_ge(zeroed, 2)
                prepare(0, first=True)
                with act.Fori(1, B) as b:
                    prepare(b)

            @block.tensor
            def _(pe):
                def turn(b):
                    pe.wait_ge(normed, b + 1)
                    pe.transpose(bank_v[:, 0:T], n[:, :], core.ident[:, :]).then_inc(turned, 1)

                def project(b, w, bank, proj):
                    for c in range(C4):
                        mm = pe.matmul(bank[:, c * T:(c + 1) * T], w[:, c * 128:(c + 1) * 128], nT[:, :],
                                       start=True, stop=True)
                    mm.then_inc(proj, 1)

                def project_kq(b):
                    pe.wait_ge(n_copied, b + 1)
                    project(b, m.wk, bank_k, k_proj)
                    project(b, m.wq, bank_q, q_proj)

                def project_v(b):
                    pe.matmul(bank_v[:, :], nT[:, :], m.wv[:, :], start=True, stop=True).then_inc(v_proj, 1)

                def project_g(b, first=False):
                    if not first:
                        pe.wait_ge(tanhed, b)
                    project(b, m.wg, bank_g, gate_proj)

                def attend(b, first=False):
                    pe.wait_ge(phi_done, 3 * (b + 1))
                    for c in range(C4):
                        if c == C4 // 2 and not first:
                            pe.wait_ge(x_done, b)
                        mm = pe.matmul(bank_a[c // 2][:, 256 * (c % 2):256 * (c % 2) + 256], phi_k[:, c, :],
                                       phi_q[:, c, :, :].rearrange("p r t -> p (r t)"), start=True, stop=True)
                        if c % 2:
                            mm.then_inc(a_done, 1)

                def numerator(b):
                    pe.wait_ge(v_copied, b + 1)
                    for h in range(H4):
                        if h % half == 0:
                            pe.wait_ge(decayed, 2 * b + h // half + 1)
                        i = h % half
                        mm = pe.matmul(bank_num[h // half][:, i * V1:(i + 1) * V1], am[:, h, :], v[:, h, :],
                                       start=True, stop=True)
                    mm.then_inc(num_done, 1)

                def turn_y(b):
                    pe.wait_ge(y_done, 2 * b + 2)
                    for c in range(C4):
                        mm = pe.transpose(bank_y[:, c * T:(c + 1) * T],
                                          y[:, 2 * c:2 * c + 2, :].rearrange("p h w -> p (h w)"), core.ident[:, :])
                    mm.then_inc(y_turned, 1)

                def out(b):
                    pe.wait_ge(gated, b + 1)
                    for c in range(C4):
                        mm = pe.matmul(bank_z[:, 0:D], yT[:, c, :], m.wo[:, c, :],
                                       start=(c == 0), stop=(c == C4 - 1))
                    mm.then_inc(out_done, 1)

                def step(b, first=False, last=False):
                    attend(b, first)
                    if not last:
                        pe.wait_ge(v_copied, b + 1)
                        turn(b + 1)
                    numerator(b)
                    if not last:
                        project_kq(b + 1)
                    turn_y(b)
                    if not last:
                        project_v(b + 1)
                    out(b)
                    if not last:
                        project_g(b + 1)

                pe.wait_ge(m.loaded, 80)
                turn(0)
                project_kq(0)
                project_v(0)
                project_g(0, first=True)
                step(0, first=True)
                with pe.Fori(1, B - 1) as b:
                    step(b)
                step(B - 1, last=True)


NH5 = 16
D5 = D // NH5
TOP = 4
COS, SIN, CAS, SAC = range(4)
BH = B * NH5
HALVES = BH // 128


def autocorrelation(core, a):
    nc = core.nc
    groups = B // Q
    (loaded, ctx_loaded0, ctx_loaded1, zeroed, scaled, s_var, s_rstd, normed, q_turned, c_turned, zq_copied, zc_copied, projected, read,
     spectra, odd_done, even_done, diff_done, summed, corr_done, corr_copied, top, idx, coded, w_sum, w_exp, kernels,
     k_turned, k_copied, k_spec, k_spec_copied, biased, y_part, y_done, o_done, o_copied, out_done, x_done) = core.sems(
        "au", "loaded ctx_loaded0 ctx_loaded1 zeroed scaled var rstd normed q_turned c_turned zq_copied zc_copied projected read "
        "spectra odd_done even_done diff_done summed corr_done corr_copied top idx coded w_sum w_exp kernels "
        "k_turned k_copied k_spec k_spec_copied biased y_part y_done o_done o_copied out_done x_done")
    ctx_loaded = (ctx_loaded0, ctx_loaded1)
    bank_zq, bank_zc = core.bank[0:2]
    bank_qc, bank_qs, bank_ke, bank_ko, bank_vc, bank_vs = core.bank[2:8]

    def four(ap):
        return ap.rearrange("p (i d) -> p i d", i=Q)

    with ExitStack() as ctx:
        def sb(name, shape, dt=FP32):
            return ctx.enter_context(nc.sbuf_tensor(name, shape, dt))

        dft = sb("au_dft", [T, 4, T])
        inv = sb("au_inv", [T, T])
        wq, wk, wv, wo = (sb(f"au_{w}", [D, D]) for w in ("wq", "wk", "wv", "wo"))
        bias = [sb(f"au_bias_{w}", [T, Q, D]) for w in ("q", "k", "v")]
        out_bias = sb("au_out_bias", [T, D])
        iota = sb("au_iota", [128, T])
        n = sb("au_n", [T, 2, Q, D])
        cx = sb("au_ctx", [T, 2, Q, D])
        zq = sb("au_zq", [D, 2, 2, T])
        zc = sb("au_zc", [D, 2, 4, T])
        q_cas, q_sac = sb("au_q_cas", [T, Q, D]), sb("au_q_sac", [T, Q, D])
        k_even = sb("au_k_even", [T, Q, D])
        even, odd = sb("au_even", [T, 2, Q, D]), sb("au_odd", [T, 2, Q, D])
        v_cas, v_sac = sb("au_v_cas", [T, B, D]), sb("au_v_sac", [T, B, D])
        spec = sb("au_spec", [T, B, NH5])
        corr = sb("au_corr", [128, HALVES, T])
        top_v = sb("au_top_v", [128, HALVES, 8])
        top_i = sb("au_top_i", [128, HALVES, 8], U32)
        lag = sb("au_lag", [128, HALVES, 8])
        w, w_tot, w_inv = sb("au_w", [128, HALVES, TOP]), sb("au_w_tot", [128, HALVES]), sb("au_w_inv", [128, HALVES])
        pick = sb("au_pick", [128, HALVES, TOP, T])
        kern_t = sb("au_kern_t", [T, BH])
        k_sp = sb("au_k_sp", [T, 2, B, NH5])
        y_even, y_odd = sb("au_y_even", [T, 2, Q, D]), sb("au_y_odd", [T, 2, Q, D])
        oT = sb("au_oT", [D, 2, T])

        with nc.Block() as block:
            @block.sync
            def _(sp):
                def load_ctx(g):
                    sp.dma_start(cx[:, g % 2, :, :],
                                 a["ctx_1024"][Q * g:Q * g + Q].rearrange("b t d -> t b d"))\
                        .then_inc(ctx_loaded[g % 2], 16)

                sp.dma_start(dft[:, :, :], a["c_dft"].rearrange("p (k t) -> p k t", k=4)).then_inc(loaded, 16)
                load_ctx(0)
                for dst, src in ((wq, "auto_WqT"), (wk, "auto_WkT"), (wv, "auto_WvT"), (wo, "auto_WoT"),
                                 (iota, "c_iota")):
                    sp.dma_start(dst[:, :], a[src]).then_inc(loaded, 16)
                sp.dma_start(out_bias[:, :], a["L1_xattn_bo"].partition_broadcast(T)).then_inc(loaded, 16)
                load_ctx(1)
                sp.wait_ge(zeroed, 3)
                for dst, src in zip(bias, ("L1_xattn_bq", "L1_xattn_bk", "L1_xattn_bv")):
                    for i in range(Q):
                        sp.dma_start(dst[0:1, i, :], a[src].unsqueeze(0)).then_inc(loaded, 16)
                for g in range(2, groups):
                    sp.wait_ge(c_turned, Q * (g - 1))
                    load_ctx(g)

            @block.vector
            def _(dve):
                def prepare(g, par):
                    for i in range(Q):
                        normalise(core, dve, n[:, par, i, :], Q * g + i).then_inc(normed, 1)

                def correlate(g, par):
                    dve.wait_ge(projected, Q * (g + 1))
                    dve.wait_ge(even_done, g)
                    for dst, bank, b in ((q_cas[:, :, :], bank_qc, bias[0]), (k_even[:, :, :], bank_ke, bias[1]),
                                         (q_sac[:, :, :], bank_qs, bias[0]),
                                         (v_cas[:, bass.ds(Q * g, Q), :], bank_vc, bias[2]),
                                         (v_sac[:, bass.ds(Q * g, Q), :], bank_vs, bias[2])):
                        dve.tensor_tensor(dst, four(bank[:, :]), b[:, :, :], ALU.add).then_inc(spectra, 1)
                    dve.wait_ge(spectra, 5 * g + 3)
                    dve.tensor_tensor(odd[:, par, :, :], four(bank_ko[:, :]), q_sac[:, :, :], ALU.mult)\
                        .then_inc(odd_done, 1)

                def head_sums(g, par):
                    dve.wait_ge(diff_done, g + 1)
                    dve.tensor_reduce(spec[:, bass.ds(Q * g, Q), :],
                                      even[:, par, :, :].rearrange("p i (h d) -> p i h d", d=D5), AX.X, ALU.add)\
                        .then_inc(summed, 1)

                for t in bias:
                    dve.memset(t[:, :, :], 0.0).then_inc(zeroed, 1)
                norm_dve(core, dve, s_var)
                dve.wait_ge(s_rstd, 2)
                prepare(0, 0)
                prepare(1, 1)
                dve.wait_ge(loaded, 16 * (7 + 3 * Q))
                for t in bias:
                    dve.tensor_scalar(t[0:1, :, :], t[0:1, :, :], float(T), None, ALU.mult).then_inc(scaled, 1)
                dve.tensor_scalar(inv[:, :], dft[:, CAS, :], 1.0 / T, None, ALU.mult).then_inc(scaled, 1)
                dve.wait_ge(scaled, 4)
                dve.sem_inc(even_done, 1)
                for g in range(groups):
                    correlate(g, g % 2)
                    if g + 2 < groups:
                        dve.wait_ge(q_turned, Q * (g + 1))
                        prepare(g + 2, g % 2)
                    head_sums(g, g % 2)

                for i in range(HALVES):
                    dve.wait_ge(corr_copied, i + 1)
                    dve.max(top_v[:, i, :], corr[:, i, :]).then_inc(top, 1)
                dve.wait_ge(top, HALVES)
                for i in range(HALVES):
                    dve.max_index(top_i[:, i, :], top_v[:, i, :], corr[:, i, :]).then_inc(idx, 1)
                dve.tensor_tensor(w[:, :, :], top_v[:, :, 0:TOP], top_v[:, :, 0:1].to_broadcast([128, HALVES, TOP]),
                                  ALU.subtract).then_inc(coded, 1)
                dve.wait_ge(idx, HALVES)
                dve.tensor_copy(lag[:, :, :], top_i[:, :, :]).then_inc(coded, 1)
                dve.wait_ge(w_exp, 1)
                dve.tensor_reduce(w_tot[:, :], w[:, :, :], AX.X, ALU.add).then_inc(w_sum, 1)
                dve.wait_ge(w_sum, 1)
                dve.reciprocal(w_inv[:, :], w_tot[:, :]).then_inc(w_sum, 1)
                dve.wait_ge(w_sum, 2)
                dve.tensor_tensor(w[:, :, :], w[:, :, :], w_inv[:, :].unsqueeze(2).to_broadcast([128, HALVES, TOP]),
                                  ALU.mult).then_inc(w_sum, 1)
                dve.wait_ge(w_sum, 3)
                dve.wait_ge(coded, 2)
                for i in range(HALVES):
                    for k in range(TOP):
                        dve.tensor_scalar(pick[:, i, k, :], iota[:, :], lag[:, i, k:k + 1], w[:, i, k:k + 1],
                                          ALU.is_equal, ALU.mult).then_inc(kernels, 1)
                count = HALVES * TOP
                for step in (2, 1):
                    dve.wait_ge(kernels, count)
                    dve.tensor_tensor(pick[:, :, 0:step, :], pick[:, :, 0:step, :], pick[:, :, step:2 * step, :],
                                      ALU.add).then_inc(kernels, 1)
                    count += 1

                def convolve(g, par):
                    k = [k_sp[:, r, bass.ds(Q * g, Q), :].rearrange("p b h -> p (b h)").unsqueeze(2)
                         .to_broadcast([T, Q * NH5, D5]) for r in range(2)]
                    for r, (y, src) in enumerate(((y_even, v_cas), (y_odd, v_sac))):
                        dve.tensor_tensor(y[:, par, :, :].rearrange("p i (h d) -> p (i h) d", d=D5),
                                          src[:, bass.ds(Q * g, Q), :].rearrange("p i (h d) -> p (i h) d", d=D5),
                                          k[r], ALU.mult).then_inc(y_part, 1)
                    dve.wait_ge(y_part, 2 * g + 2)
                    dve.tensor_tensor(y_even[:, par, :, :], y_even[:, par, :, :], y_odd[:, par, :, :], ALU.add)\
                        .then_inc(y_done, 1)

                def finish(b):
                    dve.wait_ge(out_done, b + 1)
                    dve.tensor_tensor(core.x[:, b, :], core.bank[2 + b % 2][:, 0:D], core.x[:, b, :], ALU.add)\
                        .then_inc(x_done, 1)
                    dve.wait_ge(x_done, b + 1)
                    dve.bn_stats(core.stats[:, b, :], core.x[:, b, :]).then_inc(s_var, 1)

                dve.wait_ge(k_spec_copied, 2)
                dve.wait_ge(biased, B)
                convolve(0, 0)
                for g in range(groups):
                    if g + 1 < groups:
                        if g >= 1:
                            dve.wait_ge(o_done, Q * g)
                        convolve(g + 1, (g + 1) % 2)
                    for i in range(Q):
                        finish(Q * g + i)
                dve.wait_ge(s_var, 6 + B)

            @block.gpsimd
            def _(pool):
                norm_pool(core, pool, s_var, s_rstd)
                for g in range(groups):
                    par = g % 2
                    pool.wait_ge(spectra, 5 * g + 2)
                    if g >= 2:
                        pool.wait_ge(summed, g - 1)
                    pool.tensor_tensor(even[:, par, :, :], q_cas[:, :, :], k_even[:, :, :], ALU.mult)\
                        .then_inc(even_done, 1)
                    pool.wait_ge(odd_done, g + 1)
                    pool.wait_ge(even_done, g + 2)
                    pool.tensor_tensor(even[:, par, :, :], even[:, par, :, :], odd[:, par, :, :], ALU.subtract)\
                        .then_inc(diff_done, 1)
                pool.wait_ge(normed, B)
                pool.wait_ge(loaded, 16 * (7 + 3 * Q))
                with pool.Fori(0, B) as b:
                    pool.tensor_tensor(core.x[:, b, :], core.x[:, b, :], out_bias[:, :], ALU.add).then_inc(biased, 1)

            @block.scalar
            def _(act):
                for b in range(B):
                    act.wait_ge(q_turned, b + 1)
                    if b >= 2:
                        act.wait_ge(projected, b - 1)
                    act.activation(zq[:, b % 2, :, :], bank_zq[:, 0:2 * T].rearrange("p (k t) -> p k t", k=2),
                                   ACT.Copy).then_inc(zq_copied, 1)
                    act.wait_ge(c_turned, b + 1)
                    act.activation(zc[:, b % 2, :, :], bank_zc[:, :].rearrange("p (k t) -> p k t", k=4),
                                   ACT.Copy).then_inc(zc_copied, 1)
                for i in range(HALVES):
                    act.wait_ge(corr_done, i + 1)
                    act.activation(corr[:, i, :], core.bank[i][:, 0:T], ACT.Copy, scale=1.0 / D5)\
                        .then_inc(corr_copied, 1)
                act.wait_ge(coded, 1)
                act.activation(w[:, :, :], w[:, :, :], ACT.Exp).then_inc(w_exp, 1)
                act.wait_ge(k_turned, 1)
                act.activation(kern_t[:, :], core.bank[4][:, 0:BH], ACT.Copy).then_inc(k_copied, 1)
                for r in range(2):
                    act.wait_ge(k_spec, r + 1)
                    act.activation(k_sp[:, r, :, :], core.bank[5 + r][:, 0:BH].rearrange("p (b h) -> p b h", b=B),
                                   ACT.Copy).then_inc(k_spec_copied, 1)
                for b in range(B):
                    act.wait_ge(o_done, b + 1)
                    if b >= 2:
                        act.wait_ge(out_done, b - 1)
                    act.activation(oT[:, b % 2, :], core.bank[b % 2][:, 0:T], ACT.Copy).then_inc(o_copied, 1)

            @block.tensor
            def _(pe):
                def transform(b):
                    g, i = b // Q, b % Q
                    if b >= 1:
                        pe.wait_ge(zq_copied, b)
                    pe.wait_ge(normed, b + 1)
                    pe.matmul(bank_zq[:, 0:2 * T], n[:, g % 2, i, :],
                              dft[:, CAS:SAC + 1, :].rearrange("p k t -> p (k t)"), start=True, stop=True)\
                        .then_inc(q_turned, 1)
                    if b >= 1:
                        pe.wait_ge(zc_copied, b)
                    pe.wait_ge(ctx_loaded[g % 2], 16 * (g // 2 + 1))
                    pe.matmul(bank_zc[:, :], cx[:, g % 2, i, :], dft[:, :, :].rearrange("p k t -> p (k t)"),
                              start=True, stop=True).then_inc(c_turned, 1)

                def project(b):
                    g, i = b // Q, b % Q
                    if i == 0 and g >= 1:
                        pe.wait_ge(spectra, 5 * g)
                        pe.wait_ge(odd_done, g)
                    cols = slice(i * D, (i + 1) * D)
                    pe.wait_ge(zq_copied, b + 1)
                    pe.matmul(bank_qc[:, cols], zq[:, b % 2, 0, :], wq[:, :], start=True, stop=True)
                    pe.matmul(bank_qs[:, cols], zq[:, b % 2, 1, :], wq[:, :], start=True, stop=True)
                    pe.wait_ge(zc_copied, b + 1)
                    for bank, k, wgt in ((bank_ke, COS, wk), (bank_ko, SIN, wk), (bank_vc, CAS, wv),
                                         (bank_vs, SAC, wv)):
                        mm = pe.matmul(bank[:, cols], zc[:, b % 2, k, :], wgt[:, :], start=True, stop=True)
                    mm.then_inc(projected, 1)

                pe.wait_ge(loaded, 16 * (7 + 3 * Q))
                transform(0)
                for b in range(B):
                    if b + 1 < B:
                        transform(b + 1)
                    project(b)
                pe.wait_ge(scaled, 4)
                for i in range(HALVES):
                    seqs = B // HALVES
                    pe.wait_ge(summed, groups // HALVES * (i + 1))
                    pe.matmul(core.bank[i][:, 0:T],
                              spec[:, seqs * i:seqs * (i + 1), :].rearrange("p b h -> p (b h)"), inv[:, :],
                              start=True, stop=True).then_inc(corr_done, 1)
                pe.wait_ge(kernels, HALVES * TOP + 2)
                for i in range(HALVES):
                    mm = pe.transpose(core.bank[4][:, i * 128:(i + 1) * 128], pick[:, i, 0, :], core.ident[:, :])
                mm.then_inc(k_turned, 1)
                pe.wait_ge(k_copied, 1)
                for r, k in enumerate((COS, SIN)):
                    pe.matmul(core.bank[5 + r][:, 0:BH], dft[:, k, :], kern_t[:, :], start=True, stop=True)\
                        .then_inc(k_spec, 1)

                def inverse(b):
                    g, i = b // Q, b % Q
                    if i == 0:
                        pe.wait_ge(y_done, g + 1)
                    if b >= 2:
                        pe.wait_ge(o_copied, b - 1)
                    pe.matmul(core.bank[b % 2][:, 0:T], y_even[:, g % 2, i, :], inv[:, :], start=True, stop=True)\
                        .then_inc(o_done, 1)

                def out(b):
                    pe.wait_ge(o_copied, b + 1)
                    if b >= 2:
                        pe.wait_ge(x_done, b - 1)
                    pe.matmul(core.bank[2 + b % 2][:, 0:D], oT[:, b % 2, :], wo[:, :], start=True, stop=True)\
                        .then_inc(out_done, 1)

                inverse(0)
                for b in range(B):
                    if b + 1 < B:
                        inverse(b + 1)
                    out(b)


E6 = 8
H6 = 512
CH6 = H6 // 128
CAP = -(-12 * B * T // (10 * E6))
ROWS = [min(128, CAP - r) for r in range(0, CAP, 128)]
TILES = E6 * len(ROWS)
DROPPED = 4096
BITS = 30
ROUND = 3
TRIALS = (1 << ROUND) - 1


def experts(core, a, out):
    nc = core.nc
    n_rows = nc.dram_tensor("mo_n_rows", (B * T, D), FP32, kind="Internal").ap()
    planes = nc.dram_tensor("mo_planes", (2 * B * T, D), FP32, kind="Internal").ap()
    with ExitStack() as ctx:
        def sb(name, shape, dt=FP32):
            return ctx.enter_context(nc.sbuf_tensor(name, shape, dt))

        gate = [sb(f"mo_gate{k}", [T, B]) for k in range(2)]
        src_row = sb("mo_src_row", [128, TILES], U32)
        dst_row = sb("mo_dst_row", [128, TILES], U32)
        b1 = sb("mo_b1", [128, E6, CH6])
        b2 = sb("mo_b2", [128, E6, D])
        with ExitStack() as part:
            route(core, a, part, gate, src_row, dst_row, n_rows, planes, b1, b2)
        expert_loop(core, a, out, gate, src_row, dst_row, n_rows, planes, b1, b2)


def route(core, a, ctx, gate, src_row, dst_row, n_rows, planes, b1, b2):
    nc = core.nc
    groups = B // Q

    def sb(name, shape, dt=FP32):
        return ctx.enter_context(nc.sbuf_tensor(name, shape, dt))

    wr, br = sb("ro_wr", [D, E6]), sb("ro_br", [T, E6])
    iota = sb("ro_iota", [T, E6])
    base = sb("ro_base", [128, 1])
    trial_bits = sb("ro_trial_bits", [128, BITS // ROUND, TRIALS], I32)
    same = sb("ro_same", [128, 128])
    earlier = sb("ro_earlier", [128, 128])
    lanes = sb("ro_lanes", [T, T])
    lanes_b = sb("ro_lanes_b", [T, T], BF16)
    lane = sb("ro_lane", [128, 1])
    seq_code = sb("ro_seq_code", [T, 2, B])
    n4, nT = sb("ro_n4", [T, 2, Q, D]), sb("ro_nT", [D, Q * T])
    p, tmp, tmp2 = sb("ro_p", [T, B, E6]), sb("ro_tmp", [T, B, E6]), sb("ro_tmp2", [T, B, E6])
    pick = [sb(f"ro_pick{k}", [T, B, E6]) for k in range(2)]
    v = sb("ro_v", [T, B, E6])
    red = sb("ro_red", [T, B])
    vT, positive = sb("ro_vT", [128, T]), sb("ro_positive", [128, T])
    reached = sb("ro_reached", [128, TRIALS, T], BF16)
    trial = sb("ro_trial", [128, TRIALS], I32)
    count = sb("ro_count", [128, TRIALS])
    passed = sb("ro_passed", [128, 1 + TRIALS])
    keep, equal, upto = sb("ro_keep", [128, T]), sb("ro_equal", [128, T]), sb("ro_upto", [128, T])
    level = passed[:, 0:1]
    need, offset = sb("ro_need", [128, 1]), sb("ro_offset", [128, 1])
    zeros = sb("ro_zeros", [128, 2 * D])
    slot_f = sb("ro_slot_f", [T, 2, B])
    slot_i, slot_lo, slot_hi = (sb(f"ro_{w}", [T, 2, B], I32) for w in ("slot_i", "slot_lo", "slot_hi"))
    lo, hi = sb("ro_lo", [T, 2, B], BF16), sb("ro_hi", [T, 2, B])
    at_row = sb("ro_at_row", [T, 2, B, 128], BF16)
    at_tile = sb("ro_at_tile", [T, 2, B, TILES])
    codes = sb("ro_codes", [T, 2, B, 2, TILES], BF16)
    code_sum = sb("ro_code_sum", [128, 2, TILES])
    empty = sb("ro_empty", [128, TILES])
    (loaded, n_out0, n_out1, cleared, made, s_var, s_rstd, normed, turned, n_copied, logits, biased, s, expd, v_turned, counted,
     compared, totalled, summed, slots_turned, lanes_made, rows_marked, coded, mapped) = core.sems(
        "ro", "loaded n_out0 n_out1 cleared made var rstd normed turned n_copied logits biased step expd v_turned counted "
        "compared totalled summed slots_turned lanes_made rows_marked coded mapped")
    n_out = (n_out0, n_out1)
    bank_n, bank_c, bank_v, bank_s, bank_m = core.bank[0:5]
    bank_l = core.bank[5:7]
    CONSTANTS = 12
    picked = 18

    def per_token(ap):
        return ap.unsqueeze(2).to_broadcast([T, B, E6])

    def per_expert(ap):
        return ap.unsqueeze(1).to_broadcast([T, B, E6])

    with nc.Block() as block:
        @block.sync
        def _(sp):
            for dst, src in ((wr, a["L1_ffn_Wr"]), (br, a["L1_ffn_br"].partition_broadcast(T)),
                             (iota, a["c_expert"].partition_broadcast(T)), (base, a["c_base"]), (same, a["c_same"]),
                             (earlier, a["c_earlier"]), (lanes, a["c_iota"]), (lane, a["c_lane"])):
                sp.dma_start(dst[:, :], src).then_inc(loaded, 16)
            for dst, src in ((trial_bits, "c_trial_bits"), (seq_code, "c_seq_code")):
                sp.dma_start(dst[:, :, :].rearrange("t i e -> t (i e)"), a[src].partition_broadcast(T))\
                    .then_inc(loaded, 16)
            sp.dma_start(b1[:, :, :], a["moe_b1_col"].rearrange("p (e c) -> p e c", e=E6)).then_inc(loaded, 16)
            sp.dma_start(b2[:, :, :].rearrange("p e d -> p (e d)"),
                         a["L1_ffn_b2"].rearrange("e d -> (e d)").partition_broadcast(T)).then_inc(loaded, 16)
            with sp.Fori(0, groups // 2) as i:
                for par in range(2):
                    g = 2 * i + par
                    sp.wait_ge(normed, Q * (g + 1))
                    sp.dma_start(n_rows[bass.ds(Q * T * g, Q * T), :].rearrange("(i t) d -> t i d", i=Q),
                                 n4[:, par, :, :]).then_inc(n_out[par], 16)
            sp.wait_ge(loaded, 16 * CONSTANTS)
            for par in range(2):
                sp.wait_ge(n_out[par], 16 * groups // 2)

        @block.gpsimd
        def _(pool):
            pool.memset(zeros[:, :], 0.0).then_inc(made, 1)
            norm_pool(core, pool, s_var, s_rstd)
            pool.wait_ge(made, 1)
            pool.dma_start(planes.rearrange("s d -> (s d)").rearrange("(p e n) -> p e n", p=128, n=2 * D),
                           over(zeros[:, :], B)).then_inc(cleared, 16)
            pool.wait_ge(cleared, 16)

        @block.scalar
        def _(act):
            with act.Fori(0, groups) as g:
                act.wait_ge(turned, g + 1)
                act.activation(nT[:, :], bank_n[:, :], ACT.Copy).then_inc(n_copied, 1)
            act.wait_ge(s, 2)
            act.activation(p[:, :, :], p[:, :, :], ACT.Exp).then_inc(expd, 1)

        @block.tensor
        def _(pe):
            pe.wait_ge(loaded, 16 * CONSTANTS)
            with pe.Fori(0, groups // 2) as j:
                for par in range(2):
                    g = 2 * j + par
                    pe.wait_ge(normed, Q * (g + 1))
                    for i in range(Q):
                        mm = pe.transpose(bank_n[:, i * T:(i + 1) * T], n4[:, par, i, :], core.ident[:, :])
                    mm.then_inc(turned, 1)
                    pe.wait_ge(n_copied, g + 1)
                    for i in range(Q):
                        mm = pe.matmul(bank_l[par][:, i * E6:(i + 1) * E6], nT[:, i * T:(i + 1) * T], wr[:, :],
                                       start=True, stop=True)
                    mm.then_inc(logits, 1)
            pe.wait_ge(s, picked)
            pe.transpose(bank_v[:, 0:T], v[:, :, :].rearrange("t b e -> t (b e)"), core.ident[:, :])\
                .then_inc(v_turned, 1)
            with pe.Fori(0, BITS // ROUND) as i:
                pe.wait_ge(counted, i + 1)
                pe.matmul(bank_c[:, 0:TRIALS], same[:, :], count[:, :], start=True, stop=True).then_inc(compared, 1)
            pe.wait_ge(counted, BITS // ROUND + 1)
            pe.matmul(bank_c[:, 0:1], same[:, :], count[:, 0:1], start=True, stop=True).then_inc(compared, 1)
            for k in range(2):
                pe.wait_ge(totalled, k + 1)
                pe.matmul(bank_s[:, k:k + 1], earlier[:, :], upto[:, T - 1:T], start=True, stop=True)\
                    .then_inc(summed, 1)
            pe.wait_ge(totalled, 3)
            pe.transpose(bank_v[:, 0:128], upto[:, :], core.ident[:, :]).then_inc(slots_turned, 1)
            pe.wait_ge(coded, 2)
            for k in range(2):
                pe.wait_ge(rows_marked, k + 1)
                for b in range(B):
                    mm = pe.matmul(bank_m[:, 0:2 * TILES], at_row[:, k, b, :],
                                   codes[:, k, b, :, :].rearrange("t c s -> t (c s)"),
                                   start=(k == 0 and b == 0), stop=(k == 1 and b == B - 1))
            mm.then_inc(mapped, 1)

        @block.vector
        def _(dve):
            steps = 0

            def done(ins):
                nonlocal steps
                steps += 1
                ins.then_inc(s, 1)
                dve.wait_ge(s, steps)

            def prepare(g, par):
                for i in range(Q):
                    normalise(core, dve, n4[:, par, i, :], Q * g + i).then_inc(normed, 1)

            def add_bias(g, par):
                dve.wait_ge(logits, g + 1)
                dve.tensor_tensor(p[:, bass.ds(Q * g, Q), :],
                                  bank_l[par][:, 0:Q * E6].rearrange("t (i e) -> t i e", i=Q),
                                  over(br[:, :], Q), ALU.add).then_inc(biased, 1)

            norm_dve(core, dve, s_var)
            dve.wait_ge(s_rstd, 2)
            prepare(0, 0)
            prepare(1, 1)
            dve.wait_ge(loaded, 16 * CONSTANTS)
            dve.tensor_copy(lanes_b[:, :], lanes[:, :]).then_inc(lanes_made, 1)
            with dve.Fori(0, groups // 2 - 1) as i:
                for par in range(2):
                    add_bias(2 * i + par, par)
                    dve.wait_ge(n_out[par], 16 * (i + 1))
                    prepare(2 * i + par + 2, par)
            for par in range(2):
                add_bias(groups - 2 + par, par)
            dve.wait_ge(biased, groups)

            done(dve.tensor_reduce(red[:, :], p[:, :, :], AX.X, ALU.max))
            done(dve.tensor_tensor(p[:, :, :], p[:, :, :], per_token(red[:, :]), ALU.subtract))
            dve.wait_ge(expd, 1)
            done(dve.tensor_reduce(red[:, :], p[:, :, :], AX.X, ALU.add))
            done(dve.reciprocal(red[:, :], red[:, :]))
            done(dve.tensor_tensor(p[:, :, :], p[:, :, :], per_token(red[:, :]), ALU.mult))

            for k in range(2):
                q = (p, tmp2)[k]
                done(dve.tensor_reduce(gate[k][:, :], q[:, :, :], AX.X, ALU.max))
                done(dve.tensor_tensor(tmp[:, :, :], q[:, :, :], per_token(gate[k][:, :]), ALU.is_equal))
                done(dve.tensor_tensor(tmp[:, :, :], tmp[:, :, :], per_expert(iota[:, :]), ALU.mult))
                done(dve.tensor_reduce(red[:, :], tmp[:, :, :], AX.X, ALU.min))
                done(dve.tensor_tensor(pick[k][:, :, :], per_expert(iota[:, :]), per_token(red[:, :]), ALU.is_equal))
                if k == 0:
                    done(dve.scalar_tensor_tensor(out=tmp2[:, :, :].rearrange("t b e -> t (b e)"),
                                                  in0=pick[0][:, :, :].rearrange("t b e -> t (b e)"), scalar=-4.0,
                                                  in1=p[:, :, :].rearrange("t b e -> t (b e)"),
                                                  op0=ALU.mult, op1=ALU.add))
            done(dve.tensor_tensor(tmp[:, :, :], pick[0][:, :, :], pick[1][:, :, :], ALU.add))
            done(dve.tensor_tensor(v[:, :, :], tmp[:, :, :], p[:, :, :], ALU.mult))
            assert steps == picked
            dve.wait_ge(v_turned, 1)
            done(dve.tensor_copy(vT[:, :], bank_v[:, 0:T]))
            done(dve.memset(level, 0.0))

            with dve.Fori(0, BITS // ROUND) as i:
                c = steps + 4 * i
                dve.tensor_tensor(trial[:, :], trial_bits[:, i, :], level.bitcast(I32).to_broadcast([128, TRIALS]),
                                  ALU.bitwise_or).then_inc(s, 1)
                dve.wait_ge(s, c + 1)
                dve.tensor_tensor(reached[:, :, :], over(vT[:, :], TRIALS),
                                  trial[:, :].bitcast(FP32).unsqueeze(2).to_broadcast([128, TRIALS, T]), ALU.is_ge)\
                    .then_inc(s, 1)
                dve.wait_ge(s, c + 2)
                dve.tensor_reduce(count[:, :], reached[:, :, :], AX.X, ALU.add).then_inc(counted, 1)
                dve.wait_ge(compared, i + 1)
                dve.scalar_tensor_tensor(out=passed[:, 1:1 + TRIALS], in0=bank_c[:, 0:TRIALS], scalar=CAP - 0.5,
                                         in1=trial[:, :].bitcast(FP32), op0=ALU.is_ge, op1=ALU.mult).then_inc(s, 1)
                dve.wait_ge(s, c + 3)
                dve.tensor_reduce(level, passed[:, :], AX.X, ALU.max).then_inc(s, 1)
                dve.wait_ge(s, c + 4)
            steps += 4 * (BITS // ROUND)
            done(dve.tensor_scalar(keep[:, :], vT[:, :], level, None, ALU.is_gt))
            dve.tensor_reduce(count[:, 0:1], keep[:, :], AX.X, ALU.add).then_inc(counted, 1)
            done(dve.tensor_scalar(positive[:, :], vT[:, :], 0.0, None, ALU.is_gt))
            done(dve.scalar_tensor_tensor(out=equal[:, :], in0=vT[:, :], scalar=level, in1=positive[:, :],
                                          op0=ALU.is_equal, op1=ALU.mult))
            dve.tensor_tensor_scan(upto[:, :], core.ones[:, :], equal[:, :], 0.0, ALU.mult, ALU.add)\
                .then_inc(totalled, 1)
            dve.wait_ge(compared, BITS // ROUND + 1)
            done(dve.tensor_scalar(need[:, :], bank_c[:, 0:1], -float(CAP), None, ALU.add))
            dve.wait_ge(summed, 1)
            done(dve.tensor_tensor(offset[:, :], bank_s[:, 0:1], need[:, :], ALU.add))
            done(dve.tensor_scalar(upto[:, :], upto[:, :], offset[:, :], 0.5, ALU.add, ALU.is_lt))
            done(dve.tensor_tensor(equal[:, :], equal[:, :], upto[:, :], ALU.mult))
            done(dve.tensor_tensor(keep[:, :], keep[:, :], equal[:, :], ALU.add))
            dve.tensor_tensor_scan(upto[:, :], core.ones[:, :], keep[:, :], 0.0, ALU.mult, ALU.add)\
                .then_inc(totalled, 1)
            dve.wait_ge(summed, 2)
            done(dve.tensor_tensor(offset[:, :], bank_s[:, 1:2], base[:, :], ALU.add))
            dve.scalar_tensor_tensor(out=upto[:, :], in0=upto[:, :], scalar=offset[:, :], in1=keep[:, :],
                                     op0=ALU.add, op1=ALU.mult).then_inc(totalled, 1)

            dve.wait_ge(slots_turned, 1)
            turned_slots = bank_v[:, 0:128].rearrange("t (b e) -> t b e", e=E6)
            for k, product in enumerate((tmp, tmp2)):
                done(dve.tensor_tensor(product[:, :, :], turned_slots, pick[k][:, :, :], ALU.mult))
                done(dve.tensor_reduce(slot_f[:, k, :], product[:, :, :], AX.X, ALU.add))
            done(dve.tensor_scalar(slot_i[:, :, :], slot_f[:, :, :], float(DROPPED), None, ALU.add))
            done(dve.tensor_scalar(slot_lo[:, :, :], slot_i[:, :, :], 127, None, ALU.bitwise_and))
            done(dve.tensor_copy(lo[:, :, :], slot_lo[:, :, :]))
            done(dve.tensor_scalar(slot_hi[:, :, :], slot_i[:, :, :], 7, None, ALU.logical_shift_right))
            done(dve.tensor_copy(hi[:, :, :], slot_hi[:, :, :]))
            at = at_tile[:, :, :, :].rearrange("t k b s -> t (k b) s")
            done(dve.tensor_tensor(at, over(lanes[:, 0:TILES], 2 * B),
                                   hi[:, :, :].rearrange("t k b -> t (k b)").unsqueeze(2)
                                   .to_broadcast([T, 2 * B, TILES]), ALU.is_equal))
            dve.tensor_scalar(codes[:, :, :, 0, :].rearrange("t k b s -> t (k b) s"), at, lane[:, :], None, ALU.mult)\
                .then_inc(coded, 1)
            dve.tensor_tensor(codes[:, :, :, 1, :].rearrange("t k b s -> t (k b) s"), at,
                              seq_code[:, :, :].rearrange("t k b -> t (k b)").unsqueeze(2)
                              .to_broadcast([T, 2 * B, TILES]), ALU.mult).then_inc(coded, 1)
            dve.wait_ge(lanes_made, 1)
            for k in range(2):
                dve.tensor_tensor(at_row[:, k, :, :], over(lanes_b[:, :], B),
                                  lo[:, k, :].unsqueeze(2).to_broadcast([T, B, 128]), ALU.is_equal)\
                    .then_inc(rows_marked, 1)
            dve.wait_ge(mapped, 1)
            code, token = code_sum[:, 1, :], code_sum[:, 0, :]
            done(dve.tensor_copy(code_sum[:, :, :], bank_m[:, 0:2 * TILES].rearrange("p (c s) -> p c s", c=2)))
            done(dve.tensor_scalar(empty[:, :], code, 0.0, float(2 * DROPPED), ALU.is_equal, ALU.mult))
            done(dve.scalar_tensor_tensor(out=token, in0=code, scalar=float(T), in1=token, op0=ALU.mult, op1=ALU.add))
            done(dve.tensor_scalar(token, token, -float(T), None, ALU.add))
            done(dve.tensor_tensor(dst_row[:, :], token, empty[:, :], ALU.add))
            done(dve.tensor_scalar(src_row[:, :], dst_row[:, :], B * T - 1, None, ALU.bitwise_and))


def expert_loop(core, a, out, gate, src_row, dst_row, n_rows, planes, b1, b2):
    nc = core.nc
    (w_in0, w_in1, x_in0, x_in1, turned, x_copied, up_done, silu_done, down_done, y_added, stored0, stored1,
     x_part, x_done, x_out) = core.sems(
        "mo", "w_in0 w_in1 x_in0 x_in1 turned x_copied up_done silu_done down_done y_added stored0 stored1 "
        "x_part x_done x_out")
    w_in, x_in, stored = (w_in0, w_in1), (x_in0, x_in1), (stored0, stored1)
    bank_x, bank_up, bank_y = core.bank[0], core.bank[1:3], core.bank[3:6]
    groups = B // Q
    fetched = [core.sem(f"mo_fetched{g}") for g in range(groups)]
    at = [128 * r for r in range(len(ROWS))]
    with ExitStack() as ctx:
        def sb(name, shape):
            return ctx.enter_context(nc.sbuf_tensor(name, shape, FP32))

        w1, w2 = sb("mo_w1", [D, 2, H6]), sb("mo_w2", [128, 2, CH6, D])
        rows = sb("mo_rows", [128, 2, len(ROWS), D])
        xT = sb("mo_xT", [D, CAP])
        h = sb("mo_h", [128, CH6, CAP])
        y = sb("mo_y", [128, 2, len(ROWS), D])
        got = sb("mo_got", [T, 2, B, D])
        with nc.Block() as block:
            @block.sync
            def _(sp):
                def load_weights(e, par):
                    sp.dma_start(w1[:, par, :], a["L1_ffn_W1"][bass.ds(e, 1)].rearrange("e d h -> (e d) h"))\
                        .then_inc(w_in[par], 16)
                    sp.dma_start(w2[:, par, :, :], a["L1_ffn_W2"][bass.ds(e, 1)]
                                 .rearrange("e (c p) d -> p (e c) d", p=128)).then_inc(w_in[par], 16)

                load_weights(0, 0)
                load_weights(1, 1)
                with sp.Fori(1, E6 // 2) as i:
                    for par in range(2):
                        e = 2 * i + par
                        sp.wait_ge(down_done, e - 1)
                        load_weights(e, par)
                for par in range(2):
                    sp.wait_ge(stored[par], 16 * len(ROWS) * E6 // 2)
                for g in range(groups):
                    for k in range(2):
                        sp.dma_start(got[:, k, Q * g:Q * g + Q, :],
                                     planes[(k * B + Q * g) * T:(k * B + Q * g + Q) * T, :]
                                     .rearrange("(i t) d -> t i d", i=Q)).then_inc(fetched[g], 16)
                for g in range(groups):
                    sp.wait_ge(x_done, Q * g + Q)
                    sp.dma_start(out[Q * g:Q * g + Q].rearrange("b t d -> t b d"), core.x[:, Q * g:Q * g + Q, :])\
                        .then_inc(x_out, 16)
                sp.wait_ge(x_out, 16 * groups)

            @block.gpsimd
            def _(pool):
                def gather(e):
                    for r, m in enumerate(ROWS):
                        tile = len(ROWS) * e + r
                        pool.indirect_dma_start(
                            out=rows[0:m, e % 2, r, :], out_offset=None, in_=n_rows,
                            in_offset=bass.IndirectOffsetOnAxis(ap=src_row[0:m, tile:tile + 1], axis=0))\
                            .then_inc(x_in[e % 2], 16)

                def scatter(e):
                    for r, m in enumerate(ROWS):
                        tile = len(ROWS) * e + r
                        pool.indirect_dma_start(
                            out=planes, out_offset=bass.IndirectOffsetOnAxis(ap=dst_row[0:m, tile:tile + 1], axis=0),
                            in_=y[0:m, e % 2, r, :], in_offset=None, bounds_check=2 * B * T - 1, oob_is_err=False)\
                            .then_inc(stored[e % 2], 16)

                gather(0)
                gather(1)
                for e in range(E6):
                    if e + 2 < E6:
                        pool.wait_ge(turned, e + 1)
                        gather(e + 2)
                    pool.wait_ge(y_added, e + 1)
                    scatter(e)

            @block.tensor
            def _(pe):
                def turn(e, par):
                    pe.wait_ge(x_in[par], 8 * len(ROWS) * (e + 2 - par))
                    for r, m in enumerate(ROWS):
                        mm = pe.transpose(bank_x[:, at[r]:at[r] + m], rows[0:m, par, r, :], core.ident[0:m, 0:m])
                    mm.then_inc(turned, 1)

                def up(e, par, c):
                    if c == 0:
                        pe.wait_ge(x_copied, e + 1)
                        pe.wait_ge(w_in[par], 16 * (e + 2 - par))
                    if c >= 2:
                        pe.wait_ge(silu_done, CH6 * e + c - 1)
                    pe.matmul(bank_up[c % 2][:, 0:CAP], w1[:, par, c * 128:(c + 1) * 128], xT[:, :],
                              start=True, stop=True).then_inc(up_done, 1)

                def down(e, par, c, first=False):
                    pe.wait_ge(silu_done, CH6 * e + c + 1)
                    if c == 0 and not first:
                        pe.wait_ge(y_added, e)
                    for r, m in enumerate(ROWS):
                        mm = pe.matmul(bank_y[r][0:m, 0:D], h[:, c, at[r]:at[r] + m], w2[:, par, c, :],
                                       start=(c == 0), stop=(c == CH6 - 1))
                    if c == CH6 - 1:
                        mm.then_inc(down_done, 1)

                def step(e, par, first=False, last=False):
                    up(e, par, 0)
                    up(e, par, 1)
                    down(e, par, 0, first)
                    up(e, par, 2)
                    down(e, par, 1)
                    up(e, par, 3)
                    down(e, par, 2)
                    if not last:
                        turn(e + 1, 1 - par)
                    down(e, par, 3)

                turn(0, 0)
                step(0, 0, first=True)
                with pe.Fori(0, E6 // 2 - 1) as i:
                    step(2 * i + 1, 1)
                    step(2 * i + 2, 0)
                step(E6 - 1, 1, last=True)

            @block.scalar
            def _(act):
                with act.Fori(0, E6) as e:
                    for c in range(CH6):
                        act.wait_ge(up_done, CH6 * e + c + 1)
                        act.activation(h[:, c, :], bank_up[c % 2][:, 0:CAP], ACT.Silu,
                                       bias=b1[:, e, c:c + 1]).then_inc(silu_done, 1)

            @block.vector
            def _(dve):
                def copy_x(e):
                    dve.wait_ge(turned, e + 1)
                    dve.tensor_copy(xT[:, :], bank_x[:, 0:CAP]).then_inc(x_copied, 1)

                def add_bias(e, par, first=False):
                    dve.wait_ge(down_done, e + 1)
                    if not first:
                        dve.wait_ge(stored[par], 8 * len(ROWS) * (e - par))
                    for r, m in enumerate(ROWS):
                        ins = dve.tensor_tensor(y[0:m, par, r, :], bank_y[r][0:m, 0:D], b2[0:m, e, :], ALU.add)
                    ins.then_inc(y_added, 1)

                copy_x(0)
                copy_x(1)
                add_bias(0, 0, first=True)
                copy_x(2)
                add_bias(1, 1, first=True)
                with dve.Fori(1, E6 // 2 - 1) as i:
                    copy_x(2 * i + 1)
                    add_bias(2 * i, 0)
                    copy_x(2 * i + 2)
                    add_bias(2 * i + 1, 1)
                copy_x(E6 - 1)
                add_bias(E6 - 2, 0)
                add_bias(E6 - 1, 1)
                for g in range(groups):
                    dve.wait_ge(fetched[g], 32)
                    for k, signal in enumerate((x_part, x_done)):
                        for i in range(Q):
                            b = Q * g + i
                            if k == 1:
                                dve.wait_ge(x_part, b + 1)
                            dve.scalar_tensor_tensor(out=core.x[:, b, :], in0=got[:, k, b, :],
                                                     scalar=gate[k][:, b:b + 1], in1=core.x[:, b, :],
                                                     op0=ALU.mult, op1=ALU.add).then_inc(signal, 1)
def decoder(nc, a, out):
    with ExitStack() as ctx:
        core = Core(nc, ctx)
        lin = LinMem(core)
        with ExitStack() as part:
            f = FoldMem(core, part)
            m = AttnMem(core, part)
            setup(core, m, f, lin, a)
            softmax_attention(core, m, f, 0)
            softmax_attention(core, m, f, 1)
        core.free_semaphores()
        feed_forward(core, f)
        linear_attention(core, lin)
        autocorrelation(core, a)
        experts(core, a, out)


def _constants():
    p = np.arange(128)
    c = {"c_ident": np.eye(128, dtype=np.float32)}
    for name, pick in (("c_mask_j", p // DH % J), ("c_mask_g", p // (DH * J))):
        c[name] = np.repeat(pick[:, None] == np.arange(J), T, axis=1).astype(np.float32)
    gap = p[None, :] - p[:, None]
    c["c_gap"] = np.maximum(gap, 0).astype(np.float32)
    c["c_tri"] = (gap >= 0).astype(np.float32)
    angle = 2 * np.pi * (p[:, None] * p[None, :] % T) / T
    cos, sin = np.cos(angle), np.sin(angle)
    c["c_dft"] = np.concatenate([cos, sin, cos + sin, cos - sin], axis=1).astype(np.float32)
    c["c_iota"] = np.tile(p.astype(np.float32), (128, 1))
    c["c_expert"] = (np.arange(E6) - E6).astype(np.float32)
    row = p % E6
    c["c_base"] = (row * len(ROWS) * 128 - DROPPED - 1).astype(np.float32)[:, None]
    same = row[:, None] == row[None, :]
    c["c_same"] = same.astype(np.float32)
    c["c_earlier"] = (same & (gap > 0)).astype(np.float32)
    c["c_lane"] = p.astype(np.float32)[:, None]
    c["c_seq_code"] = np.arange(1, 2 * B + 1).astype(np.float32)
    low = BITS - ROUND * np.arange(1, BITS // ROUND + 1)
    c["c_trial_bits"] = (np.arange(1, TRIALS + 1)[None, :] << low[:, None]).astype(np.int32).reshape(-1)
    return c


def _butterfly_stages(w, forward):
    pair = np.arange(H3 // 2)
    out = []
    for n in range(STAGES):
        stage = n if forward else STAGES - 1 - n
        index = 2 * pair if forward else pair
        for _ in range(n):
            index = (index * 2 % H3 + index * 2 // H3) if forward else (index // 2 + index % 2 * (H3 // 2))
        low = (1 << stage) - 1
        number = (index & low) | ((index >> (stage + 1)) << stage)
        factors = w[stage][number]
        out.append(factors.transpose(1, 0, 2) if forward else factors.transpose(2, 1, 0))
    return np.ascontiguousarray(np.stack(out).reshape(-1))


def kernel(**inputs):
    import concourse.bacc as _bacc
    from concourse.bass_utils import run_bass_kernel_spmd as _run

    arrays = {k: np.ascontiguousarray(v) for k, v in inputs.items() if k != "L0_attn_mask"}
    arrays["ctxT"] = np.ascontiguousarray(inputs["ctx_1024"].transpose(0, 2, 1))
    arrays["L0_xattn_w_outT"] = np.ascontiguousarray(inputs["L0_xattn_w_out"].T)
    for name, w, forward in (("up_stages", "L0_ffn_up_weights", True), ("down_stages", "L0_ffn_down_weights", False)):
        arrays[name] = _butterfly_stages(inputs[w], forward)
    arrays["W_conT"] = np.ascontiguousarray(inputs["L0_ffn_W_con"].T)
    arrays["up_bias_col"] = np.ascontiguousarray(inputs["L0_ffn_up_bias"].reshape(CH, 128).T)
    for name, w in (("lin_WqT", "L1_attn_W_Q"), ("lin_WkT", "L1_attn_W_K"), ("lin_WvT", "L1_attn_W_V"),
                    ("lin_WgT", "L1_attn_W_g_w"), ("lin_WoT", "L1_attn_W_O")):
        arrays[name] = np.ascontiguousarray(inputs[w].T)
    for name, w in (("auto_WqT", "L1_xattn_Wq"), ("auto_WkT", "L1_xattn_Wk"), ("auto_WvT", "L1_xattn_Wv"),
                    ("auto_WoT", "L1_xattn_Wo")):
        arrays[name] = np.ascontiguousarray(inputs[w].T)
    arrays["moe_b1_col"] = np.ascontiguousarray(
        inputs["L1_ffn_b1"].reshape(E6, CH6, 128).transpose(2, 0, 1).reshape(128, E6 * CH6))
    arrays["gate_bias_col"] = np.ascontiguousarray(inputs["L1_attn_W_g_b"].reshape(C4, 128).T)
    arrays.update(_constants())
    nc = _bacc.Bacc("TRN2", target_bir_lowering=False, num_devices=1)
    args = {k: nc.dram_tensor("in_" + k, v.shape, mybir.dt.from_np(v.dtype), kind="ExternalInput").ap()
            for k, v in arrays.items()}
    out = nc.dram_tensor("out_0", (B, T, D), FP32, kind="ExternalOutput").ap()
    decoder(nc, args, out)
    r = _run(nc, [{"in_" + k: v for k, v in arrays.items()}], core_ids=[0])
    return r.results[0]["out_0"]
```

```python
import numpy as np
from contextlib import ExitStack

import concourse.bass as bass
from concourse import mybir

FP32 = mybir.dt.float32
BF16 = mybir.dt.bfloat16
I32 = mybir.dt.int32
U32 = mybir.dt.uint32
ALU = mybir.AluOpType
ACT = mybir.ActivationFunctionType
AX = mybir.AxisListType

B = 16
T = 128
D = 128
EPS = 1e-5
G, J = 4, 4
DH = D // (G * J)
EARLY, LATE = slice(0, 12), slice(12, B)


class Core:

    def __init__(self, nc, ctx):
        self.nc, self.ctx = nc, ctx
        self.x = self.sb("x", [T, B, D])
        self.stats = self.sb("stats", [T, B, 6])
        self.mean = self.sb("mean", [T, B, 1])
        self.rstd = self.sb("rstd", [T, B, 1])
        self.dev = self.sb("dev", [T, B])
        self.var = self.sb("var", [T, B])
        self.eps = self.sb("eps", [T, B])
        self.neg_half = self.sb("neg_half", [T, B])
        self.ident = self.sb("ident", [128, 128])
        self.ident_b = self.sb("ident_b", [128, 128], BF16)
        self.ones = self.sb("ones", [128, 128])
        self.bank = [ctx.enter_context(nc.psum_tensor(f"bank{i}", [128, 512], FP32)) for i in range(8)]
        self.layer_sems = []

    def sb(self, name, shape, dt=FP32):
        return self.ctx.enter_context(self.nc.sbuf_tensor(name, shape, dt))

    def sem(self, name):
        self.layer_sems.append(self.nc.alloc_semaphore(name))
        return self.layer_sems[-1]

    def sems(self, layer, names):
        return [self.sem(f"{layer}_{n}") for n in names.split()]

    def keep_sem(self, name):
        return self.nc.alloc_semaphore(name)

    def free_semaphores(self):
        self.nc.clear_and_free_semaphores(self.layer_sems)
        self.layer_sems = []
        self.nc.all_engine_barrier()


def over(ap, n):
    p, m = ap.shape
    return ap.unsqueeze(1).to_broadcast([p, n, m])


def setup(core, m, f, lin, a):
    nc = core.nc
    x_in0, x_in1, x_in2, x_in3, loaded, decay_in, made, zeroed, stat, decay_ready, raised, s_var, s_rstd = core.sems(
        "setup", "x_in0 x_in1 x_in2 x_in3 loaded decay_in made zeroed stat decay_ready raised var rstd")
    x_in = (x_in0, x_in1, x_in2, x_in3)
    with nc.Block() as block:
        @block.sync
        def _(sp):
            for h in range(4):
                sp.dma_start(core.x[:, 4 * h:4 * h + 4, :],
                             a["x"][4 * h:4 * h + 4].rearrange("b t d -> t b d")).then_inc(x_in[h], 16)
            for dst, src in ((core.ident, "c_ident"), (m.wq, "L0_attn_Wq"), (m.wk, "L0_attn_Wk"),
                             (m.wv, "L0_attn_Wv"), (m.w_out[0], "L0_attn_Wout")):
                sp.dma_start(dst[:, :], a[src]).then_inc(loaded, 16)
            for dst, src in ((m.mask_j, "c_mask_j"), (m.mask_g, "c_mask_g")):
                sp.dma_start(dst[:, :, :], a[src].rearrange("p (j t) -> p j t", j=J)).then_inc(loaded, 16)
            sp.dma_start(f.up[:, :], a["L0_ffn_W_exp"]).then_inc(f.up_loaded, 16)
            sp.dma_start(f.bias[:, :], a["L0_ffn_b_exp"].unsqueeze(0)).then_inc(f.up_loaded, 16)
            sp.dma_start(f.w_up[:, :, :, :].rearrange("p s o n -> p (s o n)"),
                         a["up_stages"].partition_broadcast(D)).then_inc(f.up_loaded, 16)
            sp.dma_start(m.w_out[1][:, :], a["L0_xattn_w_outT"]).then_inc(m.cross_loaded, 16)
            sp.dma_start(m.bias[:, :], a["L0_xattn_b_out"].partition_broadcast(T)).then_inc(m.cross_loaded, 16)
            sp.dma_start(m.ctx[:, :, :], a["ctx_1024"].rearrange("b t d -> t b d")).then_inc(m.cross_loaded, 16)
            sp.dma_start(m.ctxT[:, :, :], a["ctxT"].rearrange("b d t -> d b t")).then_inc(m.cross_loaded, 16)
            sp.dma_start(f.down_w[:, :], a["W_conT"]).then_inc(f.down_loaded, 16)
            sp.dma_start(f.w_down[:, :, :, :].rearrange("p s o n -> p (s o n)"),
                         a["down_stages"].partition_broadcast(D)).then_inc(f.down_loaded, 16)
            sp.dma_start(f.up_bias[:, :], a["up_bias_col"]).then_inc(f.bias_loaded, 16)
            for i, src in enumerate(("L0_ffn_b_con", "L0_ffn_down_bias")):
                sp.dma_start(f.out_bias[:, i, :], a[src].partition_broadcast(T)).then_inc(f.bias_loaded, 16)
            for dst, src in ((lin.wq, "lin_WqT"), (lin.wk, "lin_WkT"), (lin.wv, "lin_WvT"), (lin.wg, "lin_WgT")):
                sp.dma_start(dst[:, :], a[src]).then_inc(lin.loaded, 16)
            sp.dma_start(lin.wo[:, :, :], a["lin_WoT"].rearrange("(c p) e -> p c e", p=128)).then_inc(lin.loaded, 16)

        @block.gpsimd
        def _(pool):
            pool.memset(core.ones[:, :], 1.0).then_inc(made, 1)
            pool.memset(core.eps[:, :], EPS).then_inc(made, 1)
            pool.memset(core.neg_half[:, :], -0.5).then_inc(made, 1)
            pool.wait_ge(loaded, 112)
            pool.tensor_copy(core.ident_b[:, :], core.ident[:, :]).then_inc(made, 1)
            pool.wait_ge(made, 4)
            inverse_deviation(core, pool, EARLY, s_var, s_rstd)
            pool.wait_ge(s_rstd, 2)

        @block.scalar
        def _(act):
            for dst, src in ((lin.decay, a["L1_attn_decay_log"].partition_broadcast(T)), (lin.gap, a["c_gap"]),
                             (lin.tri, a["c_tri"]), (lin.gate_bias, a["gate_bias_col"])):
                act.dma_start(dst[:, :], src).then_inc(decay_in, 16)
            act.wait_ge(decay_ready, 1)
            act.activation(lin.decay[:, :], lin.decay[:, :], ACT.Exp, scale=-1.0).then_inc(raised, 1)
            act.wait_ge(raised, 1)
            act.activation(lin.decay[:, :], lin.decay[:, :], ACT.Ln, bias=1.0).then_inc(raised, 1)
            act.wait_ge(decay_ready, 3)
            for h in range(H4):
                act.activation(lin.mask[:, h, :], lin.gap[:, :], ACT.Exp, scale=lin.decay[:, h:h + 1])\
                    .then_inc(raised, 1)

        @block.vector
        def _(dve):
            def take_stats(h):
                dve.wait_ge(x_in[h], 16)
                for b in range(4 * h, 4 * h + 4):
                    dve.bn_stats(core.stats[:, b, :], core.x[:, b, :]).then_inc(stat, 1)

            dve.memset(m.v[:, :, :, :], 0.0).then_inc(zeroed, 1)
            dve.wait_ge(zeroed, 1)
            dve.memset(m.v[:, :, :, DH:DH + 1], 1.0).then_inc(zeroed, 1)
            dve.wait_ge(decay_in, 64)
            dve.tensor_scalar(lin.decay[:, :], lin.decay[:, :], -80.0, None, ALU.max).then_inc(decay_ready, 1)
            dve.tensor_scalar(lin.gate_bias[:, :], lin.gate_bias[:, :], 0.5, None, ALU.mult).then_inc(decay_ready, 1)
            take_stats(0)
            dve.wait_ge(raised, 2)
            dve.tensor_scalar(lin.decay[:, :], lin.decay[:, :], -1.0, None, ALU.mult).then_inc(decay_ready, 1)
            for h in range(1, 4):
                take_stats(h)
            dve.wait_ge(stat, EARLY.stop)
            variance(core, dve, EARLY, s_var)
            dve.wait_ge(raised, 2 + H4)
            dve.tensor_tensor(lin.mask[:, :, :], lin.mask[:, :, :], over(lin.tri[:, :], H4), ALU.mult)\
                .then_inc(decay_ready, 1)
            dve.wait_ge(decay_ready, 4)
            dve.wait_ge(stat, B)
            dve.wait_ge(zeroed, 2)


def variance(core, dve, seqs, s_var):
    st, mean, dev, var = core.stats[:, seqs, :], core.mean[:, seqs, 0], core.dev[:, seqs], core.var[:, seqs]
    dve.tensor_tensor(mean, st[:, :, 1], st[:, :, 4], ALU.add).then_inc(s_var, 1)
    dve.tensor_tensor(dev, st[:, :, 1], st[:, :, 4], ALU.subtract).then_inc(s_var, 1)
    dve.tensor_tensor(var, st[:, :, 2], st[:, :, 5], ALU.add).then_inc(s_var, 1)
    dve.wait_ge(s_var, 3)
    dve.tensor_scalar(mean, mean, 0.5, None, ALU.mult).then_inc(s_var, 1)
    dve.scalar_tensor_tensor(out=dev, in0=dev, scalar=0.25, in1=dev, op0=ALU.mult, op1=ALU.mult).then_inc(s_var, 1)
    dve.wait_ge(s_var, 5)
    dve.scalar_tensor_tensor(out=var, in0=var, scalar=1.0 / D, in1=dev, op0=ALU.mult, op1=ALU.add)\
        .then_inc(s_var, 1)


def inverse_deviation(core, pool, seqs, s_var, s_rstd):
    pool.wait_ge(s_var, 6)
    pool.tensor_tensor(core.var[:, seqs], core.var[:, seqs], core.eps[:, seqs], ALU.add).then_inc(s_rstd, 1)
    pool.wait_ge(s_rstd, 1)
    pool.tensor_tensor(core.rstd[:, seqs, 0], core.var[:, seqs], core.neg_half[:, seqs], ALU.pow)\
        .then_inc(s_rstd, 1)


def normalise(core, dve, dst, b):
    return dve.tensor_scalar(dst, core.x[:, b, :], core.mean[:, b, :], core.rstd[:, b, :],
                             ALU.subtract, ALU.mult)


class AttnMem:

    def __init__(self, core, part):
        def sb(name, shape, dt=FP32):
            return part.enter_context(core.nc.sbuf_tensor(name, shape, dt))

        self.n = sb("at_n", [T, 2, D])
        self.nT = sb("at_nT", [D, T])
        self.qT = sb("at_qT", [D, T])
        self.kT = sb("at_kT", [D, T])
        self.q_j = sb("at_q_j", [D, 2, J, T])
        self.k_g = sb("at_k_g", [D, 2, G, T])
        self.q_gb = sb("at_q_gb", [D, G, T], BF16)
        self.k_jb = sb("at_k_jb", [D, J, T], BF16)
        self.v = sb("at_v", [T, 2, G * J, 32])
        self.nmax = sb("at_nmax", [T, G * J], BF16)
        self.p = sb("at_p", [T, G, J, T])
        self.o_raw = sb("at_o_raw", [128, G, T])
        self.rden = sb("at_rden", [T, G, J])
        self.o = sb("at_o", [T, G * J, DH])
        self.oT = sb("at_oT", [D, T])
        self.mask_j = sb("at_mask_j", [D, J, T])
        self.mask_g = sb("at_mask_g", [D, G, T])
        self.w_out = [sb(f"at_w_out{i}", [D, D]) for i in range(2)]
        self.wq, self.wk, self.wv = (sb(f"at_{w}", [D, D]) for w in ("wq", "wk", "wv"))
        self.ctx = sb("ctx", [T, B, D])
        self.ctxT = sb("ctxT", [D, B, T])
        self.bias = sb("at_bias", [T, D])
        self.cross_loaded = core.sem("at_cross_loaded")


def softmax_attention(core, m, f, layer):
    nc = core.nc
    cross = layer == 1
    (s_var, s_rstd, stat, next_var, next_rstd, normed, n_turned, n_copied, projected, qk_copied, v_copied,
     masked, k_masked, res_made, scored, maxed, shifted, exped, pv_done, raw_copied, raw_turned, rden_done,
     o_done, o_turned, o_copied, out_done, x_done) = core.sems(
        f"at{layer}",
        "var rstd stat next_var next_rstd normed n_turned n_copied projected qk_copied v_copied masked "
        "k_masked res_made scored maxed shifted exped pv_done raw_copied raw_turned rden_done o_done "
        "o_turned o_copied out_done x_done")
    bank_st, bank_s = core.bank[0:2], core.bank[2:4]
    bank_p, bank_v, bank_d, bank_z = core.bank[4:8]
    qk_copies = 1 if cross else 2
    scale = float(DH) ** -0.5
    LAST = B - 1
    PAIRS = (B - 2) // 2

    with nc.Block() as block:
        @block.vector
        def _(dve):
            def prepare(b, par, reused=True):
                if reused:
                    dve.wait_ge(res_made, b - 1)
                normalise(core, dve, m.n[:, par, :], b).then_inc(normed, 1)

            def maximum(b, g):
                dve.wait_ge(scored, G * b + g + 1)
                dve.tensor_reduce(m.nmax[:, J * g:J * g + J],
                                  bank_s[g % 2][:, :].rearrange("p (j t) -> p j t", j=J),
                                  AX.X, ALU.max, negate=True).then_inc(maxed, 1)

            def divide(b):
                raw = bank_d[:, :].rearrange("p (h w) -> p h w", w=32)
                dve.wait_ge(raw_turned, b + 1)
                dve.reciprocal(m.rden[:, :, :], raw[:, :, DH].rearrange("p (g j) -> p g j", g=G))\
                    .then_inc(rden_done, 1)
                dve.wait_ge(rden_done, b + 1)
                dve.tensor_tensor(m.o[:, :, :], raw[:, :, 0:DH],
                                  m.rden[:, :, :].rearrange("p g j -> p (g j)").unsqueeze(2)
                                  .to_broadcast([T, G * J, DH]), ALU.mult).then_inc(o_done, 1)

            def finish(b):
                dve.wait_ge(out_done, b + 1)
                dve.wait_ge(res_made, b + 1)
                dve.tensor_tensor(core.x[:, b, :], bank_z[:, 0:D], core.x[:, b, :], ALU.add)\
                    .then_inc(x_done, 1)
                dve.wait_ge(x_done, b + 1)
                dve.bn_stats(core.stats[:, b, :], core.x[:, b, :]).then_inc(stat, 1)

            def mask_k(b):
                dve.wait_ge(qk_copied, qk_copies * (b + 1))
                dve.tensor_tensor(m.k_jb[:, :, :], over(m.ctxT[:, b, :] if cross else m.kT[:, :], J),
                                  m.mask_j[:, :, :], ALU.mult).then_inc(k_masked, 1)

            def products(stage):
                if not cross and stage is not None:
                    fold_products(dve, stage, f.w_up, f.up, f.part_up, f.up_done)

            def sums(stage):
                if not cross and stage is not None:
                    fold_sums(dve, stage, f.up, f.part_up, f.up_done, forward=True)

            def step(b, par, first=False, last=False, stage=None):
                if not first:
                    divide(b - 1)
                products(stage)
                mask_k(b + 1)
                sums(stage)
                if not first:
                    finish(b - 1)
                if not last:
                    prepare(b + 2, par)
                for g in range(G):
                    maximum(b + 1, g)

            if cross:
                dve.wait_ge(m.cross_loaded, 64)
            prepare(0, 0, reused=False)
            variance(core, dve, LATE, s_var)
            prepare(1, 1, reused=False)
            mask_k(0)
            for g in range(G):
                maximum(0, g)
            dve.wait_ge(s_rstd, 2)
            if not cross:
                dve.wait_ge(f.up_loaded, 48)
            step(0, 0, first=True, stage=0)
            with dve.Fori(0, PAIRS - 1) as i:
                step(2 * i + 1, 1)
                step(2 * i + 2, 0, stage=i + 1)
            step(LAST - 2, 1)
            step(LAST - 1, 0, last=True, stage=PAIRS)
            variance(core, dve, EARLY, next_var)
            for b, stage in ((LAST - 1, STAGES - 1), (LAST, None)):
                divide(b)
                products(stage)
                sums(stage)
                finish(b)
            dve.wait_ge(stat, B)

        @block.gpsimd
        def _(pool):
            def prepare(b, par):
                pool.wait_ge(normed, b + 1)
                pool.tensor_tensor(core.x[:, b, :], core.x[:, b, :],
                                   m.bias[:, :] if cross else m.n[:, par, :], ALU.add).then_inc(res_made, 1)
                pool.wait_ge(qk_copied, qk_copies * (b + 1))
                kT = m.ctxT[:, b, :] if cross else m.kT[:, :]
                for dst, src, mask in ((m.q_gb[:, :, :], m.qT[:, :], m.mask_g),
                                       (m.k_g[:, par, :, :], kT, m.mask_g),
                                       (m.q_j[:, par, :, :], m.qT[:, :], m.mask_j)):
                    pool.tensor_tensor(dst, over(src, G), mask[:, :, :], ALU.mult).then_inc(masked, 1)

            def fold(stage):
                if cross:
                    fold_products(pool, stage, f.w_down, f.down_w, f.part_down, f.down_done)
                    fold_sums(pool, stage, f.down_w, f.part_down, f.down_done, forward=False)
                else:
                    fold_products(pool, stage, f.w_up[0:1], f.bias, f.part_bias, f.bias_done)
                    fold_sums(pool, stage, f.bias, f.part_bias, f.bias_done, forward=True)

            inverse_deviation(core, pool, LATE, s_var, s_rstd)
            if cross:
                pool.wait_ge(m.cross_loaded, 64)
            prepare(0, 0)
            prepare(1, 1)
            if cross:
                pool.wait_ge(f.down_loaded, 32)
            else:
                pool.wait_ge(f.up_loaded, 48)
            fold(0)
            with pool.Fori(0, PAIRS) as i:
                prepare(2 * i + 2, 0)
                prepare(2 * i + 3, 1)
                fold(i + 1)
            fold(STAGES - 1)
            inverse_deviation(core, pool, EARLY, next_var, next_rstd)
            pool.wait_ge(next_rstd, 2)
            if cross:
                pool.wait_ge(f.bias_loaded, 48)
                pool.tensor_tensor(f.out_bias[:, 0, :], f.out_bias[:, 0, :], f.out_bias[:, 1, :], ALU.add)\
                    .then_inc(f.bias_done, 1)
                pool.wait_ge(f.bias_done, 2 * STAGES + 1)

        @block.scalar
        def _(act):
            def copy_n(b):
                act.wait_ge(n_turned, b + 1)
                dst = m.qT if cross else m.nT
                act.activation(dst[:, :], bank_p[:, 0:T], ACT.Copy)\
                    .then_inc(qk_copied if cross else n_copied, 1)

            def copy_qkv(b, par):
                v_dst = m.v[:, par, :, 0:DH]
                if cross:
                    act.activation(v_dst, m.ctx[:, b, :].rearrange("p (h d) -> p h d", d=DH), ACT.Copy)\
                        .then_inc(v_copied, 1)
                    return
                act.wait_ge(projected, b + 1)
                act.activation(m.qT[:, :], bank_p[:, T:2 * T], ACT.Copy).then_inc(qk_copied, 1)
                act.activation(m.kT[:, :], bank_p[:, 2 * T:3 * T], ACT.Copy).then_inc(qk_copied, 1)
                act.activation(v_dst, bank_p[:, 3 * T:3 * T + D].rearrange("p (h d) -> p h d", d=DH), ACT.Copy)\
                    .then_inc(v_copied, 1)

            def exps(b, g):
                act.wait_ge(shifted, G * b + g + 1)
                act.activation(m.p[:, g, :, :], bank_st[g % 2][:, :].rearrange("p (j t) -> p j t", j=J),
                               ACT.Exp, scale=scale).then_inc(exped, 1)

            def copy_raw(b):
                act.wait_ge(pv_done, b + 1)
                act.activation(m.o_raw[:, :, :], bank_v[:, :].rearrange("p (g t) -> p g t", g=G), ACT.Copy)\
                    .then_inc(raw_copied, 1)

            def copy_o(b):
                act.wait_ge(o_turned, b + 1)
                act.activation(m.oT[:, :], bank_z[:, D:D + T], ACT.Copy).then_inc(o_copied, 1)

            def step(b, par, first=False, last=False):
                if not first:
                    copy_raw(b - 1)
                exps(b, 0)
                if not last:
                    copy_n(b + 1)
                exps(b, 1)
                if not last:
                    copy_qkv(b + 1, 1 - par)
                if not first:
                    copy_o(b - 1)
                exps(b, 2)
                exps(b, 3)

            if cross:
                act.wait_ge(m.cross_loaded, 64)
            copy_n(0)
            copy_qkv(0, 0)
            step(0, 0, first=True)
            with act.Fori(0, PAIRS) as i:
                step(2 * i + 1, 1)
                step(2 * i + 2, 0)
            step(LAST, 1, last=True)
            copy_raw(LAST)
            copy_o(LAST)

        @block.tensor
        def _(pe):
            def turn(b, par):
                pe.wait_ge(normed, b + 1)
                pe.transpose(bank_p[:, 0:T], m.n[:, par, :], core.ident[:, :]).then_inc(n_turned, 1)

            def project(b):
                if cross:
                    return
                pe.wait_ge(n_copied, b + 1)
                pe.matmul(bank_p[:, T:2 * T], m.wq[:, :], m.nT[:, :], start=True, stop=True)
                pe.matmul(bank_p[:, 2 * T:3 * T], m.wk[:, :], m.nT[:, :], start=True, stop=True)
                pe.matmul(bank_p[:, 3 * T:3 * T + D], m.nT[:, :], m.wv[:, :], start=True, stop=True)\
                    .then_inc(projected, 1)

            def scores(b, g):
                if g == 0:
                    pe.wait_ge(masked, 3 * b + 1)
                    pe.wait_ge(k_masked, b + 1)
                if g >= 2:
                    pe.wait_ge(maxed, G * b + g - 1)
                pe.matmul(bank_s[g % 2][:, :], m.q_gb[:, g, :],
                          m.k_jb[:, :, :].rearrange("p j t -> p (j t)"), start=True, stop=True)\
                    .then_inc(scored, 1)

            def shifted_scores(b, par, g):
                if g == 0:
                    pe.wait_ge(masked, 3 * b + 3)
                if g >= 2:
                    pe.wait_ge(exped, G * b + g - 1)
                pe.wait_ge(maxed, G * b + g + 1)
                for j in range(J):
                    h = J * g + j
                    pe.matmul(bank_st[g % 2][:, j * T:(j + 1) * T],
                              m.nmax[:, h:h + 1].to_broadcast([T, T]), core.ident_b[:, :],
                              start=(j == 0), stop=False, skip_group_check=True)
                pe.matmul(bank_st[g % 2][:, :], m.k_g[:, par, g, :],
                          m.q_j[:, par, :, :].rearrange("p j t -> p (j t)"), start=False, stop=True,
                          skip_group_check=True).then_inc(shifted, 1)

            def values(b, par):
                pe.wait_ge(v_copied, b + 1)
                pe.wait_ge(exped, G * b + G - 1)
                for g in range(G):
                    if g == G - 1:
                        pe.wait_ge(exped, G * (b + 1))
                    for j in range(J):
                        mm = pe.matmul(bank_v[32 * j:32 * j + 32, g * T:(g + 1) * T],
                                       m.v[:, par, J * g + j, :], m.p[:, g, j, :], start=True, stop=True)
                mm.then_inc(pv_done, 1)

            def turn_raw(b):
                pe.wait_ge(raw_copied, b + 1)
                for g in range(G):
                    mm = pe.transpose(bank_d[:, g * T:(g + 1) * T], m.o_raw[:, g, :], core.ident[:, :])
                mm.then_inc(raw_turned, 1)

            def turn_o(b):
                pe.wait_ge(o_done, b + 1)
                pe.transpose(bank_z[:, D:D + T], m.o[:, :, :].rearrange("p h d -> p (h d)"), core.ident[:, :])\
                    .then_inc(o_turned, 1)

            def out(b):
                pe.wait_ge(o_copied, b + 1)
                pe.matmul(bank_z[:, 0:D], m.oT[:, :], m.w_out[layer][:, :], start=True, stop=True)\
                    .then_inc(out_done, 1)

            def step(b, par, first=False, last=False):
                shifted_scores(b, par, 0)
                if not last:
                    pe.wait_ge(v_copied, b + 1)
                    turn(b + 1, 1 - par)
                if not first:
                    turn_raw(b - 1)
                shifted_scores(b, par, 1)
                if not last:
                    project(b + 1)
                if not first:
                    turn_o(b - 1)
                shifted_scores(b, par, 2)
                if not first:
                    out(b - 1)
                shifted_scores(b, par, 3)
                if not last:
                    scores(b + 1, 0)
                    scores(b + 1, 1)
                values(b, par)
                if not last:
                    scores(b + 1, 2)
                    scores(b + 1, 3)

            turn(0, 0)
            project(0)
            for g in range(G):
                scores(0, g)
            step(0, 0, first=True)
            with pe.Fori(0, PAIRS) as i:
                step(2 * i + 1, 1)
                step(2 * i + 2, 0)
            step(LAST, 1, last=True)
            turn_raw(LAST)
            turn_o(LAST)
            out(LAST)


H3 = 512
CH = H3 // 128
STAGES = 9
Q = 4


class FoldMem:

    def __init__(self, core, part):
        sb = core.sb

        def sb_part(name, shape):
            return part.enter_context(core.nc.sbuf_tensor(name, shape, FP32))

        self.up = sb("fo_up", [D, H3])
        self.bias = sb("fo_bias", [1, H3])
        self.down_w = sb("fo_down_w", [D, H3])
        self.up_bias = sb("fo_up_bias", [128, CH])
        self.bias_col = sb("fo_bias_col", [128, CH])
        self.down = sb("fo_down", [128, CH, D])
        self.out_bias = sb("fo_out_bias", [T, 2, D])
        self.w_up = sb_part("fo_w_up", [D, STAGES, 2, H3])
        self.w_down = sb_part("fo_w_down", [D, STAGES, 2, H3])
        self.part_up, self.part_down = sb_part("fo_part_up", [D, 2, H3]), sb_part("fo_part_down", [D, 2, H3])
        self.part_bias = sb_part("fo_part_bias", [1, 2, H3])
        self.up_loaded, self.down_loaded, self.bias_loaded, self.up_done, self.down_done, self.bias_done = core.sems(
            "fo", "up_loaded down_loaded bias_loaded up_done down_done bias_done")


def fold_products(eng, stage, w, row, part, done):
    if not (isinstance(stage, int) and stage == 0):
        eng.wait_ge(done, 2 * stage)
    eng.tensor_tensor(part[:, :, :], w[:, stage, :, :], over(row[:, :], 2), ALU.mult).then_inc(done, 1)


def fold_sums(eng, stage, row, part, done, forward):
    eng.wait_ge(done, 2 * stage + 1)
    if forward:
        dst = row[:, :].rearrange("p (o k) -> p o k", o=2)
        a, b = (part[:, :, :].rearrange("p o (k i) -> p o k i", i=2)[:, :, :, i] for i in range(2))
    else:
        dst = row[:, :].rearrange("p (k o) -> p o k", o=2)
        a, b = (part[:, :, :].rearrange("p o (i k) -> p o i k", i=2)[:, :, i, :] for i in range(2))
    eng.tensor_tensor(dst, a, b, ALU.add).then_inc(done, 1)


def feed_forward(core, f):
    nc = core.nc
    (folded_turned, folded_copied, s_var, s_rstd, stat, next_var, next_rstd, normed, turned, n_copied, biased,
     up_done, gelu_done, down_done, x_done) = core.sems(
        "ff",
        "folded_turned folded_copied var rstd stat next_var next_rstd normed turned n_copied biased "
        "up_done gelu_done down_done x_done")
    bank_n, bank_up, bank_down, bank_fold = core.bank[0], core.bank[1:3], core.bank[3:7], core.bank[7]
    groups = B // Q
    with ExitStack() as ctx:
        def sb(name, shape):
            return ctx.enter_context(nc.sbuf_tensor(name, shape, FP32))

        n = sb("ff_n", [T, Q, D])
        nT = sb("ff_nT", [D, Q * T])
        h = sb("ff_h", [128, CH, Q * T])
        w_up = f.up
        with nc.Block() as block:
            @block.vector
            def _(dve):
                def prepare(q):
                    for i in range(Q):
                        normalise(core, dve, n[:, i, :], Q * q + i).then_inc(normed, 1)
                    dve.wait_ge(turned, q + 1)
                    dve.tensor_copy(nT[:, :], bank_n[:, :]).then_inc(n_copied, 1)

                def finish(q):
                    dve.wait_ge(down_done, q + 1)
                    dve.wait_ge(biased, Q * (q + 1))
                    for i in range(Q):
                        dve.tensor_tensor(core.x[:, Q * q + i, :], bank_down[i][:, 0:D], core.x[:, Q * q + i, :],
                                          ALU.add).then_inc(x_done, 1)
                    for i in range(Q):
                        dve.wait_ge(x_done, Q * q + i + 1)
                        dve.bn_stats(core.stats[:, Q * q + i, :], core.x[:, Q * q + i, :]).then_inc(stat, 1)

                prepare(0)
                dve.wait_ge(folded_turned, 1)
                dve.tensor_tensor(f.bias_col[:, :], bank_down[0][:, 0:CH], f.up_bias[:, :], ALU.add)\
                    .then_inc(folded_copied, 1)
                variance(core, dve, LATE, s_var)
                dve.wait_ge(s_rstd, 2)
                with dve.Fori(0, groups - 1) as q:
                    prepare(q + 1)
                    finish(q)
                dve.wait_ge(stat, EARLY.stop)
                variance(core, dve, EARLY, next_var)
                finish(groups - 1)
                dve.wait_ge(stat, B)

            @block.gpsimd
            def _(pool):
                inverse_deviation(core, pool, LATE, s_var, s_rstd)
                with pool.Fori(0, B) as b:
                    pool.wait_ge(normed, b + 1)
                    pool.tensor_tensor(core.x[:, b, :], core.x[:, b, :], f.out_bias[:, 0, :], ALU.add)\
                        .then_inc(biased, 1)
                inverse_deviation(core, pool, EARLY, next_var, next_rstd)
                pool.wait_ge(next_rstd, 2)

            @block.scalar
            def _(act):
                act.wait_ge(folded_turned, 2)
                act.activation(f.down[:, :, :], bank_fold[:, :].rearrange("p (c d) -> p c d", c=CH), ACT.Copy)\
                    .then_inc(folded_copied, 1)
                act.wait_ge(folded_copied, 2)

                def gelu(q):
                    for c in range(CH):
                        act.wait_ge(up_done, CH * q + c + 1)
                        act.activation(h[:, c, :], bank_up[c % 2][:, :], ACT.Gelu, bias=f.bias_col[:, c:c + 1])\
                            .then_inc(gelu_done, 1)

                gelu(0)
                with act.Fori(1, groups) as q:
                    gelu(q)

            @block.tensor
            def _(pe):
                def turn(q):
                    pe.wait_ge(normed, Q * (q + 1))
                    for i in range(Q):
                        mm = pe.transpose(bank_n[:, i * T:(i + 1) * T], n[:, i, :], core.ident[:, :])
                    mm.then_inc(turned, 1)

                def up(q, c):
                    if c == 0:
                        pe.wait_ge(n_copied, q + 1)
                    if c >= 2:
                        pe.wait_ge(gelu_done, CH * q + c - 1)
                    pe.matmul(bank_up[c % 2][:, :], w_up[:, c * 128:(c + 1) * 128], nT[:, :],
                              start=True, stop=True).then_inc(up_done, 1)

                def down(q, c, first):
                    pe.wait_ge(gelu_done, CH * q + c + 1)
                    if c == 0 and not first:
                        pe.wait_ge(x_done, Q * q)
                    for i in range(Q):
                        mm = pe.matmul(bank_down[i][:, 0:D], h[:, c, i * T:(i + 1) * T], f.down[:, c, :],
                                       start=(c == 0), stop=(c == CH - 1))
                    if c == CH - 1:
                        mm.then_inc(down_done, 1)

                def step(q, first=False, last=False):
                    up(q, 0)
                    up(q, 1)
                    down(q, 0, first)
                    up(q, 2)
                    down(q, 1, first)
                    up(q, 3)
                    down(q, 2, first)
                    if not last:
                        turn(q + 1)
                    down(q, 3, first)

                turn(0)
                for c in range(CH):
                    mm = pe.matmul(bank_down[0][:, c:c + 1], f.bias[:, c * 128:(c + 1) * 128],
                                   core.ones[0:1, 0:1], start=True, stop=True)
                mm.then_inc(folded_turned, 1)
                for c in range(CH):
                    mm = pe.transpose(bank_fold[:, c * D:(c + 1) * D], f.down_w[:, c * 128:(c + 1) * 128],
                                      core.ident[:, :])
                mm.then_inc(folded_turned, 1)
                pe.wait_ge(folded_copied, 2)
                step(0, first=True)
                with pe.Fori(1, groups - 1) as q:
                    step(q)
                step(groups - 1, last=True)


H4, K4 = 8, 64
C4 = H4 * K4 // 128
DEN_EPS = 1e-6


class LinMem:
    def __init__(self, core):
        sb = core.sb
        self.wq, self.wk, self.wv, self.wg = (sb(f"li_{w}", [D, C4 * 128]) for w in ("wq", "wk", "wv", "wg"))
        self.wo = sb("li_wo", [128, C4, D])
        self.gate_bias = sb("li_gate_bias", [128, C4])
        self.decay = sb("li_decay", [T, H4])
        self.gap = sb("li_gap", [T, T])
        self.tri = sb("li_tri", [T, T])
        self.mask = sb("li_mask", [T, H4, T])
        self.loaded = core.keep_sem("li_loaded")


def linear_attention(core, m, au, a):
    nc = core.nc
    (s_var, s_rstd, stat, next_var, next_rstd, normed, turned, n_copied, k_proj, q_proj, gate_proj, v_proj,
     clipped, raised, tanhed, v_copied, zeroed, phi_done, a_done, decayed, num_done, den_done, inv_done,
     y_done, y_turned, gated, out_done, x_done) = core.sems(
        "li",
        "var rstd stat next_var next_rstd normed turned n_copied k_proj q_proj gate_proj v_proj clipped "
        "raised tanhed v_copied zeroed phi_done a_done decayed num_done den_done inv_done y_done y_turned "
        "gated out_done x_done")
    bank_q, bank_k, bank_g, bank_v = core.bank[0:4]
    bank_a, bank_num = core.bank[4:6], core.bank[6:8]
    bank_y, bank_z = core.bank[4:6]
    half = H4 // 2
    V1 = K4 + 1

    def by_chunk(ap):
        return ap.rearrange("p (c t) -> p c t", c=C4)

    with ExitStack() as ctx:
        def sb(name, shape):
            return ctx.enter_context(nc.sbuf_tensor(name, shape, FP32))

        n = sb("li_n", [T, D])
        nT = sb("li_nT", [D, T])
        clip_k, clip_q = sb("li_clip_k", [128, C4, T]), sb("li_clip_q", [128, C4, T])
        exp_k, exp_q = sb("li_exp_k", [128, C4, T]), sb("li_exp_q", [128, C4, T])
        phi_k = sb("li_phi_k", [128, C4, T])
        phi_q = sb("li_phi_q", [128, C4, 2, T])
        v = sb("li_v", [T, H4, V1])
        tanh = sb("li_tanh", [128, C4, T])
        am = sb("li_am", [T, H4, T])
        den, inv = sb("li_den", [T, H4]), sb("li_inv", [T, H4])
        y = sb("li_y", [T, H4, K4])
        yT = sb("li_yT", [128, C4, T])

        with nc.Block() as block:
            @block.sync
            def _(sp):
                au.load(sp, a)

            @block.vector
            def _(dve):
                def prepare(b):
                    normalise(core, dve, n[:, :], b).then_inc(normed, 1)

                def phi(b):
                    dve.wait_ge(raised, 2 * b + 1)
                    dve.scalar_tensor_tensor(out=phi_k[:, :, :], in0=by_chunk(bank_k[:, :]), scalar=0.0,
                                             in1=exp_k[:, :, :], op0=ALU.max, op1=ALU.add).then_inc(phi_done, 1)
                    dve.wait_ge(raised, 2 * b + 2)
                    for r in range(2):
                        rows = slice(64 * r, 64 * r + 64)
                        dve.scalar_tensor_tensor(out=phi_q[rows, :, r, :], in0=by_chunk(bank_q[rows, :]), scalar=0.0,
                                                 in1=exp_q[rows, :, :], op0=ALU.max, op1=ALU.add)\
                            .then_inc(phi_done, 1)

                def decay(b):
                    for i in range(2):
                        dve.wait_ge(a_done, 2 * b + i + 1)
                        dve.tensor_tensor(am[:, half * i:half * i + half, :],
                                          bank_a[i][:, :].rearrange("p (h t) -> p h t", h=half),
                                          m.mask[:, half * i:half * i + half, :], ALU.mult).then_inc(decayed, 1)

                def divide(b):
                    dve.wait_ge(num_done, b + 1)
                    for i in range(2):
                        num = bank_num[i][:, 0:half * V1].rearrange("p (h w) -> p h w", w=V1)
                        dve.tensor_scalar(den[:, half * i:half * i + half], num[:, :, K4], DEN_EPS, 2.0,
                                          ALU.add, ALU.mult).then_inc(den_done, 1)
                    dve.wait_ge(den_done, 2 * b + 2)
                    dve.reciprocal(inv[:, :], den[:, :]).then_inc(inv_done, 1)
                    dve.wait_ge(inv_done, b + 1)
                    for i in range(2):
                        num = bank_num[i][:, 0:half * V1].rearrange("p (h w) -> p h w", w=V1)
                        dve.tensor_tensor(y[:, half * i:half * i + half, :], num[:, :, 0:K4],
                                          inv[:, half * i:half * i + half].unsqueeze(2)
                                          .to_broadcast([T, half, K4]), ALU.mult).then_inc(y_done, 1)

                def gate(b):
                    dve.wait_ge(y_turned, b + 1)
                    dve.wait_ge(tanhed, b + 1)
                    dve.scalar_tensor_tensor(out=yT[:, :, :], in0=tanh[:, :, :], scalar=1.0,
                                             in1=by_chunk(bank_y[:, :]), op0=ALU.add, op1=ALU.mult)\
                        .then_inc(gated, 1)

                def finish(b):
                    dve.wait_ge(out_done, b + 1)
                    dve.tensor_tensor(core.x[:, b, :], bank_z[:, 0:D], core.x[:, b, :], ALU.add).then_inc(x_done, 1)
                    dve.wait_ge(x_done, b + 1)
                    dve.bn_stats(core.stats[:, b, :], core.x[:, b, :]).then_inc(stat, 1)

                def step(b, left=2):
                    decay(b)
                    divide(b)
                    gate(b)
                    if left >= 1:
                        phi(b + 1)
                    if left >= 2:
                        prepare(b + 2)
                    finish(b)

                prepare(0)
                dve.memset(phi_q[:, :, :, :], 0.0).then_inc(zeroed, 1)
                dve.memset(v[:, :, K4:V1], 1.0).then_inc(zeroed, 1)
                variance(core, dve, LATE, s_var)
                dve.wait_ge(s_rstd, 2)
                dve.wait_ge(zeroed, 2)
                phi(0)
                prepare(1)
                with dve.Fori(0, B // 2 - 1) as i:
                    step(2 * i)
                    step(2 * i + 1)
                step(B - 2, left=1)
                variance(core, dve, EARLY, next_var)
                step(B - 1, left=0)
                dve.wait_ge(stat, B)

            @block.gpsimd
            def _(pool):
                inverse_deviation(core, pool, LATE, s_var, s_rstd)
                au.make_constants(pool)
                inverse_deviation(core, pool, EARLY, next_var, next_rstd)
                pool.wait_ge(next_rstd, 2)

            @block.scalar
            def _(act):
                def prepare(b, first=False):
                    act.wait_ge(turned, b + 1)
                    act.activation(nT[:, :], bank_v[:, 0:T], ACT.Copy).then_inc(n_copied, 1)
                    for i, (proj, bank, clip, ex) in enumerate(((k_proj, bank_k, clip_k, exp_k),
                                                                (q_proj, bank_q, clip_q, exp_q))):
                        act.wait_ge(proj, b + 1)
                        act.activation(clip[:, :, :], by_chunk(bank[:, :]), ACT.Relu, scale=-1.0)\
                            .then_inc(clipped, 1)
                        act.wait_ge(clipped, 2 * b + i + 1)
                        act.activation(ex[:, :, :], clip[:, :, :], ACT.Exp, scale=-1.0).then_inc(raised, 1)
                    act.wait_ge(v_proj, b + 1)
                    if first:
                        act.wait_ge(zeroed, 2)
                    act.activation(v[:, :, 0:K4], bank_v[:, :].rearrange("p (h w) -> p h w", h=H4), ACT.Copy)\
                        .then_inc(v_copied, 1)
                    act.wait_ge(gate_proj, b + 1)
                    if not first:
                        act.wait_ge(gated, b)
                    for c in range(C4):
                        ins = act.activation(tanh[:, c, :], bank_g[:, c * T:(c + 1) * T], ACT.Tanh,
                                             bias=m.gate_bias[:, c:c + 1], scale=0.5)
                    ins.then_inc(tanhed, 1)

                prepare(0, first=True)
                with act.Fori(1, B) as b:
                    prepare(b)

            @block.tensor
            def _(pe):
                def turn(b):
                    pe.wait_ge(normed, b + 1)
                    pe.transpose(bank_v[:, 0:T], n[:, :], core.ident[:, :]).then_inc(turned, 1)

                def project(b, w, bank, proj):
                    for c in range(C4):
                        mm = pe.matmul(bank[:, c * T:(c + 1) * T], w[:, c * 128:(c + 1) * 128], nT[:, :],
                                       start=True, stop=True)
                    mm.then_inc(proj, 1)

                def project_kq(b):
                    pe.wait_ge(n_copied, b + 1)
                    project(b, m.wk, bank_k, k_proj)
                    project(b, m.wq, bank_q, q_proj)

                def project_v(b):
                    pe.matmul(bank_v[:, :], nT[:, :], m.wv[:, :], start=True, stop=True).then_inc(v_proj, 1)

                def project_g(b, first=False):
                    if not first:
                        pe.wait_ge(tanhed, b)
                    project(b, m.wg, bank_g, gate_proj)

                def attend(b, first=False):
                    pe.wait_ge(phi_done, 3 * (b + 1))
                    for c in range(C4):
                        if c == C4 // 2 and not first:
                            pe.wait_ge(x_done, b)
                        mm = pe.matmul(bank_a[c // 2][:, 256 * (c % 2):256 * (c % 2) + 256], phi_k[:, c, :],
                                       phi_q[:, c, :, :].rearrange("p r t -> p (r t)"), start=True, stop=True)
                        if c % 2:
                            mm.then_inc(a_done, 1)

                def numerator(b):
                    pe.wait_ge(v_copied, b + 1)
                    for h in range(H4):
                        if h % half == 0:
                            pe.wait_ge(decayed, 2 * b + h // half + 1)
                        i = h % half
                        mm = pe.matmul(bank_num[h // half][:, i * V1:(i + 1) * V1], am[:, h, :], v[:, h, :],
                                       start=True, stop=True)
                    mm.then_inc(num_done, 1)

                def turn_y(b):
                    pe.wait_ge(y_done, 2 * b + 2)
                    for c in range(C4):
                        mm = pe.transpose(bank_y[:, c * T:(c + 1) * T],
                                          y[:, 2 * c:2 * c + 2, :].rearrange("p h w -> p (h w)"), core.ident[:, :])
                    mm.then_inc(y_turned, 1)

                def out(b):
                    pe.wait_ge(gated, b + 1)
                    for c in range(C4):
                        mm = pe.matmul(bank_z[:, 0:D], yT[:, c, :], m.wo[:, c, :],
                                       start=(c == 0), stop=(c == C4 - 1))
                    mm.then_inc(out_done, 1)

                def step(b, first=False, last=False):
                    attend(b, first)
                    if not last:
                        pe.wait_ge(v_copied, b + 1)
                        turn(b + 1)
                    numerator(b)
                    if not last:
                        project_kq(b + 1)
                    turn_y(b)
                    if not last:
                        project_v(b + 1)
                    out(b)
                    if not last:
                        project_g(b + 1)

                pe.wait_ge(m.loaded, 80)
                turn(0)
                project_kq(0)
                project_v(0)
                project_g(0, first=True)
                step(0, first=True)
                with pe.Fori(1, B - 1) as b:
                    step(b)
                step(B - 1, last=True)


NH5 = 16
D5 = D // NH5
TOP = 4
COS, SIN, CAS, SAC = range(4)
BH = B * NH5
HALVES = BH // 128


class AutoMem:

    def __init__(self, core):
        sb = core.sb
        self.dft = sb("au_dft", [T, 4, T])
        self.inv = sb("au_inv", [T, T])
        self.wq, self.wk, self.wv, self.wo = (sb(f"au_{w}", [D, D]) for w in ("wq", "wk", "wv", "wo"))
        self.bias = [sb(f"au_bias_{w}", [T, Q, D]) for w in ("q", "k", "v")]
        self.out_bias = sb("au_out_bias", [T, D])
        self.iota = sb("au_iota", [128, T])
        self.ctx = sb("au_ctx", [T, 2, Q, D])
        self.loaded, self.zeroed, self.scaled = core.sems("ac", "loaded zeroed scaled")
        self.ctx_loaded = core.sems("ac", "ctx_loaded0 ctx_loaded1")

    def load_ctx(self, sp, a, g):
        sp.dma_start(self.ctx[:, g % 2, :, :], a["ctx_1024"][Q * g:Q * g + Q].rearrange("b t d -> t b d"))\
            .then_inc(self.ctx_loaded[g % 2], 16)

    def load(self, sp, a):
        sp.dma_start(self.dft[:, :, :], a["c_dft"].rearrange("p (k t) -> p k t", k=4)).then_inc(self.loaded, 16)
        for dst, src in ((self.wq, "auto_WqT"), (self.wk, "auto_WkT"), (self.wv, "auto_WvT"), (self.wo, "auto_WoT"),
                         (self.iota, "c_iota")):
            sp.dma_start(dst[:, :], a[src]).then_inc(self.loaded, 16)
        sp.dma_start(self.out_bias[:, :], a["L1_xattn_bo"].partition_broadcast(T)).then_inc(self.loaded, 16)
        self.load_ctx(sp, a, 0)
        self.load_ctx(sp, a, 1)
        sp.wait_ge(self.zeroed, 3)
        for dst, src in zip(self.bias, ("L1_xattn_bq", "L1_xattn_bk", "L1_xattn_bv")):
            for i in range(Q):
                sp.dma_start(dst[0:1, i, :], a[src].unsqueeze(0)).then_inc(self.loaded, 16)

    def make_constants(self, pool):
        for t in self.bias:
            pool.memset(t[:, :, :], 0.0).then_inc(self.zeroed, 1)
        pool.wait_ge(self.loaded, 16 * (7 + 3 * Q))
        for t in self.bias:
            pool.tensor_scalar(t[0:1, :, :], t[0:1, :, :], float(T), None, ALU.mult).then_inc(self.scaled, 1)
        pool.tensor_scalar(self.inv[:, :], self.dft[:, CAS, :], 1.0 / T, None, ALU.mult).then_inc(self.scaled, 1)
        pool.wait_ge(self.scaled, 4)


def autocorrelation(core, m, ro, a):
    nc = core.nc
    groups = B // Q
    (s_var, s_rstd, stat, next_var, next_rstd, normed, q_turned, c_turned, zq_copied, zc_copied, projected,
     spectra, odd_done, even_done, diff_done, summed, corr_done, corr_copied, top, idx, coded, w_sum, w_exp,
     kernels, k_turned, k_copied, k_spec, k_spec_copied, biased, y_cos_done, y_sin_done, y_done, o_done,
     o_copied, out_done, x_done) = core.sems(
        "au",
        "var rstd stat next_var next_rstd normed q_turned c_turned zq_copied zc_copied projected spectra "
        "odd_done even_done diff_done summed corr_done corr_copied top idx coded w_sum w_exp kernels "
        "k_turned k_copied k_spec k_spec_copied biased y_cos_done y_sin_done y_done o_done o_copied "
        "out_done x_done")
    dft, inv, wq, wk, wv, wo, iota, cx = m.dft, m.inv, m.wq, m.wk, m.wv, m.wo, m.iota, m.ctx
    bias, out_bias, ctx_loaded = m.bias, m.out_bias, m.ctx_loaded
    bank_zq, bank_zc = core.bank[0:2]
    bank_qc, bank_qs, bank_ke, bank_ko, bank_vc, bank_vs = core.bank[2:8]

    def four(ap):
        return ap.rearrange("p (i d) -> p i d", i=Q)

    with ExitStack() as ctx:
        def sb(name, shape, dt=FP32):
            return ctx.enter_context(nc.sbuf_tensor(name, shape, dt))

        n = sb("au_n", [T, 2, Q, D])
        zq = sb("au_zq", [D, 2, 2, T])
        zc = sb("au_zc", [D, 2, 2, T])
        q_cas, q_sac = sb("au_q_cas", [T, Q, D]), sb("au_q_sac", [T, Q, D])
        k_even = sb("au_k_even", [T, Q, D])
        even, odd = sb("au_even", [T, 2, Q, D]), sb("au_odd", [T, 2, Q, D])
        v_cos, v_sin = sb("au_v_cos", [T, B, D]), sb("au_v_sin", [T, B, D])
        spec = sb("au_spec", [T, B, NH5])
        corr = sb("au_corr", [128, HALVES, T])
        top_v = sb("au_top_v", [128, HALVES, 8])
        top_i = sb("au_top_i", [128, HALVES, 8], U32)
        lag = sb("au_lag", [128, HALVES, 8])
        w, w_tot, w_inv = sb("au_w", [128, HALVES, TOP]), sb("au_w_tot", [128, HALVES]), sb("au_w_inv", [128, HALVES])
        pick = sb("au_pick", [128, HALVES, TOP, T])
        kern_t = sb("au_kern_t", [T, BH])
        k_sp = sb("au_k_sp", [T, 2, B, NH5])
        y, y_sin = sb("au_y", [T, B, D]), sb("au_y_sin", [T, B, D])
        oT = sb("au_oT", [D, 2, T])

        def by_head(eng, y, v, r, g, done):
            seqs = slice(Q * g, Q * g + Q)
            k = k_sp[:, r, seqs, :].rearrange("p b h -> p (b h)").unsqueeze(2).to_broadcast([T, Q * NH5, D5])
            eng.tensor_tensor(y[:, seqs, :].rearrange("p i (h d) -> p (i h) d", d=D5),
                              v[:, seqs, :].rearrange("p i (h d) -> p (i h) d", d=D5), k, ALU.mult)\
                .then_inc(done, 1)

        with nc.Block() as block:
            @block.sync
            def _(sp):
                ro.load(sp, a)
                for g in range(2, groups):
                    sp.wait_ge(c_turned, Q * (g - 1))
                    m.load_ctx(sp, a, g)
                sp.wait_ge(ro.loaded, 16 * 12)

            @block.vector
            def _(dve):
                def prepare(g, par):
                    for i in range(Q):
                        normalise(core, dve, n[:, par, i, :], Q * g + i).then_inc(normed, 1)

                def correlate(g, par):
                    dve.wait_ge(projected, Q * (g + 1))
                    for dst, bank, b in ((q_cas[:, :, :], bank_qc, bias[0]), (k_even[:, :, :], bank_ke, bias[1]),
                                         (q_sac[:, :, :], bank_qs, bias[0])):
                        dve.tensor_tensor(dst, four(bank[:, :]), b[:, :, :], ALU.add).then_inc(spectra, 1)
                    dve.wait_ge(spectra, 5 * g + 3)
                    dve.tensor_tensor(odd[:, par, :, :], four(bank_ko[:, :]), q_sac[:, :, :], ALU.mult)\
                        .then_inc(odd_done, 1)
                    dve.tensor_tensor(v_cos[:, Q * g:Q * g + Q, :], four(bank_vc[:, :]), bias[2][:, :, :], ALU.add)\
                        .then_inc(spectra, 1)
                    dve.tensor_copy(v_sin[:, Q * g:Q * g + Q, :], four(bank_vs[:, :])).then_inc(spectra, 1)

                def head_sums(g, par):
                    dve.wait_ge(diff_done, g + 1)
                    dve.tensor_reduce(spec[:, bass.ds(Q * g, Q), :],
                                      even[:, par, :, :].rearrange("p i (h d) -> p i h d", d=D5), AX.X, ALU.add)\
                        .then_inc(summed, 1)

                prepare(0, 0)
                prepare(1, 1)
                variance(core, dve, LATE, s_var)
                dve.wait_ge(s_rstd, 2)
                for g in range(groups):
                    correlate(g, g % 2)
                    if g + 2 < groups:
                        dve.wait_ge(q_turned, Q * (g + 1))
                        prepare(g + 2, g % 2)
                    head_sums(g, g % 2)

                for i in range(HALVES):
                    dve.wait_ge(corr_copied, i + 1)
                    dve.max(top_v[:, i, :], corr[:, i, :]).then_inc(top, 1)
                dve.wait_ge(top, HALVES)
                for i in range(HALVES):
                    dve.max_index(top_i[:, i, :], top_v[:, i, :], corr[:, i, :]).then_inc(idx, 1)
                dve.tensor_tensor(w[:, :, :], top_v[:, :, 0:TOP], top_v[:, :, 0:1].to_broadcast([128, HALVES, TOP]),
                                  ALU.subtract).then_inc(coded, 1)
                dve.wait_ge(idx, HALVES)
                dve.tensor_copy(lag[:, :, :], top_i[:, :, :]).then_inc(coded, 1)
                dve.wait_ge(w_exp, 1)
                dve.tensor_reduce(w_tot[:, :], w[:, :, :], AX.X, ALU.add).then_inc(w_sum, 1)
                dve.wait_ge(w_sum, 1)
                dve.reciprocal(w_inv[:, :], w_tot[:, :]).then_inc(w_sum, 1)
                dve.wait_ge(w_sum, 2)
                dve.tensor_tensor(w[:, :, :], w[:, :, :], w_inv[:, :].unsqueeze(2).to_broadcast([128, HALVES, TOP]),
                                  ALU.mult).then_inc(w_sum, 1)
                dve.wait_ge(w_sum, 3)
                dve.wait_ge(coded, 2)
                for i in range(HALVES):
                    for k in range(TOP):
                        dve.tensor_scalar(pick[:, i, k, :], iota[:, :], lag[:, i, k:k + 1], w[:, i, k:k + 1],
                                          ALU.is_equal, ALU.mult).then_inc(kernels, 1)
                count = HALVES * TOP
                for step in (2, 1):
                    dve.wait_ge(kernels, count)
                    dve.tensor_tensor(pick[:, :, 0:step, :], pick[:, :, 0:step, :], pick[:, :, step:2 * step, :],
                                      ALU.add).then_inc(kernels, 1)
                    count += 1

                def convolve(g):
                    seqs = slice(Q * g, Q * g + Q)
                    dve.wait_ge(y_cos_done, g + 1)
                    dve.wait_ge(y_sin_done, g + 1)
                    dve.tensor_tensor(y[:, seqs, :], y[:, seqs, :], y_sin[:, seqs, :], ALU.add)\
                        .then_inc(y_done, 1)

                def finish(g):
                    dve.wait_ge(out_done, Q * (g + 1))
                    dve.tensor_tensor(core.x[:, Q * g:Q * g + Q, :], four(core.bank[2 + g % 2][:, :]),
                                      core.x[:, Q * g:Q * g + Q, :], ALU.add).then_inc(x_done, 1)
                    dve.wait_ge(x_done, g + 1)
                    for b in range(Q * g, Q * g + Q):
                        dve.bn_stats(core.stats[:, b, :], core.x[:, b, :]).then_inc(stat, 1)

                dve.wait_ge(k_spec_copied, 2)
                dve.wait_ge(biased, B)
                by_head(dve, y, v_cos, 0, 0, y_cos_done)
                for g in range(1, groups):
                    by_head(dve, y, v_cos, 0, g, y_cos_done)
                    convolve(g - 1)
                convolve(groups - 1)
                for g in range(groups):
                    if g == groups - 1:
                        dve.wait_ge(stat, EARLY.stop)
                        variance(core, dve, EARLY, next_var)
                    finish(g)
                dve.wait_ge(stat, B)

            @block.gpsimd
            def _(pool):
                inverse_deviation(core, pool, LATE, s_var, s_rstd)
                for g in range(groups):
                    par = g % 2
                    pool.wait_ge(spectra, 5 * g + 2)
                    if g >= 2:
                        pool.wait_ge(summed, g - 1)
                    pool.tensor_tensor(even[:, par, :, :], q_cas[:, :, :], k_even[:, :, :], ALU.mult)\
                        .then_inc(even_done, 1)
                    pool.wait_ge(odd_done, g + 1)
                    pool.wait_ge(even_done, g + 1)
                    pool.tensor_tensor(even[:, par, :, :], even[:, par, :, :], odd[:, par, :, :], ALU.subtract)\
                        .then_inc(diff_done, 1)
                pool.wait_ge(normed, B)
                with pool.Fori(0, B) as b:
                    pool.tensor_tensor(core.x[:, b, :], core.x[:, b, :], out_bias[:, :], ALU.add).then_inc(biased, 1)
                pool.wait_ge(k_spec_copied, 2)
                for g in range(groups):
                    by_head(pool, y_sin, v_sin, 1, g, y_sin_done)
                inverse_deviation(core, pool, EARLY, next_var, next_rstd)
                pool.wait_ge(next_rstd, 2)

            @block.scalar
            def _(act):
                def copy_transforms(b, par, reused=True):
                    act.wait_ge(q_turned, b + 1)
                    if reused:
                        act.wait_ge(projected, b - 1)
                    act.activation(zq[:, par, :, :], bank_zq[:, 0:2 * T].rearrange("p (k t) -> p k t", k=2),
                                   ACT.Copy).then_inc(zq_copied, 1)
                    act.wait_ge(c_turned, b + 1)
                    act.activation(zc[:, par, :, :], bank_zc[:, 0:2 * T].rearrange("p (k t) -> p k t", k=2),
                                   ACT.Copy).then_inc(zc_copied, 1)

                for par in range(2):
                    copy_transforms(par, par, reused=False)
                with act.Fori(1, B // 2) as i:
                    for par in range(2):
                        copy_transforms(2 * i + par, par)
                for i in range(HALVES):
                    act.wait_ge(corr_done, i + 1)
                    act.activation(corr[:, i, :], core.bank[i][:, 0:T], ACT.Copy, scale=1.0 / D5)\
                        .then_inc(corr_copied, 1)
                act.wait_ge(coded, 1)
                act.activation(w[:, :, :], w[:, :, :], ACT.Exp).then_inc(w_exp, 1)
                act.wait_ge(k_turned, 1)
                act.activation(kern_t[:, :], core.bank[4][:, 0:BH], ACT.Copy).then_inc(k_copied, 1)
                for r in range(2):
                    act.wait_ge(k_spec, r + 1)
                    act.activation(k_sp[:, r, :, :], core.bank[5 + r][:, 0:BH].rearrange("p (b h) -> p b h", b=B),
                                   ACT.Copy).then_inc(k_spec_copied, 1)

                def copy_o(b, par, reused=True):
                    act.wait_ge(o_done, b + 1)
                    if reused:
                        act.wait_ge(out_done, b - 1)
                    act.activation(oT[:, par, :], core.bank[par][:, 0:T], ACT.Copy).then_inc(o_copied, 1)

                for par in range(2):
                    copy_o(par, par, reused=False)
                with act.Fori(1, B // 2) as i:
                    for par in range(2):
                        copy_o(2 * i + par, par)

            @block.tensor
            def _(pe):
                def transform(b):
                    g, i = b // Q, b % Q
                    if b >= 1:
                        pe.wait_ge(zq_copied, b)
                    pe.wait_ge(normed, b + 1)
                    pe.matmul(bank_zq[:, 0:2 * T], n[:, g % 2, i, :],
                              dft[:, CAS:SAC + 1, :].rearrange("p k t -> p (k t)"), start=True, stop=True)\
                        .then_inc(q_turned, 1)
                    if b >= 1:
                        pe.wait_ge(zc_copied, b)
                    pe.wait_ge(ctx_loaded[g % 2], 16 * (g // 2 + 1))
                    pe.matmul(bank_zc[:, 0:2 * T], cx[:, g % 2, i, :],
                              dft[:, COS:SIN + 1, :].rearrange("p k t -> p (k t)"),
                              start=True, stop=True).then_inc(c_turned, 1)

                def project(b):
                    g, i = b // Q, b % Q
                    cols = slice(i * D, (i + 1) * D)
                    pe.wait_ge(zq_copied, b + 1)
                    pe.wait_ge(zc_copied, b + 1)
                    for bank, z, wgt, reader, place in (
                            (bank_qc, zq[:, b % 2, 0, :], wq, spectra, 5 * g - 4),
                            (bank_ke, zc[:, b % 2, COS, :], wk, spectra, 5 * g - 3),
                            (bank_qs, zq[:, b % 2, 1, :], wq, spectra, 5 * g - 2),
                            (bank_ko, zc[:, b % 2, SIN, :], wk, odd_done, g),
                            (bank_vc, zc[:, b % 2, COS, :], wv, spectra, 5 * g - 1),
                            (bank_vs, zc[:, b % 2, SIN, :], wv, spectra, 5 * g)):
                        if i == 0 and g >= 1:
                            pe.wait_ge(reader, place)
                        mm = pe.matmul(bank[:, cols], z, wgt[:, :], start=True, stop=True)
                    mm.then_inc(projected, 1)

                transform(0)
                for b in range(B):
                    if b + 1 < B:
                        transform(b + 1)
                    project(b)
                for i in range(HALVES):
                    seqs = B // HALVES
                    pe.wait_ge(summed, groups // HALVES * (i + 1))
                    pe.matmul(core.bank[i][:, 0:T],
                              spec[:, seqs * i:seqs * (i + 1), :].rearrange("p b h -> p (b h)"), inv[:, :],
                              start=True, stop=True).then_inc(corr_done, 1)
                pe.wait_ge(kernels, HALVES * TOP + 2)
                for i in range(HALVES):
                    mm = pe.transpose(core.bank[4][:, i * 128:(i + 1) * 128], pick[:, i, 0, :], core.ident[:, :])
                mm.then_inc(k_turned, 1)
                pe.wait_ge(k_copied, 1)
                for r, k in enumerate((CAS, SAC)):
                    pe.matmul(core.bank[5 + r][:, 0:BH], dft[:, k, :], kern_t[:, :], start=True, stop=True)\
                        .then_inc(k_spec, 1)

                def inverse(b):
                    g, i = b // Q, b % Q
                    if i == 0:
                        pe.wait_ge(y_done, g + 1)
                    if b >= 2:
                        pe.wait_ge(o_copied, b - 1)
                    pe.matmul(core.bank[b % 2][:, 0:T], y[:, b, :], inv[:, :], start=True, stop=True)\
                        .then_inc(o_done, 1)

                def out(b):
                    g, i = b // Q, b % Q
                    pe.wait_ge(o_copied, b + 1)
                    if i == 0 and g >= 2:
                        pe.wait_ge(x_done, g - 1)
                    pe.matmul(core.bank[2 + g % 2][:, i * D:(i + 1) * D], oT[:, b % 2, :], wo[:, :],
                              start=True, stop=True).then_inc(out_done, 1)

                inverse(0)
                for b in range(B):
                    if b + 1 < B:
                        inverse(b + 1)
                    out(b)


E6 = 8
H6 = 512
CH6 = H6 // 128
CAP = -(-12 * B * T // (10 * E6))
ROWS = [min(128, CAP - r) for r in range(0, CAP, 128)]
TILES = E6 * len(ROWS)
DROPPED = 4096
BITS = 30
ROUND = 3
TRIALS = (1 << ROUND) - 1
UNROLL = 5
HALF = B // 2


def experts(core, m, a, out):
    nc = core.nc
    n_rows = nc.dram_tensor("mo_n_rows", (B * T, D), FP32, kind="Internal").ap()
    planes = nc.dram_tensor("mo_planes", (2 * B * T, D), FP32, kind="Internal").ap()
    with ExitStack() as ctx:
        def sb(name, shape, dt=FP32):
            return ctx.enter_context(nc.sbuf_tensor(name, shape, dt))

        gate = [sb(f"mo_gate{k}", [T, B]) for k in range(2)]
        src_row = sb("mo_src_row", [128, TILES], U32)
        dst_row = sb("mo_dst_row", [128, TILES], U32)
        with ExitStack() as part:
            route(core, m, part, gate, src_row, dst_row, n_rows, planes)
        expert_loop(core, a, out, gate, src_row, dst_row, n_rows, planes, m.b1, m.b2)


class RouteMem:

    def __init__(self, core):
        sb = core.sb
        self.wr, self.br = sb("ro_wr", [D, E6]), sb("ro_br", [T, E6])
        self.iota = sb("ro_iota", [T, E6])
        self.base = sb("ro_base", [128, 1])
        self.trial_bits = sb("ro_trial_bits", [128, BITS // ROUND, TRIALS * E6], I32)
        self.same = sb("ro_same", [128, 128])
        self.earlier = sb("ro_earlier", [128, 128])
        self.lanes = sb("ro_lanes", [T, T])
        self.lane = sb("ro_lane", [128, 1])
        self.seq_code = sb("ro_seq_code", [T, 2, B])
        self.b1 = sb("mo_b1", [128, E6, CH6])
        self.b2 = sb("mo_b2", [128, E6, D])
        self.loaded, = core.sems("rc", "loaded")

    def load(self, sp, a):
        for dst, src in ((self.wr, a["L1_ffn_Wr"]), (self.br, a["L1_ffn_br"].partition_broadcast(T)),
                         (self.iota, a["c_expert"].partition_broadcast(T)), (self.base, a["c_base"]),
                         (self.same, a["c_same"]), (self.earlier, a["c_earlier"]), (self.lanes, a["c_iota"]),
                         (self.lane, a["c_lane"])):
            sp.dma_start(dst[:, :], src).then_inc(self.loaded, 16)
        for dst, src in ((self.trial_bits, "c_trial_bits"), (self.seq_code, "c_seq_code")):
            sp.dma_start(dst[:, :, :].rearrange("t i e -> t (i e)"), a[src].partition_broadcast(T))\
                .then_inc(self.loaded, 16)
        sp.dma_start(self.b1[:, :, :], a["moe_b1_col"].rearrange("p (e c) -> p e c", e=E6)).then_inc(self.loaded, 16)
        sp.dma_start(self.b2[:, :, :].rearrange("p e d -> p (e d)"),
                     a["L1_ffn_b2"].rearrange("e d -> (e d)").partition_broadcast(T)).then_inc(self.loaded, 16)


def route(core, m, ctx, gate, src_row, dst_row, n_rows, planes):
    nc = core.nc
    groups = B // Q

    def sb(name, shape, dt=FP32):
        return ctx.enter_context(nc.sbuf_tensor(name, shape, dt))

    wr, br, iota, base, trial_bits, same, earlier, lanes, lane, seq_code = (
        m.wr, m.br, m.iota, m.base, m.trial_bits, m.same, m.earlier, m.lanes, m.lane, m.seq_code)
    lanes_b = sb("ro_lanes_b", [T, T], BF16)
    n4, nT = sb("ro_n4", [T, 2, Q, D]), sb("ro_nT", [D, 2, Q * T])
    p, tmp, tmp2 = sb("ro_p", [T, B, E6]), sb("ro_tmp", [T, B, E6]), sb("ro_tmp2", [T, B, E6])
    pick = [sb(f"ro_pick{k}", [T, B, E6]) for k in range(2)]
    v = sb("ro_v", [T, B, E6])
    red = sb("ro_red", [T, B])
    positive, above, tied = sb("ro_positive", [T, B, E6]), sb("ro_above", [T, B, E6]), sb("ro_tied", [T, B, E6])
    reached = sb("ro_reached", [T, B, TRIALS, E6], BF16)
    trial = sb("ro_trial", [T, TRIALS, E6], I32)
    passed = sb("ro_passed", [T, 1 + TRIALS, E6])
    level = sb("ro_level", [T, E6])
    ones_b = sb("ro_ones_b", [T, T], BF16)
    count = sb("ro_count", [128, 1])
    keep, equal, upto = sb("ro_keep", [128, T]), sb("ro_equal", [128, T]), sb("ro_upto", [128, T])
    need, offset = sb("ro_need", [128, 1]), sb("ro_offset", [128, 1])
    zeros = sb("ro_zeros", [128, 2 * D])
    slot_f = sb("ro_slot_f", [T, 2, B])
    slot_i, slot_lo, slot_hi = (sb(f"ro_{w}", [T, 2, B], I32) for w in ("slot_i", "slot_lo", "slot_hi"))
    lo, hi = sb("ro_lo", [T, 2, B], BF16), sb("ro_hi", [T, 2, B])
    at_row = sb("ro_at_row", [T, 2, B, 128], BF16)
    at_tile = sb("ro_at_tile", [T, 2, B, TILES])
    codes = sb("ro_codes", [T, 2, B, 2, TILES], BF16)
    code_sum = sb("ro_code_sum", [128, 2, TILES])
    empty = sb("ro_empty", [128, TILES])
    (n_out0, n_out1, cleared, made, s_var, s_rstd, normed, turned, n_copied, logits, biased, s, expd,
     reached_done, flagged, flags_turned, counted, compared, totalled, summed, slots_turned, lanes_made,
     rows_marked, coded, mapped) = core.sems(
        "ro",
        "n_out0 n_out1 cleared made var rstd normed turned n_copied logits biased step expd reached_done "
        "flagged flags_turned counted compared totalled summed slots_turned lanes_made rows_marked coded "
        "mapped")
    n_out = (n_out0, n_out1)
    bank_c, bank_v, bank_s, bank_m = core.bank[0:4]
    bank_l, bank_n = core.bank[4:6], core.bank[6:8]

    def per_token(ap):
        return ap.unsqueeze(2).to_broadcast([T, B, E6])

    def per_expert(ap):
        return ap.unsqueeze(1).to_broadcast([T, B, E6])

    with nc.Block() as block:
        @block.sync
        def _(sp):
            with sp.Fori(0, groups // 2) as i:
                for par in range(2):
                    g = 2 * i + par
                    sp.wait_ge(normed, Q * (g + 1))
                    sp.dma_start(n_rows[bass.ds(Q * T * g, Q * T), :].rearrange("(i t) d -> t i d", i=Q),
                                 n4[:, par, :, :]).then_inc(n_out[par], 16)
            for par in range(2):
                sp.wait_ge(n_out[par], 16 * groups // 2)

        @block.gpsimd
        def _(pool):
            pool.memset(zeros[:, :], 0.0).then_inc(made, 1)
            pool.memset(ones_b[:, :], 1.0).then_inc(made, 1)
            inverse_deviation(core, pool, LATE, s_var, s_rstd)
            pool.wait_ge(made, 2)
            pool.dma_start(planes.rearrange("s d -> (s d)").rearrange("(p e n) -> p e n", p=128, n=2 * D),
                           over(zeros[:, :], B)).then_inc(cleared, 16)
            pool.wait_ge(cleared, 16)

        @block.scalar
        def _(act):
            with act.Fori(0, groups // 2) as i:
                for par in range(2):
                    act.wait_ge(turned, 2 * i + par + 1)
                    act.activation(nT[:, par, :], bank_n[par][:, :], ACT.Copy).then_inc(n_copied, 1)
            act.wait_ge(s, 2)
            act.activation(p[:, :, :], p[:, :, :], ACT.Exp).then_inc(expd, 1)

        @block.tensor
        def _(pe):
            def turn(g, par):
                pe.wait_ge(normed, Q * (g + 1))
                for i in range(Q):
                    mm = pe.transpose(bank_n[par][:, i * T:(i + 1) * T], n4[:, par, i, :], core.ident[:, :])
                mm.then_inc(turned, 1)

            def logit(g, par):
                pe.wait_ge(n_copied, g + 1)
                for i in range(Q):
                    mm = pe.matmul(bank_l[par][:, i * E6:(i + 1) * E6], nT[:, par, i * T:(i + 1) * T], wr[:, :],
                                   start=True, stop=True)
                mm.then_inc(logits, 1)

            turn(0, 0)
            with pe.Fori(0, groups // 2 - 1) as j:
                turn(2 * j + 1, 1)
                logit(2 * j, 0)
                turn(2 * j + 2, 0)
                logit(2 * j + 1, 1)
            turn(groups - 1, 1)
            logit(groups - 2, 0)
            logit(groups - 1, 1)
            pe.wait_ge(made, 2)
            with pe.Fori(0, BITS // ROUND) as i:
                for b in range(B):
                    if b % HALF == 0:
                        pe.wait_ge(reached_done, 2 * i + b // HALF + 1)
                    mm = pe.matmul(bank_c[:, 0:TRIALS * E6], ones_b[:, :],
                                   reached[:, b, :, :].rearrange("t j e -> t (j e)"),
                                   start=(b == 0), stop=(b == B - 1))
                mm.then_inc(compared, 1)
            for k, flags in enumerate((above, tied)):
                pe.wait_ge(flagged, k + 1)
                mm = pe.transpose(bank_v[:, k * T:(k + 1) * T], flags[:, :, :].rearrange("t b e -> t (b e)"),
                                  core.ident[:, :])
            mm.then_inc(flags_turned, 1)
            pe.wait_ge(counted, 1)
            pe.matmul(bank_c[:, 0:1], same[:, :], count[:, :], start=True, stop=True).then_inc(compared, 1)
            for k in range(2):
                pe.wait_ge(totalled, k + 1)
                pe.matmul(bank_s[:, k:k + 1], earlier[:, :], upto[:, T - 1:T], start=True, stop=True)\
                    .then_inc(summed, 1)
            pe.wait_ge(totalled, 3)
            pe.transpose(bank_v[:, 0:128], upto[:, :], core.ident[:, :]).then_inc(slots_turned, 1)
            pe.wait_ge(coded, 2)
            for k in range(2):
                pe.wait_ge(rows_marked, k + 1)
                for b in range(B):
                    mm = pe.matmul(bank_m[:, 0:2 * TILES], at_row[:, k, b, :],
                                   codes[:, k, b, :, :].rearrange("t c s -> t (c s)"),
                                   start=(k == 0 and b == 0), stop=(k == 1 and b == B - 1))
            mm.then_inc(mapped, 1)

        @block.vector
        def _(dve):
            steps = 0

            def done(ins):
                nonlocal steps
                steps += 1
                ins.then_inc(s, 1)
                dve.wait_ge(s, steps)

            def prepare(g, par):
                for i in range(Q):
                    normalise(core, dve, n4[:, par, i, :], Q * g + i).then_inc(normed, 1)

            def add_bias(g, par):
                dve.wait_ge(logits, g + 1)
                dve.tensor_tensor(p[:, bass.ds(Q * g, Q), :],
                                  bank_l[par][:, 0:Q * E6].rearrange("t (i e) -> t i e", i=Q),
                                  over(br[:, :], Q), ALU.add).then_inc(biased, 1)

            prepare(0, 0)
            prepare(1, 1)
            variance(core, dve, LATE, s_var)
            dve.wait_ge(s_rstd, 2)
            dve.tensor_copy(lanes_b[:, :], lanes[:, :]).then_inc(lanes_made, 1)
            with dve.Fori(0, groups // 2 - 1) as i:
                for par in range(2):
                    add_bias(2 * i + par, par)
                    dve.wait_ge(n_out[par], 16 * (i + 1))
                    prepare(2 * i + par + 2, par)
            for par in range(2):
                add_bias(groups - 2 + par, par)
            dve.wait_ge(biased, groups)

            done(dve.tensor_reduce(red[:, :], p[:, :, :], AX.X, ALU.max))
            done(dve.tensor_tensor(p[:, :, :], p[:, :, :], per_token(red[:, :]), ALU.subtract))
            dve.wait_ge(expd, 1)
            done(dve.tensor_reduce(red[:, :], p[:, :, :], AX.X, ALU.add))
            done(dve.reciprocal(red[:, :], red[:, :]))
            done(dve.tensor_tensor(p[:, :, :], p[:, :, :], per_token(red[:, :]), ALU.mult))

            for k in range(2):
                q = (p, tmp2)[k]
                done(dve.tensor_reduce(gate[k][:, :], q[:, :, :], AX.X, ALU.max))
                done(dve.tensor_tensor(tmp[:, :, :], q[:, :, :], per_token(gate[k][:, :]), ALU.is_equal))
                done(dve.tensor_tensor(tmp[:, :, :], tmp[:, :, :], per_expert(iota[:, :]), ALU.mult))
                done(dve.tensor_reduce(red[:, :], tmp[:, :, :], AX.X, ALU.min))
                done(dve.tensor_tensor(pick[k][:, :, :], per_expert(iota[:, :]), per_token(red[:, :]), ALU.is_equal))
                if k == 0:
                    done(dve.scalar_tensor_tensor(out=tmp2[:, :, :].rearrange("t b e -> t (b e)"),
                                                  in0=pick[0][:, :, :].rearrange("t b e -> t (b e)"), scalar=-4.0,
                                                  in1=p[:, :, :].rearrange("t b e -> t (b e)"),
                                                  op0=ALU.mult, op1=ALU.add))
            done(dve.tensor_tensor(tmp[:, :, :], pick[0][:, :, :], pick[1][:, :, :], ALU.add))
            done(dve.tensor_tensor(v[:, :, :], tmp[:, :, :], p[:, :, :], ALU.mult))
            done(dve.tensor_scalar(positive[:, :, :], v[:, :, :], 0.0, None, ALU.is_gt))
            done(dve.memset(level[:, :], 0.0))

            def search(i):
                c = steps + 4 * i
                dve.tensor_tensor(trial[:, :, :], trial_bits[:, i, :].rearrange("t (j e) -> t j e", e=E6),
                                  over(level[:, :].bitcast(I32), TRIALS), ALU.bitwise_or).then_inc(s, 1)
                dve.tensor_copy(passed[:, 0, :], level[:, :]).then_inc(s, 1)
                dve.wait_ge(s, c + 2)
                for half in range(2):
                    seqs = slice(HALF * half, HALF * half + HALF)
                    dve.tensor_tensor(reached[:, seqs, :, :],
                                      v[:, seqs, :].unsqueeze(2).to_broadcast([T, HALF, TRIALS, E6]),
                                      trial[:, :, :].bitcast(FP32).unsqueeze(1)
                                      .to_broadcast([T, HALF, TRIALS, E6]), ALU.is_ge).then_inc(reached_done, 1)
                dve.wait_ge(compared, i + 1)
                dve.scalar_tensor_tensor(out=passed[:, 1:1 + TRIALS, :].rearrange("t j e -> t (j e)"),
                                         in0=bank_c[:, 0:TRIALS * E6], scalar=CAP - 0.5,
                                         in1=trial[:, :, :].bitcast(FP32).rearrange("t j e -> t (j e)"),
                                         op0=ALU.is_ge, op1=ALU.mult).then_inc(s, 1)
                dve.wait_ge(s, c + 3)
                dve.tensor_reduce(level[:, :], passed[:, :, :].rearrange("t j e -> t e j"), AX.X, ALU.max)\
                    .then_inc(s, 1)
                dve.wait_ge(s, c + 4)

            with dve.Fori(0, BITS // ROUND // UNROLL) as i:
                for k in range(UNROLL):
                    search(UNROLL * i + k)
            steps += 4 * (BITS // ROUND)
            dve.tensor_tensor(above[:, :, :], v[:, :, :], per_expert(level[:, :]), ALU.is_gt).then_inc(flagged, 1)
            done(dve.tensor_tensor(tied[:, :, :], v[:, :, :], per_expert(level[:, :]), ALU.is_equal))
            dve.tensor_tensor(tied[:, :, :], tied[:, :, :], positive[:, :, :], ALU.mult).then_inc(flagged, 1)

            dve.wait_ge(flags_turned, 1)
            done(dve.tensor_copy(keep[:, :], bank_v[:, 0:T]))
            done(dve.tensor_copy(equal[:, :], bank_v[:, T:2 * T]))
            dve.tensor_reduce(count[:, :], keep[:, :], AX.X, ALU.add).then_inc(counted, 1)
            dve.tensor_tensor_scan(upto[:, :], core.ones[:, :], equal[:, :], 0.0, ALU.mult, ALU.add)\
                .then_inc(totalled, 1)
            dve.wait_ge(compared, BITS // ROUND + 1)
            done(dve.tensor_scalar(need[:, :], bank_c[:, 0:1], -float(CAP), None, ALU.add))
            dve.wait_ge(summed, 1)
            done(dve.tensor_tensor(offset[:, :], bank_s[:, 0:1], need[:, :], ALU.add))
            done(dve.tensor_scalar(upto[:, :], upto[:, :], offset[:, :], 0.5, ALU.add, ALU.is_lt))
            done(dve.tensor_tensor(equal[:, :], equal[:, :], upto[:, :], ALU.mult))
            done(dve.tensor_tensor(keep[:, :], keep[:, :], equal[:, :], ALU.add))
            dve.tensor_tensor_scan(upto[:, :], core.ones[:, :], keep[:, :], 0.0, ALU.mult, ALU.add)\
                .then_inc(totalled, 1)
            dve.wait_ge(summed, 2)
            done(dve.tensor_tensor(offset[:, :], bank_s[:, 1:2], base[:, :], ALU.add))
            dve.scalar_tensor_tensor(out=upto[:, :], in0=upto[:, :], scalar=offset[:, :], in1=keep[:, :],
                                     op0=ALU.add, op1=ALU.mult).then_inc(totalled, 1)

            dve.wait_ge(slots_turned, 1)
            turned_slots = bank_v[:, 0:128].rearrange("t (b e) -> t b e", e=E6)
            for k, product in enumerate((tmp, tmp2)):
                done(dve.tensor_tensor(product[:, :, :], turned_slots, pick[k][:, :, :], ALU.mult))
                done(dve.tensor_reduce(slot_f[:, k, :], product[:, :, :], AX.X, ALU.add))
            done(dve.tensor_scalar(slot_i[:, :, :], slot_f[:, :, :], float(DROPPED), None, ALU.add))
            done(dve.tensor_scalar(slot_lo[:, :, :], slot_i[:, :, :], 127, None, ALU.bitwise_and))
            done(dve.tensor_copy(lo[:, :, :], slot_lo[:, :, :]))
            done(dve.tensor_scalar(slot_hi[:, :, :], slot_i[:, :, :], 7, None, ALU.logical_shift_right))
            done(dve.tensor_copy(hi[:, :, :], slot_hi[:, :, :]))
            at = at_tile[:, :, :, :].rearrange("t k b s -> t (k b) s")
            done(dve.tensor_tensor(at, over(lanes[:, 0:TILES], 2 * B),
                                   hi[:, :, :].rearrange("t k b -> t (k b)").unsqueeze(2)
                                   .to_broadcast([T, 2 * B, TILES]), ALU.is_equal))
            dve.tensor_scalar(codes[:, :, :, 0, :].rearrange("t k b s -> t (k b) s"), at, lane[:, :], None, ALU.mult)\
                .then_inc(coded, 1)
            dve.tensor_tensor(codes[:, :, :, 1, :].rearrange("t k b s -> t (k b) s"), at,
                              seq_code[:, :, :].rearrange("t k b -> t (k b)").unsqueeze(2)
                              .to_broadcast([T, 2 * B, TILES]), ALU.mult).then_inc(coded, 1)
            dve.wait_ge(lanes_made, 1)
            for k in range(2):
                dve.tensor_tensor(at_row[:, k, :, :], over(lanes_b[:, :], B),
                                  lo[:, k, :].unsqueeze(2).to_broadcast([T, B, 128]), ALU.is_equal)\
                    .then_inc(rows_marked, 1)
            dve.wait_ge(mapped, 1)
            code, token = code_sum[:, 1, :], code_sum[:, 0, :]
            done(dve.tensor_copy(code_sum[:, :, :], bank_m[:, 0:2 * TILES].rearrange("p (c s) -> p c s", c=2)))
            done(dve.tensor_scalar(empty[:, :], code, 0.0, float(2 * DROPPED), ALU.is_equal, ALU.mult))
            done(dve.scalar_tensor_tensor(out=token, in0=code, scalar=float(T), in1=token, op0=ALU.mult, op1=ALU.add))
            done(dve.tensor_scalar(token, token, -float(T), None, ALU.add))
            done(dve.tensor_tensor(dst_row[:, :], token, empty[:, :], ALU.add))
            done(dve.tensor_scalar(src_row[:, :], dst_row[:, :], B * T - 1, None, ALU.bitwise_and))


def expert_loop(core, a, out, gate, src_row, dst_row, n_rows, planes, b1, b2):
    nc = core.nc
    (w_in0, w_in1, x_in0, x_in1, turned, x_copied, up_done, silu_done, down_done, y_added, stored0, stored1,
     x_part, gated, x_done, x_out, warmed) = core.sems(
        "mo", "w_in0 w_in1 x_in0 x_in1 turned x_copied up_done silu_done down_done y_added stored0 stored1 "
        "x_part gated x_done x_out warmed")
    w_in, x_in, stored = (w_in0, w_in1), (x_in0, x_in1), (stored0, stored1)
    bank_x, bank_up, bank_y = core.bank[0], core.bank[1:3], core.bank[3:6]
    groups = B // Q
    fetched = [core.sem(f"mo_fetched{g}") for g in range(groups)]
    at = [128 * r for r in range(len(ROWS))]
    with ExitStack() as ctx:
        def sb(name, shape):
            return ctx.enter_context(nc.sbuf_tensor(name, shape, FP32))

        w1, w2 = sb("mo_w1", [D, 2, H6]), sb("mo_w2", [128, 2, CH6, D])
        rows = sb("mo_rows", [128, 2, len(ROWS), D])
        xT = sb("mo_xT", [D, CAP])
        h = sb("mo_h", [128, CH6, CAP])
        y = sb("mo_y", [128, 2, len(ROWS), D])
        got = sb("mo_got", [T, 2, B, D])
        warm = sb("mo_warm", [T, 1])
        with nc.Block() as block:
            @block.sync
            def _(sp):
                def load_weights(e, par):
                    sp.dma_start(w1[:, par, :], a["L1_ffn_W1"][bass.ds(e, 1)].rearrange("e d h -> (e d) h"))\
                        .then_inc(w_in[par], 16)
                    sp.dma_start(w2[:, par, :, :], a["L1_ffn_W2"][bass.ds(e, 1)]
                                 .rearrange("e (c p) d -> p (e c) d", p=128)).then_inc(w_in[par], 16)

                load_weights(0, 0)
                load_weights(1, 1)
                with sp.Fori(1, E6 // 2) as i:
                    for par in range(2):
                        e = 2 * i + par
                        sp.wait_ge(down_done, e - 1)
                        load_weights(e, par)
                for par in range(2):
                    sp.wait_ge(stored[par], 16 * len(ROWS) * E6 // 2)
                for g in range(groups):
                    for k in range(2):
                        sp.dma_start(got[:, k, Q * g:Q * g + Q, :],
                                     planes[(k * B + Q * g) * T:(k * B + Q * g + Q) * T, :]
                                     .rearrange("(i t) d -> t i d", i=Q)).then_inc(fetched[g], 16)
                for g in range(groups):
                    sp.wait_ge(x_done, g + 1)
                    sp.dma_start(out[Q * g:Q * g + Q].rearrange("b t d -> t b d"), core.x[:, Q * g:Q * g + Q, :])\
                        .then_inc(x_out, 16)
                sp.wait_ge(x_out, 16 * groups)

            @block.gpsimd
            def _(pool):
                def gather(e):
                    for r, m in enumerate(ROWS):
                        tile = len(ROWS) * e + r
                        pool.indirect_dma_start(
                            out=rows[0:m, e % 2, r, :], out_offset=None, in_=n_rows,
                            in_offset=bass.IndirectOffsetOnAxis(ap=src_row[0:m, tile:tile + 1], axis=0))\
                            .then_inc(x_in[e % 2], 16)

                def scatter(e):
                    for r, m in enumerate(ROWS):
                        tile = len(ROWS) * e + r
                        pool.indirect_dma_start(
                            out=planes, out_offset=bass.IndirectOffsetOnAxis(ap=dst_row[0:m, tile:tile + 1], axis=0),
                            in_=y[0:m, e % 2, r, :], in_offset=None, bounds_check=2 * B * T - 1, oob_is_err=False)\
                            .then_inc(stored[e % 2], 16)

                gather(0)
                gather(1)
                for e in range(E6):
                    if e + 2 < E6:
                        pool.wait_ge(turned, e + 1)
                        gather(e + 2)
                    pool.wait_ge(y_added, e + 1)
                    scatter(e)

            @block.tensor
            def _(pe):
                def turn(e, par):
                    pe.wait_ge(x_in[par], 8 * len(ROWS) * (e + 2 - par))
                    for r, m in enumerate(ROWS):
                        mm = pe.transpose(bank_x[:, at[r]:at[r] + m], rows[0:m, par, r, :], core.ident[0:m, 0:m])
                    mm.then_inc(turned, 1)

                def up(e, par, c):
                    if c == 0:
                        pe.wait_ge(x_copied, e + 1)
                        pe.wait_ge(w_in[par], 16 * (e + 2 - par))
                    if c >= 2:
                        pe.wait_ge(silu_done, CH6 * e + c - 1)
                    pe.matmul(bank_up[c % 2][:, 0:CAP], w1[:, par, c * 128:(c + 1) * 128], xT[:, :],
                              start=True, stop=True).then_inc(up_done, 1)

                def down(e, par, c, first=False):
                    pe.wait_ge(silu_done, CH6 * e + c + 1)
                    if c == 0 and not first:
                        pe.wait_ge(y_added, e)
                    for r, m in enumerate(ROWS):
                        mm = pe.matmul(bank_y[r][0:m, 0:D], h[:, c, at[r]:at[r] + m], w2[:, par, c, :],
                                       start=(c == 0), stop=(c == CH6 - 1))
                    if c == CH6 - 1:
                        mm.then_inc(down_done, 1)

                def step(e, par, first=False, last=False):
                    up(e, par, 0)
                    up(e, par, 1)
                    down(e, par, 0, first)
                    up(e, par, 2)
                    down(e, par, 1)
                    up(e, par, 3)
                    down(e, par, 2)
                    if not last:
                        turn(e + 1, 1 - par)
                    down(e, par, 3)

                turn(0, 0)
                step(0, 0, first=True)
                with pe.Fori(0, E6 // 2 - 1) as i:
                    step(2 * i + 1, 1)
                    step(2 * i + 2, 0)
                step(E6 - 1, 1, last=True)

            @block.scalar
            def _(act):
                def silu(e):
                    for c in range(CH6):
                        act.wait_ge(up_done, CH6 * e + c + 1)
                        act.activation(h[:, c, :], bank_up[c % 2][:, 0:CAP], ACT.Silu,
                                       bias=b1[:, e, c:c + 1]).then_inc(silu_done, 1)

                act.activation(warm[:, :], core.eps[:, 0:1], ACT.Silu).then_inc(warmed, 1)
                silu(0)
                with act.Fori(1, E6) as e:
                    silu(e)
                act.wait_ge(warmed, 1)
                for g in range(groups):
                    act.wait_ge(fetched[g], 32)
                    for b in range(Q * g, Q * g + Q):
                        act.activation(got[:, 0, b, :], got[:, 0, b, :], ACT.Copy, scale=gate[0][:, b:b + 1])\
                            .then_inc(gated, 1)

            @block.vector
            def _(dve):
                def copy_x(e):
                    dve.wait_ge(turned, e + 1)
                    dve.tensor_copy(xT[:, :], bank_x[:, 0:CAP]).then_inc(x_copied, 1)

                def add_bias(e, par, first=False):
                    dve.wait_ge(down_done, e + 1)
                    if not first:
                        dve.wait_ge(stored[par], 8 * len(ROWS) * (e - par))
                    for r, m in enumerate(ROWS):
                        ins = dve.tensor_tensor(y[0:m, par, r, :], bank_y[r][0:m, 0:D], b2[0:m, e, :], ALU.add)
                    ins.then_inc(y_added, 1)

                copy_x(0)
                copy_x(1)
                add_bias(0, 0, first=True)
                copy_x(2)
                add_bias(1, 1, first=True)
                with dve.Fori(1, E6 // 2 - 1) as i:
                    copy_x(2 * i + 1)
                    add_bias(2 * i, 0)
                    copy_x(2 * i + 2)
                    add_bias(2 * i + 1, 1)
                copy_x(E6 - 1)
                add_bias(E6 - 2, 0)
                add_bias(E6 - 1, 1)
                for g in range(groups):
                    dve.wait_ge(fetched[g], 32)
                    for b in range(Q * g, Q * g + Q):
                        dve.scalar_tensor_tensor(out=core.x[:, b, :], in0=got[:, 1, b, :], scalar=gate[1][:, b:b + 1],
                                                 in1=core.x[:, b, :], op0=ALU.mult, op1=ALU.add).then_inc(x_part, 1)
                    seqs = slice(Q * g, Q * g + Q)
                    dve.wait_ge(x_part, Q * (g + 1))
                    dve.wait_ge(gated, Q * (g + 1))
                    dve.tensor_tensor(core.x[:, seqs, :], core.x[:, seqs, :], got[:, 0, seqs, :], ALU.add)\
                        .then_inc(x_done, 1)
def decoder(nc, a, out):
    with ExitStack() as ctx:
        core = Core(nc, ctx)
        lin = LinMem(core)
        with ExitStack() as part:
            f = FoldMem(core, part)
            m = AttnMem(core, part)
            setup(core, m, f, lin, a)
            softmax_attention(core, m, f, 0)
            softmax_attention(core, m, f, 1)
        core.free_semaphores()
        feed_forward(core, f)
        au = AutoMem(core)
        linear_attention(core, lin, au, a)
        ro = RouteMem(core)
        autocorrelation(core, au, ro, a)
        experts(core, ro, a, out)


def _constants():
    p = np.arange(128)
    c = {"c_ident": np.eye(128, dtype=np.float32)}
    for name, pick in (("c_mask_j", p // DH % J), ("c_mask_g", p // (DH * J))):
        c[name] = np.repeat(pick[:, None] == np.arange(J), T, axis=1).astype(np.float32)
    gap = p[None, :] - p[:, None]
    c["c_gap"] = np.maximum(gap, 0).astype(np.float32)
    c["c_tri"] = (gap >= 0).astype(np.float32)
    angle = 2 * np.pi * (p[:, None] * p[None, :] % T) / T
    cos, sin = np.cos(angle), np.sin(angle)
    c["c_dft"] = np.concatenate([cos, sin, cos + sin, cos - sin], axis=1).astype(np.float32)
    c["c_iota"] = np.tile(p.astype(np.float32), (128, 1))
    c["c_expert"] = (np.arange(E6) - E6).astype(np.float32)
    row = p % E6
    c["c_base"] = (row * len(ROWS) * 128 - DROPPED - 1).astype(np.float32)[:, None]
    same = row[:, None] == row[None, :]
    c["c_same"] = same.astype(np.float32)
    c["c_earlier"] = (same & (gap > 0)).astype(np.float32)
    c["c_lane"] = p.astype(np.float32)[:, None]
    c["c_seq_code"] = np.arange(1, 2 * B + 1).astype(np.float32)
    low = BITS - ROUND * np.arange(1, BITS // ROUND + 1)
    trial = np.arange(1, TRIALS + 1)[None, :] << low[:, None]
    c["c_trial_bits"] = np.repeat(trial.reshape(-1), E6).astype(np.int32)
    return c


def _butterfly_stages(w, forward):
    pair = np.arange(H3 // 2)
    out = []
    for n in range(STAGES):
        stage = n if forward else STAGES - 1 - n
        index = 2 * pair if forward else pair
        for _ in range(n):
            index = (index * 2 % H3 + index * 2 // H3) if forward else (index // 2 + index % 2 * (H3 // 2))
        low = (1 << stage) - 1
        number = (index & low) | ((index >> (stage + 1)) << stage)
        factors = w[stage][number]
        out.append(factors.transpose(1, 0, 2) if forward else factors.transpose(2, 1, 0))
    return np.ascontiguousarray(np.stack(out).reshape(-1))


def kernel(**inputs):
    import concourse.bacc as _bacc
    from concourse.bass_utils import run_bass_kernel_spmd as _run

    arrays = {k: np.ascontiguousarray(v) for k, v in inputs.items() if k != "L0_attn_mask"}
    arrays["ctxT"] = np.ascontiguousarray(inputs["ctx_1024"].transpose(0, 2, 1))
    arrays["L0_xattn_w_outT"] = np.ascontiguousarray(inputs["L0_xattn_w_out"].T)
    for name, w, forward in (("up_stages", "L0_ffn_up_weights", True), ("down_stages", "L0_ffn_down_weights", False)):
        arrays[name] = _butterfly_stages(inputs[w], forward)
    arrays["W_conT"] = np.ascontiguousarray(inputs["L0_ffn_W_con"].T)
    arrays["up_bias_col"] = np.ascontiguousarray(inputs["L0_ffn_up_bias"].reshape(CH, 128).T)
    for name, w in (("lin_WqT", "L1_attn_W_Q"), ("lin_WkT", "L1_attn_W_K"), ("lin_WvT", "L1_attn_W_V"),
                    ("lin_WgT", "L1_attn_W_g_w"), ("lin_WoT", "L1_attn_W_O")):
        arrays[name] = np.ascontiguousarray(inputs[w].T)
    for name, w in (("auto_WqT", "L1_xattn_Wq"), ("auto_WkT", "L1_xattn_Wk"), ("auto_WvT", "L1_xattn_Wv"),
                    ("auto_WoT", "L1_xattn_Wo")):
        arrays[name] = np.ascontiguousarray(inputs[w].T)
    arrays["moe_b1_col"] = np.ascontiguousarray(
        inputs["L1_ffn_b1"].reshape(E6, CH6, 128).transpose(2, 0, 1).reshape(128, E6 * CH6))
    arrays["gate_bias_col"] = np.ascontiguousarray(inputs["L1_attn_W_g_b"].reshape(C4, 128).T)
    arrays.update(_constants())
    nc = _bacc.Bacc("TRN2", target_bir_lowering=False, num_devices=1)
    args = {k: nc.dram_tensor("in_" + k, v.shape, mybir.dt.from_np(v.dtype), kind="ExternalInput").ap()
            for k, v in arrays.items()}
    out = nc.dram_tensor("out_0", (B, T, D), FP32, kind="ExternalOutput").ap()
    decoder(nc, args, out)
    r = _run(nc, [{"in_" + k: v for k, v in arrays.items()}], core_ids=[0])
    return r.results[0]["out_0"]
```
